# Optimizing a Trainium2 kernel written in Bass

```python
import numpy as np
import jax
import jax.numpy as jnp

def _softmax(x, axis=-1):
    return jax.nn.softmax(x, axis=axis)

def _gelu(x):
    return jax.nn.gelu(x, approximate=True)

def _silu(x):
    return jax.nn.silu(x)

def _sigmoid(x):
    return jax.nn.sigmoid(x)

def _layernorm(x, axis=-1, eps=1e-05):
    m = jnp.mean(x, axis=axis, keepdims=True)
    v = jnp.var(x, axis=axis, keepdims=True)
    return (x - m) / jnp.sqrt(v + eps)

def _scatter_add(tgt, idx, src, axis=0):
    return tgt.at[idx].add(src)

def _segment_sum(src, seg, n):
    return jax.ops.segment_sum(src, seg, n)
kernel_name = 'mk_audio_tower_d1_tok_audfeat256_r4_5b3251'

def setup_inputs(seed: int=0):
    np.random.seed(seed)
    _w = jnp.asarray

    def _rec_inputs():
        import jax
        import jax.numpy as jnp
        _rk = jax.random.key(seed)
        x = -5.07413e-05 + 0.999912 * jax.random.normal(jax.random.fold_in(_rk, 1), (16, 256, 64), jnp.float32)
        return x
    x = _rec_inputs()

    def _L0_tok_setup():
        import jax, jax.numpy as jnp
        from jax import lax
        import numpy as np
        B, T, C, K, STRIDE = (16, 4000, 64, 5, 2)
        EPS = 0.001
        key = jax.random.key(seed)
        k0, k1, k2, k3 = jax.random.split(key, 4)
        x = jax.random.normal(k0, (B, T, C), dtype=jnp.float32)
        w = jax.random.normal(k1, (K, 1, C), dtype=jnp.float32) * 0.1
        b = jax.random.normal(k2, (C,), dtype=jnp.float32) * 0.01
        gamma = jnp.ones((C,), dtype=jnp.float32)
        beta = jnp.zeros((C,), dtype=jnp.float32)
        alpha = jnp.full((C,), 0.25, dtype=jnp.float32) + 0.01 * jax.random.normal(k3, (C,), dtype=jnp.float32)
        return {'x': x, 'w': w, 'b': b, 'gamma': gamma, 'beta': beta, 'alpha': alpha}
    _L0_tok_all = _L0_tok_setup()
    _L0_tok_in = {k: v for k, v in _L0_tok_all.items() if k in ('w', 'b', 'gamma', 'beta', 'alpha')}
    del _L0_tok_all

    def _L0_attn_setup():
        import jax, jax.numpy as jnp
        import numpy as np
        N_HASHES = 4
        N_BUCKETS = 8
        NUM_HEADS = 8
        LN_EPS = 1e-05

        def layer_norm(x, g, b):
            m = jnp.mean(x, axis=-1, keepdims=True)
            v = jnp.mean(jnp.square(x - m), axis=-1, keepdims=True)
            return (x - m) * jax.lax.rsqrt(v + LN_EPS) * g + b
        key = jax.random.key(seed)
        ks = jax.random.split(key, 8)
        B, N, C = (16, 2048, 64)
        dff = 4 * C
        w = 0.05
        return {'x': jax.random.normal(ks[0], (B, N, C), jnp.float32), 'rotations': jax.random.normal(ks[1], (1, C, N_HASHES, N_BUCKETS // 2), jnp.float32), 'norm1_g': jnp.ones((C,), jnp.float32), 'norm1_b': jnp.zeros((C,), jnp.float32), 'q_w': jax.random.normal(ks[2], (C, C), jnp.float32) * w, 'kv_w': jax.random.normal(ks[3], (C, 2 * C), jnp.float32) * w, 'norm2_g': jnp.ones((C,), jnp.float32), 'norm2_b': jnp.zeros((C,), jnp.float32), 'fc1_w': jax.random.normal(ks[4], (C, dff), jnp.float32) * w, 'fc1_b': jnp.zeros((dff,), jnp.float32), 'fc2_w': jax.random.normal(ks[5], (dff, C), jnp.float32) * w, 'fc2_b': jnp.zeros((C,), jnp.float32)}
    _L0_attn_all = _L0_attn_setup()
    _L0_attn_in = {k: v for k, v in _L0_attn_all.items() if k in ('rotations', 'norm1_g', 'norm1_b', 'q_w', 'kv_w', 'norm2_g', 'norm2_b', 'fc1_w', 'fc1_b', 'fc2_w', 'fc2_b')}
    del _L0_attn_all

    def _L0_ffn_setup():
        import jax, jax.numpy as jnp
        import numpy as np
        B, S, D, F, E, K = (8, 512, 64, 256, 8, 2)
        key = jax.random.key(seed)
        ks = jax.random.split(key, 10)
        s = 0.02
        return {'x': jax.random.normal(ks[0], (B, S, D), dtype=jnp.float32), 'Wr': jax.random.normal(ks[1], (D, E), dtype=jnp.float32) * s, 'W1s': jax.random.normal(ks[2], (D, F), dtype=jnp.float32) * s, 'b1s': jnp.zeros((F,), dtype=jnp.float32), 'W2s': jax.random.normal(ks[3], (F, D), dtype=jnp.float32) * s, 'b2s': jnp.zeros((D,), dtype=jnp.float32), 'W1p': jax.random.normal(ks[4], (E, D, F), dtype=jnp.float32) * s, 'b1p': jnp.zeros((E, F), dtype=jnp.float32), 'W2p': jax.random.normal(ks[5], (E, F, D), dtype=jnp.float32) * s, 'b2p': jnp.zeros((E, D), dtype=jnp.float32)}
    _L0_ffn_all = _L0_ffn_setup()
    _L0_ffn_in = {k: v for k, v in _L0_ffn_all.items() if k in ('Wr', 'W1s', 'b1s', 'W2s', 'b2s', 'W1p', 'b1p', 'W2p', 'b2p')}
    del _L0_ffn_all
    return {'x': x, 'L0_tok_w': _L0_tok_in['w'], 'L0_tok_b': _L0_tok_in['b'], 'L0_tok_gamma': _L0_tok_in['gamma'], 'L0_tok_beta': _L0_tok_in['beta'], 'L0_tok_alpha': _L0_tok_in['alpha'], 'L0_attn_rotations': _L0_attn_in['rotations'], 'L0_attn_norm1_g': _L0_attn_in['norm1_g'], 'L0_attn_norm1_b': _L0_attn_in['norm1_b'], 'L0_attn_q_w': _L0_attn_in['q_w'], 'L0_attn_kv_w': _L0_attn_in['kv_w'], 'L0_attn_norm2_g': _L0_attn_in['norm2_g'], 'L0_attn_norm2_b': _L0_attn_in['norm2_b'], 'L0_attn_fc1_w': _L0_attn_in['fc1_w'], 'L0_attn_fc1_b': _L0_attn_in['fc1_b'], 'L0_attn_fc2_w': _L0_attn_in['fc2_w'], 'L0_attn_fc2_b': _L0_attn_in['fc2_b'], 'L0_ffn_Wr': _L0_ffn_in['Wr'], 'L0_ffn_W1s': _L0_ffn_in['W1s'], 'L0_ffn_b1s': _L0_ffn_in['b1s'], 'L0_ffn_W2s': _L0_ffn_in['W2s'], 'L0_ffn_b2s': _L0_ffn_in['b2s'], 'L0_ffn_W1p': _L0_ffn_in['W1p'], 'L0_ffn_b1p': _L0_ffn_in['b1p'], 'L0_ffn_W2p': _L0_ffn_in['W2p'], 'L0_ffn_b2p': _L0_ffn_in['b2p']}

def reference(x, L0_tok_w, L0_tok_b, L0_tok_gamma, L0_tok_beta, L0_tok_alpha, L0_attn_rotations, L0_attn_norm1_g, L0_attn_norm1_b, L0_attn_q_w, L0_attn_kv_w, L0_attn_norm2_g, L0_attn_norm2_b, L0_attn_fc1_w, L0_attn_fc1_b, L0_attn_fc2_w, L0_attn_fc2_b, L0_ffn_Wr, L0_ffn_W1s, L0_ffn_b1s, L0_ffn_W2s, L0_ffn_b2s, L0_ffn_W1p, L0_ffn_b1p, L0_ffn_W2p, L0_ffn_b2p):
    import jax
    import jax.numpy as jnp

    def _L0_tok_ref(x, w, b, gamma, beta, alpha):
        import jax, jax.numpy as jnp
        from jax import lax
        import numpy as np
        B, T, C, K, STRIDE = (16, 4000, 64, 5, 2)
        EPS = 0.001
        y = lax.conv_general_dilated(x, w, window_strides=(STRIDE,), padding='SAME', dimension_numbers=('NWC', 'WIO', 'NWC'), feature_group_count=C) + b
        mean = jnp.mean(y, axis=(1, 2), keepdims=True)
        var = jnp.var(y, axis=(1, 2), keepdims=True)
        yn = (y - mean) * lax.rsqrt(var + EPS) * gamma + beta
        return jnp.where(yn > 0, yn, alpha * yn)

    def _L0_attn_ref(x, rotations, norm1_g, norm1_b, q_w, kv_w, norm2_g, norm2_b, fc1_w, fc1_b, fc2_w, fc2_b):
        import jax, jax.numpy as jnp
        import numpy as np
        N_HASHES = 4
        N_BUCKETS = 8
        NUM_HEADS = 8
        LN_EPS = 1e-05

        def layer_norm(x, g, b):
            m = jnp.mean(x, axis=-1, keepdims=True)
            v = jnp.mean(jnp.square(x - m), axis=-1, keepdims=True)
            return (x - m) * jax.lax.rsqrt(v + LN_EPS) * g + b
        B, N, C = x.shape
        H = NUM_HEADS
        Dh = C // H
        scale = Dh ** (-0.5)
        x_ = layer_norm(x, norm1_g, norm1_b)
        q = (x_ @ q_w).reshape(B, N, H, Dh).transpose(0, 2, 1, 3)
        rotated = jnp.einsum('btf,fhi->bhti', x_, rotations[0])
        rotated = jnp.concatenate([rotated, -rotated], axis=-1)
        buckets = jnp.argmax(rotated, axis=-1)
        one_hot = jax.nn.one_hot(buckets, N_BUCKETS, dtype=x.dtype)
        sum_buckets = jnp.sum(one_hot, axis=2)
        pooled = jnp.einsum('bnf,bhni->bhif', x_, one_hot)
        pooled = pooled / (jax.lax.stop_gradient(sum_buckets)[..., None] + 1e-20)
        rp_x = pooled.reshape(B, N_HASHES * N_BUCKETS, C)
        sumb = jax.lax.stop_gradient(sum_buckets.reshape(B, N_HASHES * N_BUCKETS))
        M = N_HASHES * N_BUCKETS
        kv = (rp_x @ kv_w).reshape(B, M, 2, H, Dh).transpose(2, 0, 3, 1, 4)
        k, v = (kv[0], kv[1])
        attn = jnp.einsum('bhnd,bhmd->bhnm', q, k) * scale
        mask = (sumb >= 1)[:, None, None, :]
        attn = jnp.where(mask, attn, -jnp.finfo(attn.dtype).max)
        attn = jax.nn.softmax(attn, axis=-1)
        out = jnp.einsum('bhnm,bhmd->bnhd', attn, v).reshape(B, N, C)
        x = x + out
        y = layer_norm(x, norm2_g, norm2_b)
        h = jax.nn.gelu(y @ fc1_w + fc1_b, approximate=False)
        y = h @ fc2_w + fc2_b
        return x + y

    def _L0_ffn_ref(x, Wr, W1s, b1s, W2s, b2s, W1p, b1p, W2p, b2p):
        import jax, jax.numpy as jnp
        import numpy as np
        B, S, D, F, E, K = (8, 512, 64, 256, 8, 2)
        gelu = lambda t: jax.nn.gelu(t, approximate=False)
        shared = gelu(x @ W1s + b1s) @ W2s + b2s
        rw = jax.nn.softmax(x @ Wr, axis=-1)
        topw, topi = jax.lax.top_k(rw, K)
        topw = topw / jnp.sum(topw, axis=-1, keepdims=True)
        mask = jnp.sum(jax.nn.one_hot(topi, E, dtype=topw.dtype) * topw[..., None], axis=-2)
        h = gelu(jnp.einsum('bsd,edf->bsef', x, W1p) + b1p)
        priv = jnp.einsum('bsef,efd->bsed', h, W2p) + b2p
        routed = jnp.einsum('bsed,bse->bsd', priv, mask)
        return shared + routed
    h = _L0_tok_ref(x, L0_tok_w, L0_tok_b, L0_tok_gamma, L0_tok_beta, L0_tok_alpha)
    h = h + _L0_attn_ref(_layernorm(h, axis=-1), L0_attn_rotations, L0_attn_norm1_g, L0_attn_norm1_b, L0_attn_q_w, L0_attn_kv_w, L0_attn_norm2_g, L0_attn_norm2_b, L0_attn_fc1_w, L0_attn_fc1_b, L0_attn_fc2_w, L0_attn_fc2_b)
    h = h + _L0_ffn_ref(_layernorm(h, axis=-1), L0_ffn_Wr, L0_ffn_W1s, L0_ffn_b1s, L0_ffn_W2s, L0_ffn_b2s, L0_ffn_W1p, L0_ffn_b1p, L0_ffn_W2p, L0_ffn_b2p)
    return h

_drawn_inputs = setup_inputs


def setup_inputs(seed=0):
    import zlib

    import numpy as np

    out = dict(_drawn_inputs(seed))
    spreads = {'L0_tok_gamma': (1.0, 0.2),
     'L0_tok_beta': (0.0, 0.1),
     'L0_attn_norm1_g': (1.0, 0.6),
     'L0_attn_norm1_b': (0.0, 0.275),
     'L0_attn_norm2_g': (1.0, 0.592),
     'L0_attn_norm2_b': (0.0, 0.722),
     'L0_attn_fc1_b': (0.0, 0.29),
     'L0_attn_fc2_b': (0.0, 0.1),
     'L0_ffn_b1s': (0.0, 0.8),
     'L0_ffn_b2s': (0.0, 0.1),
     'L0_ffn_b1p': (0.0, 0.8),
     'L0_ffn_b2p': (0.0, 0.1)}
    factors = {'L0_tok_alpha': 4.02,
     'L0_attn_rotations': 7.997,
     'L0_attn_q_w': 8.0,
     'L0_ffn_W1s': 3.655,
     'L0_ffn_W2s': 3.114,
     'L0_ffn_W1p': 5.206,
     'L0_ffn_W2p': 4.362}
    for name, (base, spread) in spreads.items():
        noise = np.random.default_rng([zlib.crc32(name.encode()), seed]).standard_normal(out[name].shape)
        drawn = base * np.exp(spread * noise) if base else spread * noise
        out[name] = jnp.asarray(drawn.astype(out[name].dtype))
    for name, factor in factors.items():
        out[name] = (out[name] * factor).astype(out[name].dtype)
    return out
```

```python
from contextlib import ExitStack

import numpy as np

import concourse.bass as bass
from concourse import mybir

F32 = mybir.dt.float32
F16 = mybir.dt.float16
U32 = mybir.dt.uint32
ALU = mybir.AluOpType
ACT = mybir.ActivationFunctionType
AX = mybir.AxisListType.X

P = 128
GN_EPS = 1e-3
LN_EPS = 1e-5
TAPS = 5
HASHES, BUCKETS, HEADS = 4, 8, 8
M = HASHES * BUCKETS
GB = 4
SLOTS = 21
MASKED = float(2.0 ** 100)
TINY = 1e-30
FULL = 8192.0

IDENT, FOLD, HMASK, VMASK, PRI, IOTA, SEL, KCOL = 0, 128, 192, 200, 328, 336, 344, 856
N_CONST = 857


def constants():
    c = np.zeros((P, N_CONST), np.float32)
    p = np.arange(P)
    c[:, IDENT:IDENT + P] = np.eye(P)
    c[:, FOLD:FOLD + 64] = np.tile(np.eye(64), (2, 1))
    c[:64, HMASK:HMASK + HEADS] = (p[:64, None] // 8 == np.arange(HEADS))
    c[64, HMASK:HMASK + HEADS] = 1.0
    chan = np.arange(64)
    for half in range(2):
        c[:, VMASK + 64 * half:VMASK + 64 * half + 64] = (p[:, None] // M + 4 * half == chan // 8)
    c[:, PRI:PRI + 8] = 8 - np.arange(8)
    c[:, IOTA:IOTA + 8] = np.arange(8)
    for j in range(4):
        c[:16, SEL + P * j:SEL + P * j + P] = (p[:16, None] % 8 == 2 * j + p[None, :] // 64)
    c[64, KCOL], c[65, KCOL] = MASKED, -MASKED
    return c


def build(nc, ins, out):
    x = ins["x"]
    NB, T2, C = x.shape
    T = T2 // 2
    GROUPS = NB // GB
    E = ins["L0_ffn_Wr"].shape[1]
    FF = ins["L0_ffn_W1s"].shape[1]
    PAIRS = E // 2
    CHUNKS = 2 + 2 * E
    STEPS = CHUNKS // 2
    assert (T, C, E, FF) == (P, 64, 8, 256) and NB == GROUPS * GB
    TOK = GB * T

    def expert(n):
        return (n - 2) // 4 * 2 + (n - 2) % 2

    def part(n):
        return (n - 2) // 2 % 2

    STEP_SLOT = [2 * k + 3 for k in range(STEPS - 1)] + [CHUNKS]
    Z_SLOT = [STEP_SLOT[2 + 2 * j] for j in range(PAIRS)]
    MBC_SLOT = {4: (0, 1), 5: (2, 3)}
    LAST = CHUNKS + 1
    STAGE_LINKS, MOE_LINKS = 23, 7

    WQ, WROT, WFC1, WR, W1S, W1P = 0, 64, 80, 336, 344, 600
    NW = W1P + E * FF
    SEGS = [(WQ, 64), (WROT, 16), (WFC1, FF), (WR, E), (W1S, FF), (W1P, E * FF)]
    EARLY = 4
    R_B1P, R_B1S, R_FC1B, R_B2P, R_B2S, R_G1, R_B1, R_G2, R_B2, N_ROWS = 0, 16, 18, 20, 24, 25, 26, 27, 28, 29

    ctx = ExitStack()
    with ctx:
        def sb(name, shape, dt=F32):
            return ctx.enter_context(nc.sbuf_tensor(name, shape, dt))

        def ps(name, shape, dt=F32):
            return ctx.enter_context(nc.psum_tensor(name, shape, dt))

        const = sb("const", [P, N_CONST])
        ident16 = sb("ident16", [P, P], F16)
        sel16 = sb("sel16", [16, PAIRS, P], F16)
        ones_mean = sb("ones_mean", [P, P])
        nhalf = sb("nhalf", [P, 8])
        zeros = sb("zeros", [P, GB, C])
        x_taps = sb("x_taps", [P, NB, TAPS * C])
        prod = sb("prod", [P, GB, TAPS * C])
        prod_dve = sb("prod_dve", [P, GB, TAPS * C])
        y_all = sb("y_all", [P, NB, C])
        conv_w = sb("conv_w", [P, TAPS * C])
        rows_bc = sb("rows_bc", [P, 5, C])
        raw = sb("raw", [64, 464])
        wall = sb("wall", [P, NW])
        w_hi = sb("w_hi", [P, NW], F16)
        w_lo = sb("w_lo", [P, NW], F16)
        w_amax = sb("w_amax", [P, 6])
        w_max = sb("w_max", [P, 6])
        w_pow = sb("w_pow", [P, 6])
        w_rec = sb("w_rec", [P, 6])
        w_scale = sb("w_scale", [P, 6])
        w_inv = sb("w_inv", [P, 6])
        inv_q = sb("inv_q", [P, 1])
        inv_r = sb("inv_r", [P, 1])
        fc2w = sb("fc2w", [P, 2, C])
        w2s = sb("w2s", [P, 2, C])
        w2p = sb("w2p", [P, E, 2, C])
        brows = sb("brows", [N_ROWS, P])
        bcols = sb("bcols", [P, N_ROWS])
        gb1 = sb("gb1", [64, 65])
        b1rep = sb("b1rep", [64, P])
        kaug = sb("kaug", [66, 65])
        vaug = sb("vaug", [66, C])
        bq = sb("bq", [64, 1])
        brot = sb("brot", [P, GB, 16])
        bfc1 = sb("bfc1", [P, 2])

        ysum = sb("ysum", [P, GB])
        yc = sb("yc", [P, GB, C])
        ysq = sb("ysq", [P, GB, C])
        sqs = sb("sqs", [P, GB])
        gve = sb("gve", [P, GB])
        grstd = sb("grstd", [P, GB])
        yn = sb("yn", [P, GB, C])
        yg = sb("yg", [P, GB, C])
        yb = sb("yb", [P, GB, C])
        yneg = sb("yneg", [P, GB, C])
        h1 = sb("h1", [P, GB, C])
        st = sb("st", [P, 3, GB, 6])
        mv = sb("mv", [P, 3, GB, 2])
        vv1 = sb("vv1", [P, 2, GB])
        rr1 = sb("rr1", [P, 2, GB])
        vv2 = sb("vv2", [P, GB])
        rr2 = sb("rr2", [P, GB])
        vv3 = sb("vv3", [P, GB])
        rr3 = sb("rr3", [P, GB])
        xhat = sb("xhat", [P, GB, 65])
        xa = sb("xa", [P, GB, C])
        xs1 = sb("xs1", [P, GB, 2, C], F16)
        xT1 = sb("xT1", [P, TOK], F16)
        qT = sb("qT", [65, TOK])
        rot8 = sb("rot8", [P, GB * HASHES, BUCKETS])
        rmax = sb("rmax", [P, GB * HASHES])
        req = sb("req", [P, GB * HASHES, BUCKETS])
        rpri = sb("rpri", [P, GB * HASHES, BUCKETS])
        rfirst = sb("rfirst", [P, GB * HASHES])
        oh = sb("oh", [P, GB, M])
        cnt = sb("cnt", [P, 1])
        rcnt = sb("rcnt", [P, 1])
        pooled = sb("pooled", [P, 66])
        pT = sb("pT", [66, GB, 4, M])
        kbd = sb("kbd", [65, GB, HEADS, M])
        vbd = sb("vbd", [P, GB, 2, P])
        smax = sb("smax", [P, GB * HEADS])
        sexp = sb("sexp", [P, GB * HEADS, M])
        eT = sb("eT", [P, GB * 2, P])
        rden = sb("rden", [P, GB, HEADS])
        o = sb("o", [P, GB, C])
        r = sb("r", [P, GB, C])
        h1b = sb("h1b", [P, GB, C])
        rb = sb("rb", [P, GB, C])
        yhat = sb("yhat", [P, GB, C])
        xs2 = sb("xs2", [P, GB, 2, C], F16)
        xT2 = sb("xT2", [P, TOK], F16)
        fg = sb("fg", [P, 2, TOK])
        h2 = sb("h2", [P, GB, C])
        h2k = sb("h2k", [P, GB, C])
        xf = sb("xf", [P, GB, C])
        xs3 = sb("xs3", [P, GB, 2, C], F16)
        xT3 = sb("xT3", [P, TOK], F16)

        v8 = sb("v8", [P, GB, 8])
        i8 = sb("i8", [P, GB, 8], U32)
        oh2 = sb("oh2", [P, GB, 2, E])
        dlt = sb("dlt", [P, GB])
        th = sb("th", [P, GB])
        tw = sb("tw", [P, GB, 2])
        ohw = sb("ohw", [P, GB, 2, E])
        mask = sb("mask", [P, GB, E])
        ms = sb("ms", [P, GB, 2, E], F16)
        maskT = sb("maskT", [16, TOK], F16)
        mbc = sb("mbc", [P, PAIRS, TOK])
        g_ring = sb("g_ring", [P, 4, TOK])
        zt = sb("zt", [P, 2, TOK])
        zsum = sb("zsum", [P, TOK])
        ot = sb("ot", [P, GB, C])

        H = ps("H", [P, 2, 512])
        Y = ps("Y", [P, 2, 512])
        S = ps("S", [P, 2, 512])
        Tb = ps("Tb", [P, 512])
        Ub = ps("Ub", [P, 512])
        U16 = Ub[:, :].bitcast(F16)

        names = """
            taps_zero x_first x_rest early_in late_in prep_step prep_pool
            brows_zero brows_in bcols_ps bcols gb1 misc_ps misc consts16 static
            amax_early amax_late wmax_early wmax_late scale_early scale_late hi_early hi_late lo_early lo_late
            conv0 conv_rest conv_step
            stage_step ysum mean yc ysq sqs var gve grstd h1 vv1 rr1 xhat xa xh1 xl1 xt1_ps xT1 q_ps qT rot_ps
            oh pool_ps pooled pt_ps pT kv_ps kvbd scores ssub sexp et_ps eT pv_ps r rb_step rb
            vv2 rr2 yhat yh yl xt2_ps xT2 fc1_ps fg fc2_ps h2 vv3 rr3 xf xh3 xl3 xt3_ps xT3
            moe_step held router dlt th ms maskt_ps maskT mbc_ps mbc h2_kept
            mm1 gelu mm2 zsum_init z zadd folded ot stored
        """.split()
        s = {n: ctx.enter_context(nc.semaphore(n)) for n in names}

        class Chain:

            def __init__(self, eng, sem, per_group):
                self.eng, self.sem, self.per_group = eng, sem, per_group

            def start(self, g):
                self.base, self.n = g * self.per_group, 0

            def link(self, ins):
                self.n += 1
                ins.then_inc(self.sem, 1)
                self.eng.wait_ge(self.sem, self.base + self.n)

            def end(self):
                assert self.n == self.per_group, (self.n, self.per_group)

        def bc(ap, axis, shape):
            return ap.unsqueeze(axis).to_broadcast(shape)

        def spread(ap, n):
            return bass.AP(ap.tensor, 0, [[0, P], [1, n]])

        def row(ap, n):
            return bass.AP(ap.tensor, 0, [[0, 1], [1, n]])

        XROW = T2 * C
        EARLY_LOADS = [
            (conv_w[:, :], spread(ins["L0_tok_w"], TAPS * C)),
            (rows_bc[:, 0, :], spread(ins["L0_tok_b"], C)),
            (rows_bc[:, 1, :], spread(ins["L0_tok_gamma"], C)),
            (rows_bc[:, 2, :], spread(ins["L0_tok_beta"], C)),
            (rows_bc[:, 3, :], spread(ins["L0_tok_alpha"], C)),
            (rows_bc[:, 4, :], spread(ins["L0_attn_fc2_b"], C)),
            (const[:, :], ins["const"]),
            (raw[:, 0:64], ins["L0_attn_q_w"]),
            (raw[:, 64:80], ins["L0_attn_rotations"].rearrange("a c h i -> (a c) (h i)")),
            (raw[:, 80:208], ins["L0_attn_kv_w"]),
            (raw[:, 208:464], ins["L0_attn_fc1_w"]),
        ] + [d for h in range(2) for d in (
            (wall[64 * h:64 * h + 64, WQ:WQ + 64], ins["L0_attn_q_w"]),
            (wall[64 * h:64 * h + 64, WROT:WROT + 16], ins["L0_attn_rotations"].rearrange("a c h i -> (a c) (h i)")),
            (wall[64 * h:64 * h + 64, WFC1:WFC1 + FF], ins["L0_attn_fc1_w"]),
            (wall[64 * h:64 * h + 64, WR:WR + E], ins["L0_ffn_Wr"]),
        )]
        BIAS_LOADS = [
            (brows[R_B1P:R_B1P + 2 * E, :], ins["L0_ffn_b1p"].rearrange("e (c f) -> (e c) f", f=P)),
            (brows[R_B1S:R_B1S + 2, :], ins["L0_ffn_b1s"].rearrange("(c f) -> c f", f=P)),
            (brows[R_FC1B:R_FC1B + 2, :], ins["L0_attn_fc1_b"].rearrange("(c f) -> c f", f=P)),
            (brows[R_B2P:R_B2P + PAIRS, :], bass.AP(ins["L0_ffn_b2p"].tensor, 0, [[2 * C, PAIRS], [1, 2 * C]])),
            (brows[R_B2S:R_B2S + 1, 0:C], row(ins["L0_ffn_b2s"], C)),
        ] + [(brows[at:at + 1, C * h:C * h + C], row(ins[name], C)) for h in range(2) for at, name in (
            (R_G1, "L0_attn_norm1_g"), (R_B1, "L0_attn_norm1_b"), (R_G2, "L0_attn_norm2_g"), (R_B2, "L0_attn_norm2_b"))]
        LATE_LOADS = [
            (fc2w[:, :, :], ins["L0_attn_fc2_w"].rearrange("(c f) d -> f c d", f=P)),
            (w2s[:, :, :], ins["L0_ffn_W2s"].rearrange("(c f) d -> f c d", f=P)),
            (w2p[:, :, :, :], ins["L0_ffn_W2p"].rearrange("e (c f) d -> f e c d", f=P)),
        ] + [d for h in range(2) for d in (
            (wall[64 * h:64 * h + 64, W1S:W1S + FF], ins["L0_ffn_W1s"]),
            (wall[64 * h:64 * h + 64, W1P:NW].rearrange("c (e f) -> c e f", e=E), ins["L0_ffn_W1p"].rearrange("e c f -> c e f")),
        )]

        block = ctx.enter_context(nc.Block())

        @block.sync
        def _(sp):
            sp.sem_inc(s["stored"], 16)
            sp.wait_ge(s["taps_zero"], 1)
            for b0 in range(0, NB, GB):
                for p0, n, first, count in ((1, P - 2, 0, TAPS * C), (0, 1, C, 4 * C), (P - 1, 1, 0, 3 * C)):
                    src = bass.AP(x.tensor, b0 * XROW + (2 * p0 - 1) * C + first, [[2 * C, n], [XROW, GB], [1, count]])
                    sp.dma_start(x_taps[p0:p0 + n, b0:b0 + GB, first:first + count], src).then_inc(
                        s["x_first" if b0 == 0 else "x_rest"], 16)
                if b0 == 0:
                    for dst, src in LATE_LOADS:
                        sp.dma_start(dst, src).then_inc(s["late_in"], 16)
            with sp.Fori(0, GROUPS) as grp:
                sp.wait_ge(s["ot"], grp + 1)
                sp.dma_start(out[bass.ts(grp, GB)].rearrange("b t c -> t b c"), ot[:, :, :]).then_inc(s["stored"], 16)
            sp.wait_ge(s["stored"], 16 * (GROUPS + 1))

        @block.gpsimd
        def _(pool):
            prep = Chain(pool, s["prep_pool"], 0)
            prep.start(0)
            conv = Chain(pool, s["conv_step"], 0)
            conv.start(0)
            rb_chain = Chain(pool, s["rb_step"], 1)

            pool.memset(x_taps[:, :, :], 0.0).then_inc(s["taps_zero"], 1)
            pool.memset(brows[:, :], 0.0).then_inc(s["brows_zero"], 1)
            prep.link(pool.memset(ones_mean[:, :], 1.0 / (T * C)))
            prep.link(pool.memset(nhalf[:, :], -0.5))
            prep.link(pool.memset(zeros[:, :, :], 0.0))
            prep.link(pool.memset(xhat[:, :, 64:65], 1.0))
            prep.link(pool.memset(qT[64:65, :], 1.0))
            prep.link(pool.memset(pooled[:, 65:66], 1.0))
            prep.link(pool.memset(vaug[:, :], 0.0))
            pool.memset(kaug[:, :], 0.0).then_inc(s["static"], 1)

            def conv_group(b0):
                y = y_all[:, b0:b0 + GB, :]
                conv.link(pool.tensor_tensor(prod[:, :, :], x_taps[:, b0:b0 + GB, :],
                                             bc(conv_w[:, :], 1, [P, GB, TAPS * C]), ALU.mult))
                conv.link(pool.tensor_tensor(prod[:, :, 0:128], prod[:, :, 0:128], prod[:, :, 128:256], ALU.add))
                conv.link(pool.tensor_tensor(prod[:, :, 0:64], prod[:, :, 0:64], prod[:, :, 64:128], ALU.add))
                conv.link(pool.tensor_tensor(prod[:, :, 0:64], prod[:, :, 0:64], prod[:, :, 256:320], ALU.add))
                pool.tensor_tensor(y, prod[:, :, 0:64], bc(rows_bc[:, 0, :], 1, [P, GB, C]), ALU.add).then_inc(
                    s["conv_rest"], 1)

            def rsqrt(ready, out_ap, in_ap, n, done, g):
                pool.wait_ge(s[ready], g + 1)
                pool.tensor_tensor(out_ap, in_ap, n, ALU.pow).then_inc(s[done], 1)

            def moe(slot, g):
                if slot == 4:
                    pool.wait_ge(s["stored"], 16 * (g + 1))
                    pool.wait_ge(s["h2"], g + 1)
                    pool.tensor_tensor(h2k[:, :, :], h2[:, :, :], zeros[:, :, :], ALU.add).then_inc(s["h2_kept"], 1)
                for j in range(PAIRS):
                    if slot == Z_SLOT[j]:
                        if j == 0:
                            pool.wait_ge(s["zsum_init"], g + 1)
                        else:
                            pool.wait_ge(s["zadd"], PAIRS * g + j)
                        pool.wait_ge(s["z"], PAIRS * g + j + 1)
                        pool.tensor_tensor(zsum[:, :], zsum[:, :], zt[:, j % 2, :], ALU.add).then_inc(s["zadd"], 1)

            def stage(slot, g):
                if slot == 3:
                    rsqrt("gve", grstd[:, :], gve[:, :], nhalf[:, 0:GB], "grstd", g)
                elif slot == 5:
                    rsqrt("vv1", rr1[:, :, :], vv1[:, :, :], nhalf[:, :].rearrange("p (k b) -> p k b", k=2), "rr1", g)
                elif slot == 6:
                    split_low(xs1, xhat[:, :, 0:64], "xh1", "xl1", g)
                elif slot == 14:
                    rb_chain.start(g)
                    pool.wait_ge(s["r"], g + 1)
                    rb_chain.link(pool.tensor_tensor(h1b[:, :, :], h1[:, :, :], bc(rows_bc[:, 4, :], 1, [P, GB, C]), ALU.add))
                    rsqrt("vv2", rr2[:, :], vv2[:, :], nhalf[:, 0:GB], "rr2", g)
                    pool.tensor_tensor(rb[:, :, :], h1b[:, :, :], r[:, :, :], ALU.add).then_inc(s["rb"], 1)
                elif slot == 15:
                    split_low(xs2, yhat[:, :, :], "yh", "yl", g)
                elif slot == 17:
                    rsqrt("vv3", rr3[:, :], vv3[:, :], nhalf[:, 0:GB], "rr3", g)
                elif slot == 18:
                    split_low(xs3, xf[:, :, :], "xh3", "xl3", g)

            def split_low(xs, full, high, done, g):
                pool.wait_ge(s[high], g + 1)
                pool.tensor_tensor(xs[:, :, 1, :], full, xs[:, :, 0, :], ALU.subtract).then_inc(s[done], 1)

            pool.wait_ge(s["amax_early"], 1)
            pool.partition_all_reduce(w_max[:, 0:EARLY], w_amax[:, 0:EARLY], P, bass.bass_isa.ReduceOp.max).then_inc(
                s["wmax_early"], 1)
            for slot in range(SLOTS):
                stage(slot, 0)
                if slot == 3:
                    pool.wait_ge(s["early_in"], 16 * len(EARLY_LOADS))
                    pool.wait_ge(s["x_rest"], 48)
                    pool.wait_ge(s["x_rest"], 48 * (GROUPS - 1))
                if slot in (3, 6, 15):
                    conv_group(GB * {3: 1, 6: 2, 15: 3}[slot])
                if slot == 7:
                    pool.wait_ge(s["amax_late"], 1)
                    pool.partition_all_reduce(w_max[:, EARLY:6], w_amax[:, EARLY:6], P,
                                              bass.bass_isa.ReduceOp.max).then_inc(s["wmax_late"], 1)
            with pool.Fori(0, GROUPS - 1) as g:
                for slot in range(SLOTS):
                    moe(slot, g)
                    stage(slot, g + 1)
            for slot in range(SLOTS):
                moe(slot, GROUPS - 1)

        @block.scalar
        def _(act):
            for dst, src in EARLY_LOADS:
                act.dma_start(dst, src).then_inc(s["early_in"], 16)
            act.wait_ge(s["brows_zero"], 1)
            for dst, src in BIAS_LOADS:
                act.dma_start(dst, src).then_inc(s["brows_in"], 16)

            def high_parts(lo, hi, scaled, done):
                act.wait_ge(s[scaled], 1)
                for k in range(lo, hi):
                    at, n = SEGS[k]
                    ins_ = act.activation(w_hi[:, at:at + n], wall[:, at:at + n], ACT.Copy, scale=w_scale[:, k:k + 1])
                ins_.then_inc(s[done], 1)

            def high(xs, full, ready, done, g):
                act.wait_ge(s[ready], g + 1)
                act.activation(xs[:, :, 0, :], full, ACT.Copy).then_inc(s[done], 1)

            def moe(slot, g):
                if slot < CHUNKS:
                    n = slot
                    act.wait_ge(s["mm1"], CHUNKS * g + n + 1)
                    if n >= 4:
                        act.wait_ge(s["mm2"], STEPS * g + (n - 4) // 2 + 1)
                    k = 4 if n < 2 else 5
                    col = R_B1S + n if n < 2 else R_B1P + 2 * expert(n) + part(n)
                    act.activation(g_ring[:, n % 4, :], H[:, n % 2, :], ACT.Gelu, bias=bcols[:, col:col + 1],
                                   scale=w_inv[:, k:k + 1]).then_inc(s["gelu"], 1)
                if slot == 1:
                    act.wait_ge(s["dlt"], g + 1)
                    act.activation(th[:, :], dlt[:, :], ACT.Tanh, scale=inv_r[:, 0:1]).then_inc(s["th"], 1)
                if slot == 3:
                    act.wait_ge(s["maskt_ps"], g + 1)
                    act.activation(maskT[:, :], U16[0:16, 0:TOK], ACT.Copy).then_inc(s["maskT"], 1)
                if slot in MBC_SLOT:
                    for j in MBC_SLOT[slot]:
                        act.wait_ge(s["mbc_ps"], PAIRS * g + j + 1)
                        act.activation(mbc[:, j, :], S[:, j % 2, :], ACT.Copy).then_inc(s["mbc"], 1)
                if slot == STEP_SLOT[0] + 1:
                    act.wait_ge(s["mm2"], STEPS * g + 1)
                    act.activation(zsum[:, :], Y[:, 0, :], ACT.Identity, bias=bcols[:, R_B2S:R_B2S + 1]).then_inc(
                        s["zsum_init"], 1)

            def stage(slot, g):
                if slot == 1:
                    act.wait_ge(s["yc"], g + 1)
                    act.activation(ysq[:, :, :], yc[:, :, :], ACT.Square).then_inc(s["ysq"], 1)
                elif slot == 6:
                    high(xs1, xhat[:, :, 0:64], "xhat", "xh1", g)
                elif slot == 7:
                    act.wait_ge(s["xt1_ps"], g + 1)
                    act.activation(xT1[:, :], U16[:, 0:TOK], ACT.Copy).then_inc(s["xT1"], 1)
                elif slot == 8:
                    act.wait_ge(s["q_ps"], g + 1)
                    act.activation(qT[0:64, :], S[0:64, 0, :], ACT.Identity, bias=bq[:, 0:1],
                                   scale=inv_q[0:64, 0:1]).then_inc(s["qT"], 1)
                elif slot == 10:
                    act.wait_ge(s["pt_ps"], g + 1)
                    act.activation(pT[:, :, :, :], Tb[0:66, 0:P].rearrange("c (b m) -> c b m", b=GB).unsqueeze(2).to_broadcast(
                        [66, GB, 4, M]), ACT.Copy).then_inc(s["pT"], 1)
                elif slot == 12:
                    act.wait_ge(s["ssub"], g + 1)
                    act.activation(sexp[:, :, :], sexp[:, :, :], ACT.Exp).then_inc(s["sexp"], 1)
                elif slot == 13:
                    act.wait_ge(s["et_ps"], g + 1)
                    act.activation(eT[:, :, :].rearrange("p a b -> p (a b)"), S[:, :, :].rearrange("p a b -> p (a b)"),
                                   ACT.Copy).then_inc(s["eT"], 1)
                elif slot == 15:
                    high(xs2, yhat[:, :, :], "yhat", "yh", g)
                elif slot == 16:
                    act.wait_ge(s["xt2_ps"], g + 1)
                    act.activation(xT2[:, :], U16[:, 0:TOK], ACT.Copy).then_inc(s["xT2"], 1)
                    for c in range(2):
                        act.wait_ge(s["fc1_ps"], 2 * g + c + 1)
                        act.activation(fg[:, c, :], S[:, c, :], ACT.Gelu, bias=bfc1[:, c:c + 1],
                                       scale=w_inv[:, 2:3]).then_inc(s["fg"], 1)
                elif slot == 18:
                    high(xs3, xf[:, :, :], "xf", "xh3", g)
                elif slot == 19:
                    act.wait_ge(s["xt3_ps"], g + 1)
                    act.activation(xT3[:, :], U16[:, 0:TOK], ACT.Copy).then_inc(s["xT3"], 1)

            high_parts(0, EARLY, "scale_early", "hi_early")
            for slot in range(SLOTS):
                stage(slot, 0)
                if slot == 8:
                    high_parts(EARLY, 6, "scale_late", "hi_late")
            with act.Fori(0, GROUPS - 1) as g:
                for slot in range(SLOTS):
                    moe(slot, g)
                    stage(slot, g + 1)
            for slot in range(SLOTS):
                moe(slot, GROUPS - 1)

        @block.vector
        def _(dve):
            prep = Chain(dve, s["prep_step"], 0)
            prep.start(0)
            chain = Chain(dve, s["stage_step"], STAGE_LINKS)
            mchain = Chain(dve, s["moe_step"], MOE_LINKS)

            def maxima(lo, hi, done):
                for k in range(lo, hi):
                    at, n = SEGS[k]
                    ins_ = dve.tensor_reduce(w_amax[:, k:k + 1], wall[:, at:at + n], AX, ALU.max, apply_absolute_value=True)
                ins_.then_inc(s[done], 1)

            def scales(lo, hi, ready, done):
                dve.wait_ge(s[ready], 1)
                prep.link(dve.tensor_scalar(w_rec[:, lo:hi], w_max[:, lo:hi], TINY, None, ALU.max))
                prep.link(dve.tensor_scalar(w_pow[:, lo:hi].bitcast(U32), w_rec[:, lo:hi].bitcast(U32), 0x7F800000, None,
                                            ALU.bitwise_and))
                prep.link(dve.tensor_scalar(w_inv[:, lo:hi], w_pow[:, lo:hi], 1.0 / FULL, None, ALU.mult))
                dve.reciprocal(w_scale[:, lo:hi], w_inv[:, lo:hi]).then_inc(s[done], 1)
                dve.wait_ge(s[done], 1)

            def low_parts(lo, hi, high, done):
                dve.wait_ge(s[high], 1)
                for k in range(lo, hi):
                    at, n = SEGS[k]
                    ins_ = dve.scalar_tensor_tensor(w_lo[:, at:at + n], wall[:, at:at + n], w_scale[:, k:k + 1],
                                                    w_hi[:, at:at + n], ALU.mult, ALU.subtract)
                ins_.then_inc(s[done], 1)

            def conv_first():
                dve.wait_ge(s["early_in"], 16 * len(EARLY_LOADS))
                dve.wait_ge(s["x_first"], 48)
                q = prod_dve
                prep.link(dve.tensor_tensor(q[:, :, :], x_taps[:, 0:GB, :], bc(conv_w[:, :], 1, [P, GB, TAPS * C]), ALU.mult))
                prep.link(dve.tensor_tensor(q[:, :, 0:128], q[:, :, 0:128], q[:, :, 128:256], ALU.add))
                prep.link(dve.tensor_tensor(q[:, :, 0:64], q[:, :, 0:64], q[:, :, 64:128], ALU.add))
                prep.link(dve.tensor_tensor(q[:, :, 0:64], q[:, :, 0:64], q[:, :, 256:320], ALU.add))
                dve.tensor_tensor(y_all[:, 0:GB, :], q[:, :, 0:64], bc(rows_bc[:, 0, :], 1, [P, GB, C]), ALU.add).then_inc(
                    s["conv0"], 1)
                dve.wait_ge(s["conv0"], 1)

            def hold():
                dve.sem_inc(s["held"], 1)

            def stats(k, src, link):
                for b in range(GB):
                    ins_ = dve.bn_stats(st[:, k, b, :], src[:, b, :])
                link(ins_)
                hold()
                for b in range(GB):
                    ins_ = dve.bn_aggr(mv[:, k, b, :], st[:, k, b, :])
                link(ins_)

            def normalise(k, dst, src, rstd):
                for b in range(GB):
                    ins_ = dve.tensor_scalar(dst[:, b, 0:C], src[:, b, :], mv[:, k, b, 0:1], rstd(b), ALU.subtract, ALU.mult)
                return ins_

            def moe(slot, g):
                if slot == 0:
                    mchain.start(g)
                    dve.wait_ge(s["router"], g + 1)
                    hold()
                    for b in range(GB):
                        ins_ = dve.max(v8[:, b, :], Tb[:, E * b:E * b + E])
                    mchain.link(ins_)
                    hold()
                    for b in range(GB):
                        ins_ = dve.max_index(i8[:, b, :], v8[:, b, :], Tb[:, E * b:E * b + E])
                    mchain.link(ins_)
                    dve.tensor_tensor(dlt[:, :], v8[:, :, 1], v8[:, :, 0], ALU.subtract).then_inc(s["dlt"], 1)
                    mchain.link(dve.tensor_tensor(
                        oh2[:, :, :, :], const[:, IOTA:IOTA + E].unsqueeze(1).unsqueeze(1).to_broadcast([P, GB, 2, E]),
                        i8[:, :, 0:2].unsqueeze(3).to_broadcast([P, GB, 2, E]), ALU.is_equal))
                elif slot == 2:
                    dve.wait_ge(s["th"], g + 1)
                    dve.tensor_scalar(tw[:, :, 0], th[:, :], -0.5, 0.5, ALU.mult, ALU.add)
                    mchain.link(dve.tensor_scalar(tw[:, :, 1], th[:, :], 0.5, 0.5, ALU.mult, ALU.add))
                    mchain.link(dve.tensor_tensor(ohw[:, :, :, :], oh2[:, :, :, :],
                                                  tw[:, :, :].unsqueeze(3).to_broadcast([P, GB, 2, E]), ALU.mult))
                    mchain.link(dve.tensor_tensor(mask[:, :, :], ohw[:, :, 0, :], ohw[:, :, 1, :], ALU.add))
                    mchain.link(dve.tensor_copy(ms[:, :, 0, :], mask[:, :, :]))
                    dve.tensor_tensor(ms[:, :, 1, :], mask[:, :, :], ms[:, :, 0, :], ALU.subtract).then_inc(s["ms"], 1)
                for j in range(PAIRS):
                    if slot == Z_SLOT[j]:
                        dve.wait_ge(s["mm2"], STEPS * g + 3 + 2 * j)
                        dve.wait_ge(s["mbc"], PAIRS * g + j + 1)
                        if j >= 2:
                            dve.wait_ge(s["zadd"], PAIRS * g + j - 1)
                        dve.scalar_tensor_tensor(zt[:, j % 2, :], Y[:, (j + 1) % 2, :], bcols[:, R_B2P + j:R_B2P + j + 1],
                                                 mbc[:, j, :], ALU.add, ALU.mult).then_inc(s["z"], 1)
                if slot == LAST:
                    dve.wait_ge(s["folded"], g + 1)
                    dve.wait_ge(s["h2_kept"], g + 1)
                    dve.wait_ge(s["stored"], 16 * (g + 1))
                    dve.tensor_tensor(ot[:, :, :], Y[:, 1, 0:GB * C].rearrange("p (b c) -> p b c", b=GB), h2k[:, :, :],
                                      ALU.add).then_inc(s["ot"], 1)
                    mchain.end()

            def stage(slot, g):
                first = isinstance(g, int) and g == 0
                y = y_all[:, 0:GB, :] if first else y_all[:, bass.ts(g, GB), :]
                if slot == 0:
                    chain.start(g)
                    if not first:
                        dve.wait_ge(s["conv_rest"], g)
                    dve.tensor_reduce(ysum[:, :], y, AX, ALU.add).then_inc(s["ysum"], 1)
                elif slot == 1:
                    dve.wait_ge(s["mean"], g + 1)
                    dve.tensor_tensor(yc[:, :, :], y, bc(Ub[:, 0:GB], 2, [P, GB, C]), ALU.subtract).then_inc(s["yc"], 1)
                elif slot == 2:
                    dve.wait_ge(s["ysq"], g + 1)
                    dve.tensor_reduce(sqs[:, :], ysq[:, :, :], AX, ALU.add).then_inc(s["sqs"], 1)
                elif slot == 3:
                    dve.wait_ge(s["var"], g + 1)
                    dve.tensor_scalar(gve[:, :], Tb[:, 0:GB], GN_EPS, None, ALU.add).then_inc(s["gve"], 1)
                elif slot == 4:
                    dve.wait_ge(s["grstd"], g + 1)
                    chain.link(dve.tensor_tensor(yn[:, :, :], yc[:, :, :], bc(grstd[:, :], 2, [P, GB, C]), ALU.mult))
                    chain.link(dve.tensor_tensor(yg[:, :, :], yn[:, :, :], bc(rows_bc[:, 1, :], 1, [P, GB, C]), ALU.mult))
                    chain.link(dve.tensor_tensor(yb[:, :, :], yg[:, :, :], bc(rows_bc[:, 2, :], 1, [P, GB, C]), ALU.add))
                    chain.link(dve.scalar_tensor_tensor(yneg[:, :, :], yb[:, :, :], 0.0, bc(rows_bc[:, 3, :], 1, [P, GB, C]),
                                                        ALU.min, ALU.mult))
                    chain.link(dve.scalar_tensor_tensor(h1[:, :, :], yb[:, :, :], 0.0, yneg[:, :, :], ALU.max, ALU.add))
                elif slot == 5:
                    stats(0, h1, chain.link)
                    dve.tensor_scalar(vv1[:, 0, :], mv[:, 0, :, 1], LN_EPS, None, ALU.add)
                    dve.tensor_scalar(vv1[:, 1, :], mv[:, 0, :, 1], 1.0 + LN_EPS, LN_EPS ** 2, ALU.mult, ALU.add).then_inc(
                        s["vv1"], 1)
                elif slot == 6:
                    dve.wait_ge(s["rr1"], g + 1)
                    normalise(0, xhat, h1, lambda b: rr1[:, 1, b:b + 1]).then_inc(s["xhat"], 1)
                    chain.link(normalise(0, xa, h1, lambda b: rr1[:, 0, b:b + 1]))
                elif slot == 8:
                    full = [P, GB * HASHES, BUCKETS]
                    dve.wait_ge(s["rot_ps"], g + 1)
                    chain.link(dve.scalar_tensor_tensor(
                        rot8[:, :, 0:4], Tb[:, 0:64].rearrange("p (a i) -> p a i", i=4), w_inv[:, 1:2],
                        brot[:, :, :].rearrange("p b (h i) -> p (b h) i", i=4), ALU.mult, ALU.add))
                    chain.link(dve.tensor_scalar(rot8[:, :, 4:8], rot8[:, :, 0:4], -1.0, None, ALU.mult))
                    chain.link(dve.tensor_reduce(rmax[:, :], rot8[:, :, :], AX, ALU.max))
                    chain.link(dve.tensor_tensor(req[:, :, :], rot8[:, :, :], bc(rmax[:, :], 2, full), ALU.is_equal))
                    chain.link(dve.tensor_tensor(rpri[:, :, :], req[:, :, :], bc(const[:, PRI:PRI + 8], 1, full), ALU.mult))
                    chain.link(dve.tensor_reduce(rfirst[:, :], rpri[:, :, :], AX, ALU.max))
                    dve.tensor_tensor(oh[:, :, :].rearrange("p b (h i) -> p (b h) i", i=BUCKETS), rpri[:, :, :],
                                      bc(rfirst[:, :], 2, full), ALU.is_equal).then_inc(s["oh"], 1)
                elif slot == 9:
                    dve.wait_ge(s["pool_ps"], g + 1)
                    chain.link(dve.tensor_scalar(cnt[:, :], Ub[:, 64:65], 1.0, None, ALU.max))
                    chain.link(dve.reciprocal(rcnt[:, :], cnt[:, :]))
                    dve.tensor_scalar(pooled[:, 0:65], Ub[:, 0:65], rcnt[:, 0:1], None, ALU.mult).then_inc(s["pooled"], 1)
                elif slot == 11:
                    dve.wait_ge(s["kv_ps"], g + 1)
                    dve.tensor_tensor(
                        kbd[:, :, :, :], Ub[0:65, 0:P].rearrange("p (b m) -> p b m", b=GB).unsqueeze(2).to_broadcast(
                            [65, GB, HEADS, M]),
                        const[0:65, HMASK:HMASK + HEADS].unsqueeze(1).unsqueeze(3).to_broadcast([65, GB, HEADS, M]), ALU.mult)
                    dve.tensor_tensor(
                        vbd[:, :, :, 0:C], Ub[:, P:P + GB * C].rearrange("p (b c) -> p b c", b=GB).unsqueeze(2).to_broadcast(
                            [P, GB, 2, C]),
                        const[:, VMASK:VMASK + 2 * C].rearrange("p (k c) -> p k c", k=2).unsqueeze(1).to_broadcast(
                            [P, GB, 2, C]), ALU.mult).then_inc(s["kvbd"], 1)
                elif slot == 12:
                    dve.wait_ge(s["scores"], g + 1)
                    sc = S[:, :, :].rearrange("p a (b m) -> p (a b) m", m=M)
                    chain.link(dve.tensor_reduce(smax[:, :], sc, AX, ALU.max))
                    dve.tensor_tensor(sexp[:, :, :], sc, bc(smax[:, :], 2, [P, GB * HEADS, M]), ALU.subtract).then_inc(
                        s["ssub"], 1)
                elif slot == 14:
                    dve.wait_ge(s["pv_ps"], g + 1)
                    pv = Tb[:, :].rearrange("p (b c) -> p b c", b=GB)
                    chain.link(dve.reciprocal(rden[:, :, :], pv[:, :, C:2 * C:8]))
                    chain.link(dve.tensor_tensor(
                        o[:, :, :].rearrange("p b (h d) -> p b h d", h=HEADS),
                        pv[:, :, 0:C].rearrange("p b (h d) -> p b h d", h=HEADS),
                        rden[:, :, :].unsqueeze(3).to_broadcast([P, GB, HEADS, 8]), ALU.mult))
                    dve.tensor_tensor(r[:, :, :], o[:, :, :], xa[:, :, :], ALU.add).then_inc(s["r"], 1)
                    dve.wait_ge(s["r"], g + 1)
                    stats(1, r, chain.link)
                    dve.tensor_scalar(vv2[:, :], mv[:, 1, :, 1], LN_EPS, None, ALU.add).then_inc(s["vv2"], 1)
                elif slot == 15:
                    dve.wait_ge(s["rr2"], g + 1)
                    normalise(1, yhat, r, lambda b: rr2[:, b:b + 1]).then_inc(s["yhat"], 1)
                elif slot == 17:
                    dve.wait_ge(s["fc2_ps"], g + 1)
                    dve.wait_ge(s["rb"], g + 1)
                    if not first:
                        dve.wait_ge(s["h2_kept"], g)
                    dve.tensor_tensor(h2[:, :, :], Tb[:, 0:GB * C].rearrange("p (b c) -> p b c", b=GB), rb[:, :, :],
                                      ALU.add).then_inc(s["h2"], 1)
                    dve.wait_ge(s["h2"], g + 1)
                    stats(2, h2, chain.link)
                    dve.tensor_scalar(vv3[:, :], mv[:, 2, :, 1], LN_EPS, None, ALU.add).then_inc(s["vv3"], 1)
                elif slot == 18:
                    dve.wait_ge(s["rr3"], g + 1)
                    normalise(2, xf, h2, lambda b: rr3[:, b:b + 1]).then_inc(s["xf"], 1)
                    chain.end()

            dve.wait_ge(s["bcols_ps"], 1)
            dve.tensor_copy(bcols[:, :], Ub[:, 0:N_ROWS]).then_inc(s["bcols"], 1)
            dve.wait_ge(s["bcols"], 1)
            dve.wait_ge(s["early_in"], 16 * len(EARLY_LOADS))
            dve.tensor_scalar(gb1[:, 0:64], const[0:64, IDENT:IDENT + 64], bcols[0:64, R_G1:R_G1 + 1], None, ALU.mult)
            dve.tensor_copy(gb1[:, 64:65], bcols[0:64, R_B1:R_B1 + 1])
            dve.tensor_scalar(wall[:, WQ:WROT + 16], wall[:, WQ:WROT + 16], bcols[:, R_G1:R_G1 + 1], None, ALU.mult)
            prep.link(dve.tensor_scalar(wall[:, WFC1:WFC1 + FF], wall[:, WFC1:WFC1 + FF], bcols[:, R_G2:R_G2 + 1], None, ALU.mult))
            maxima(0, EARLY, "amax_early")
            dve.tensor_copy(b1rep[:, :], bcols[0:64, R_B1:R_B1 + 1].to_broadcast([64, P])).then_inc(s["gb1"], 1)
            dve.tensor_copy(sel16[:, :, :].rearrange("p j k -> p (j k)"), const[0:16, SEL:SEL + PAIRS * P])
            dve.tensor_copy(ident16[:, :], const[:, IDENT:IDENT + P])
            dve.tensor_copy(vbd[:, :, :, C:2 * C], const[:, VMASK:VMASK + 2 * C].rearrange("p (k c) -> p k c", k=2)
                            .unsqueeze(1).to_broadcast([P, GB, 2, C])).then_inc(s["consts16"], 1)
            conv_first()
            scales(0, EARLY, "wmax_early", "scale_early")
            dve.wait_ge(s["misc_ps"], 1)
            dve.wait_ge(s["static"], 1)
            dve.tensor_copy(kaug[0:65, 0:64], Tb[0:65, 0:64])
            dve.tensor_copy(kaug[64:66, 64:65], const[64:66, KCOL:KCOL + 1])
            dve.tensor_copy(vaug[0:65, :], Tb[0:65, 64:128])
            dve.tensor_scalar(bq[:, :], Tb[0:64, 128:129], 8.0 ** -0.5, None, ALU.mult)
            dve.tensor_scalar(inv_q[:, :], w_inv[:, 0:1], 8.0 ** -0.5, None, ALU.mult)
            dve.tensor_scalar(inv_r[:, :], w_inv[:, 3:4], 0.5, None, ALU.mult)
            dve.tensor_copy(brot[:, :, :], Tb[:, 130:146].unsqueeze(1).to_broadcast([P, GB, 16]))
            dve.tensor_tensor(bfc1[:, :], Tb[:, 146:148], bcols[:, R_FC1B:R_FC1B + 2], ALU.add).then_inc(s["misc"], 1)
            low_parts(0, EARLY, "hi_early", "lo_early")
            for slot in range(SLOTS):
                stage(slot, 0)
                if slot == 6:
                    dve.wait_ge(s["late_in"], 16 * len(LATE_LOADS))
                    maxima(EARLY, 6, "amax_late")
                if slot == 8:
                    scales(EARLY, 6, "wmax_late", "scale_late")
                if slot == 16:
                    low_parts(EARLY, 6, "hi_late", "lo_late")
            with dve.Fori(0, GROUPS - 1) as g:
                for slot in range(SLOTS):
                    moe(slot, g)
                    stage(slot, g + 1)
            for slot in range(SLOTS):
                moe(slot, GROUPS - 1)

        @block.tensor
        def _(pe):
            ident = const[:, IDENT:IDENT + P]

            def split_product(out_ap, at, n, rhs):
                pe.matmul(out_ap, w_hi[:, at:at + n], rhs, start=True, stop=False)
                return pe.matmul(out_ap, w_lo[:, at:at + n], rhs, start=False, stop=True)

            def split_rows(out_ap, lhs, at, n):
                pe.matmul(out_ap, lhs, w_hi[:, at:at + n], start=True, stop=False)
                return pe.matmul(out_ap, lhs, w_lo[:, at:at + n], start=False, stop=True)

            def transposes(xs, low, done, g):
                pe.wait_ge(s[low], g + 1)
                for b in range(GB):
                    ins_ = pe.transpose(U16[:, P * b:P * b + P], xs[:, b, :, :].rearrange("p k c -> p (k c)"), ident16[:, :])
                ins_.then_inc(s[done], 1)

            def moe(slot, g):
                if slot == 0:
                    pe.wait_ge(s["xT3"], g + 1)
                    for b in range(GB):
                        ins_ = split_rows(Tb[:, E * b:E * b + E], xT3[:, P * b:P * b + P], WR, E)
                    ins_.then_inc(s["router"], 1)
                if slot < CHUNKS:
                    n = slot
                    if n >= 2:
                        pe.wait_ge(s["gelu"], CHUNKS * g + n - 1)
                    at = W1S + P * n if n < 2 else W1P + FF * expert(n) + P * part(n)
                    split_product(H[:, n % 2, :], at, P, xT3[:, :]).then_inc(s["mm1"], 1)
                for k in range(STEPS):
                    if slot == STEP_SLOT[k]:
                        pe.wait_ge(s["gelu"], CHUNKS * g + 2 * k + 2)
                        if k > 0 and k % 2 == 1:
                            j = (k - 1) // 2
                            if j == 1:
                                pe.wait_ge(s["zsum_init"], g + 1)
                            elif j >= 2:
                                pe.wait_ge(s["z"], PAIRS * g + j - 1)
                        pe.wait_ge(s["static"], 1)
                        for half in range(2):
                            n = 2 * k + half
                            w = w2s[:, half, :] if k == 0 else w2p[:, expert(n), part(n), :]
                            bank = 0 if k == 0 else ((k - 1) // 2 + 1) % 2
                            ins_ = pe.matmul(Y[C * half:C * half + C, bank, :], w, g_ring[:, n % 4, :],
                                             start=(k == 0 or k % 2 == 1), stop=(k == 0 or k % 2 == 0),
                                             skip_group_check=True)
                        ins_.then_inc(s["mm2"], 1)
                if slot == 3:
                    pe.wait_ge(s["ms"], g + 1)
                    for b in range(GB):
                        ins_ = pe.transpose(U16[0:16, P * b:P * b + P], ms[:, b, :, :].rearrange("p k e -> p (k e)"), ident16[:, :])
                    ins_.then_inc(s["maskt_ps"], 1)
                if slot in MBC_SLOT:
                    for j in MBC_SLOT[slot]:
                        pe.wait_ge(s["maskT"], g + 1)
                        if j >= 2:
                            pe.wait_ge(s["mbc"], PAIRS * g + j - 1)
                        pe.matmul(S[:, j % 2, :], sel16[:, j, :], maskT[:, :], start=True, stop=True).then_inc(s["mbc_ps"], 1)
                if slot == LAST:
                    pe.wait_ge(s["zadd"], PAIRS * (g + 1))
                    pe.wait_ge(s["static"], 1)
                    for b in range(GB):
                        ins_ = pe.matmul(Y[:, 1, C * b:C * b + C], zsum[:, P * b:P * b + P], const[:, FOLD:FOLD + C],
                                         start=True, stop=True)
                    ins_.then_inc(s["folded"], 1)

            def stage(slot, g):
                if slot == 0:
                    pe.wait_ge(s["ysum"], g + 1)
                    pe.matmul(Ub[:, 0:GB], ones_mean[:, :], ysum[:, :], start=True, stop=True).then_inc(s["mean"], 1)
                elif slot == 2:
                    pe.wait_ge(s["sqs"], g + 1)
                    pe.matmul(Tb[:, 0:GB], ones_mean[:, :], sqs[:, :], start=True, stop=True).then_inc(s["var"], 1)
                elif slot == 7:
                    transposes(xs1, "xl1", "xt1_ps", g)
                elif slot == 8:
                    pe.wait_ge(s["xT1"], g + 1)
                    split_product(S[0:64, 0, :], WQ, 64, xT1[:, :]).then_inc(s["q_ps"], 1)
                    for b in range(GB):
                        ins_ = split_rows(Tb[:, 16 * b:16 * b + 16], xT1[:, P * b:P * b + P], WROT, 16)
                    ins_.then_inc(s["rot_ps"], 1)
                elif slot == 9:
                    pe.wait_ge(s["oh"], g + 1)
                    pe.wait_ge(s["static"], 1)
                    for b in range(GB):
                        ins_ = pe.matmul(Ub[M * b:M * b + M, 0:65], oh[:, b, :], xhat[:, b, :], start=True, stop=True,
                                         tile_position=(0, M * b))
                    ins_.then_inc(s["pool_ps"], 1)
                elif slot == 10:
                    pe.wait_ge(s["pooled"], g + 1)
                    pe.transpose(Tb[0:66, 0:P], pooled[:, :], ident).then_inc(s["pt_ps"], 1)
                elif slot == 11:
                    pe.wait_ge(s["pT"], g + 1)
                    pe.wait_ge(s["static"], 1)
                    pe.matmul(Ub[0:65, 0:P], kaug[:, :], pT[:, :, 0, :], start=True, stop=True)
                    for b in range(GB):
                        ins_ = pe.matmul(Ub[:, P + C * b:P + C * b + C],
                                         pT[:, b, :, :].rearrange("c h m -> c (h m)"), vaug[:, :], start=True, stop=True)
                    ins_.then_inc(s["kv_ps"], 1)
                elif slot == 12:
                    pe.wait_ge(s["kvbd"], g + 1)
                    pe.wait_ge(s["qT"], g + 1)
                    for b in range(GB):
                        ins_ = pe.matmul(S[:, b // 2, 256 * (b % 2):256 * (b % 2) + 256], qT[:, P * b:P * b + P],
                                         kbd[:, b, :, :].rearrange("p h m -> p (h m)"), start=True, stop=True)
                    ins_.then_inc(s["scores"], 1)
                elif slot == 13:
                    pe.wait_ge(s["sexp"], g + 1)
                    for k in range(2 * GB):
                        ins_ = pe.transpose(S[:, k // 4, P * (k % 4):P * (k % 4) + P],
                                            sexp[:, 4 * k:4 * k + 4, :].rearrange("p h m -> p (h m)"), ident)
                    ins_.then_inc(s["et_ps"], 1)
                elif slot == 14:
                    pe.wait_ge(s["eT"], g + 1)
                    for b in range(GB):
                        for half in range(2):
                            ins_ = pe.matmul(Tb[:, P * b:P * b + P], eT[:, 2 * b + half, :], vbd[:, b, half, :],
                                             start=(half == 0), stop=(half == 1))
                    ins_.then_inc(s["pv_ps"], 1)
                elif slot == 16:
                    transposes(xs2, "yl", "xt2_ps", g)
                    pe.wait_ge(s["xT2"], g + 1)
                    for c in range(2):
                        split_product(S[:, c, :], WFC1 + P * c, P, xT2[:, :]).then_inc(s["fc1_ps"], 1)
                elif slot == 17:
                    pe.wait_ge(s["fg"], 2 * (g + 1))
                    for b in range(GB):
                        for c in range(2):
                            ins_ = pe.matmul(Tb[:, C * b:C * b + C], fg[:, c, P * b:P * b + P], fc2w[:, c, :],
                                             start=(c == 0), stop=(c == 1))
                    ins_.then_inc(s["fc2_ps"], 1)
                elif slot == 19:
                    transposes(xs3, "xl3", "xt3_ps", g)

            pe.wait_ge(s["early_in"], 16 * len(EARLY_LOADS))
            pe.wait_ge(s["brows_in"], 16 * len(BIAS_LOADS))
            pe.transpose(Ub[:, 0:N_ROWS], brows[:, :], const[0:N_ROWS, IDENT:IDENT + N_ROWS]).then_inc(s["bcols_ps"], 1)
            pe.wait_ge(s["gb1"], 1)
            pe.matmul(Tb[0:65, 0:128], gb1[:, :], raw[:, 80:208], start=True, stop=True)
            pe.matmul(Tb[0:64, 128:129], raw[:, 0:64], bcols[0:64, R_B1:R_B1 + 1], start=True, stop=True)
            pe.matmul(Tb[:, 130:146], b1rep[:, :], raw[:, 64:80], start=True, stop=True)
            for c in range(2):
                ins_ = pe.matmul(Tb[:, 146 + c:147 + c], raw[:, 208 + P * c:208 + P * c + P], bcols[0:64, R_B2:R_B2 + 1],
                                 start=True, stop=True)
            ins_.then_inc(s["misc_ps"], 1)
            pe.wait_ge(s["consts16"], 1)
            pe.wait_ge(s["misc"], 1)
            pe.wait_ge(s["lo_early"], 1)
            pe.wait_ge(s["late_in"], 16 * len(LATE_LOADS))
            for slot in range(SLOTS):
                stage(slot, 0)
            pe.wait_ge(s["lo_late"], 1)
            with pe.Fori(0, GROUPS - 1) as g:
                for slot in range(SLOTS):
                    moe(slot, g)
                    stage(slot, g + 1)
            for slot in range(SLOTS):
                moe(slot, GROUPS - 1)


def kernel(**inputs):
    import concourse.bacc as bacc
    from concourse.bass_utils import run_bass_kernel_spmd

    nc = bacc.Bacc("TRN2", target_bir_lowering=False, num_devices=1)
    arrays, ins = {}, {}
    for name, a in {**inputs, "const": constants()}.items():
        a = np.ascontiguousarray(a)
        arrays[f"in_{name}_dram"] = a
        ins[name] = nc.dram_tensor(f"in_{name}_dram", a.shape, mybir.dt.from_np(a.dtype), kind="ExternalInput").ap()
    nb, t2, c = inputs["x"].shape
    out = nc.dram_tensor("out_0_dram", (nb, t2 // 2, c), F32, kind="ExternalOutput").ap()
    build(nc, ins, out)
    r = run_bass_kernel_spmd(nc, [arrays], core_ids=[0])
    return r.results[0]["out_0_dram"]
```

```python
from contextlib import ExitStack

import numpy as np

import concourse.bass as bass
from concourse import mybir

F32 = mybir.dt.float32
F16 = mybir.dt.float16
U32 = mybir.dt.uint32
ALU = mybir.AluOpType
ACT = mybir.ActivationFunctionType
AX = mybir.AxisListType.X

P = 128
C = 64
E = 8
FF = 256
NB, T2 = 16, 256
T = T2 // 2
GN_EPS = 1e-3
LN_EPS = 1e-5
TAPS = 5
HASHES, BUCKETS, HEADS = 4, 8, 8
M = HASHES * BUCKETS
GB = 4
GROUPS = NB // GB
TOK = GB * T
PAIRS = E // 2
CHUNKS = 2 + 2 * E
STEPS = CHUNKS // 2
MASKED = float(2.0 ** 100)
TINY = 1e-30
FULL = 8192.0

STAGE = [
    ("dve", 0, 0.4, []), ("pe", 0, 0.1, ["dve0"]), ("dve", 1, 0.4, ["pe0"]), ("act", 1, 0.35, ["dve1"]),
    ("dve", 2, 0.4, ["act1"]), ("pe", 2, 0.1, ["dve2"]), ("dve", 3, 0.1, ["pe2"]), ("pool", 3, 1.0, ["dve3"]),
    ("dve", 4, 3.5, ["pool3"]), ("pool", 4, 1.6, ["dve4"]), ("dve", 5, 0.9, ["pool4"]), ("dve", 8, 0.9, ["dve5"]),
    ("act", 5, 0.4, ["dve5"]), ("pool", 5, 0.7, ["act5"]), ("pe", 5, 0.4, ["pool5"]), ("act", 6, 0.6, ["pe5"]),
    ("pe", 6, 1.1, ["act6"]), ("dve", 6, 1.5, ["pe6"]), ("act", 7, 0.7, ["pe6"]), ("pool", 6, 0.7, ["dve4"]),
    ("pe", 7, 0.4, ["dve6"]), ("dve", 7, 0.6, ["pe7"]), ("pe", 8, 0.4, ["dve7"]), ("act", 8, 0.7, ["pe8"]),
    ("pe", 9, 1.2, ["act8"]), ("dve", 9, 1.8, ["pe9"]), ("pe", 10, 2.0, ["dve9", "act7"]), ("dve", 10, 2.4, ["pe10"]),
    ("act", 10, 2.4, ["dve10"]), ("pe", 11, 1.0, ["act10"]), ("act", 11, 1.0, ["pe11"]), ("pe", 12, 2.0, ["act11"]),
    ("dve", 12, 2.5, ["pe12", "dve8"]), ("pool", 12, 1.0, ["dve12"]), ("dve", 13, 0.9, ["pool12"]),
    ("act", 13, 0.4, ["dve13"]), ("pool", 13, 0.7, ["act13"]), ("pool", 14, 0.7, ["dve12", "pool6"]),
    ("pe", 13, 0.4, ["pool13"]), ("act", 14, 0.6, ["pe13"]), ("pe", 14, 1.0, ["act14"]), ("act", 15, 1.8, ["pe14"]),
    ("pe", 15, 1.4, ["act15"]), ("dve", 15, 1.8, ["pe15", "pool14"]), ("pool", 15, 1.0, ["dve15"]),
    ("dve", 16, 0.9, ["pool15"]), ("act", 16, 0.4, ["dve16"]), ("pool", 16, 0.7, ["act16"]), ("pe", 16, 0.4, ["pool16"]),
    ("act", 17, 0.6, ["pe16"]),
]
RINGS = [(("stage", "dve", 0), ("stage", "pe", 12)), (("stage", "pool", 6), ("stage", "dve", 15)),
         (("stage", "pe", 12), ("stage", "act", 17)), (("stage", "pe", 15), ("fold", "dve", 0)),
         (("stage", "pe", 16), ("up", "pe", CHUNKS - 1)), (("down", "act", 0), ("fold", "pe", 0))]
BANKS = [("stage", 0, "U", "dve", 1), ("stage", 2, "T", "dve", 3), ("stage", 5, "U", "act", 6),
         ("stage", 6, "T", "dve", 6), ("stage", 6, "S", "act", 7), ("stage", 7, "U", "dve", 7),
         ("stage", 8, "T", "act", 8), ("stage", 9, "U", "dve", 9), ("stage", 10, "S", "dve", 10),
         ("stage", 11, "S", "act", 11), ("stage", 12, "T", "dve", 12), ("stage", 13, "U", "act", 14),
         ("stage", 14, "S", "act", 15), ("stage", 15, "T", "dve", 15), ("stage", 16, "U", "act", 17),
         ("route", 0, "T", "dve", 0), ("route", 3, "U", "act", 3)] + [("spread", j, "S", "act", j) for j in range(PAIRS)]
PREP = [("dve", 0, 2.0, [("stage", "dve", 0)]), ("pool", 0, 0.6, ["dve0"]), ("pe", 0, 1.0, ["dve0"]),
        ("dve", 1, 1.5, ["pool0", "pe0"]), ("act", 1, 1.7, ["dve1"]), ("dve", 2, 0.9, ["act1"]),
        ("dve", 3, 2.7, ["dve2"]), ("pool", 3, 0.6, ["dve3"]), ("dve", 4, 0.4, ["pool3"]), ("act", 4, 2.8, ["dve4"]),
        ("dve", 5, 2.7, ["act4"])]
PRIORITY = {"stage": 0.6, "conv": -0.6}
HOP = 0.15


def tasks():
    table = {}

    def add(kind, g, engine, k, length, *after):
        after = [a if len(a) == 4 else (a[0], g, a[1], a[2]) for a in after]
        table[kind, g, engine, k] = (length, PRIORITY.get(kind, 0.0) - 0.1 * g, [a for a in after if a[1] >= 0])

    def names(kind, after):
        return [(kind, a.rstrip("0123456789"), int(a.lstrip("abcdefghijklmnopqrstuvwxyz"))) if isinstance(a, str) else a
                for a in after]

    for engine, k, length, after in PREP:
        add("prep", 0, engine, k, length, *names("prep", after))
    for g in range(GROUPS):
        if g > 0:
            for k in range(9):
                before = [("conv", "pool", k - 1)] if k > 0 else [("conv", g - 1, "pool", 8)] if g > 1 else []
                add("conv", g, "pool", k, 1.2 if k == 5 else 0.75, *before)
        for engine, k, length, after in STAGE:
            add("stage", g, engine, k, length, ("stage", g - 1, engine, k), *names("stage", after))
        add("route", g, "pe", 0, 0.6, ("stage", "act", 17))
        add("route", g, "dve", 0, 1.3, ("route", "pe", 0), ("route", g - 1, "dve", 2))
        add("route", g, "act", 1, 0.3, ("route", "dve", 0))
        add("route", g, "dve", 2, 1.0, ("route", "act", 1), ("route", g - 1, "pe", 3))
        add("route", g, "pe", 3, 0.4, ("route", "dve", 2))
        add("route", g, "act", 3, 0.6, ("route", "pe", 3), ("spread", g - 1, "act", PAIRS - 1))
        for j in range(PAIRS):
            before = ("spread", g - 1, "act", PAIRS - 1) if j == 0 else ("spread", "act", j - 1)
            add("spread", g, "pe", j, 0.25, ("route", "act", 3), ("sum", g - 1, "dve", j), before)
            add("spread", g, "act", j, 0.5, ("spread", "pe", j))
        for n in range(CHUNKS):
            def chunk(kind, engine, m):
                return (kind, g, engine, m) if m >= 0 else (kind, g - 1, engine, m + CHUNKS)
            add("up", g, "pe", n, 0.45, ("stage", "act", 17), chunk("up", "pe", n - 1), chunk("up", "act", n - 2))
            used = CHUNKS * g + n - 4
            add("up", g, "act", n, 0.7, ("up", "pe", n), chunk("up", "act", n - 1),
                ("down", used // CHUNKS, "pe", used % CHUNKS // 2))
        for k in range(STEPS):
            waits = {0: ("sum", g - 1, "dve", PAIRS - 1), 1: ("fold", g - 1, "dve", 0), 3: ("down", "act", 0),
                     5: ("sum", "dve", 0), 7: ("sum", "dve", 1)}.get(k, ("up", "act", 2 * k + 1))
            add("down", g, "pe", k, 0.9, ("up", "act", 2 * k + 1), waits,
                ("down", "pe", k - 1) if k > 0 else ("down", g - 1, "pe", STEPS - 1))
        add("down", g, "act", 0, 0.5, ("down", "pe", 0))
        for j in range(PAIRS):
            def pair(engine, i):
                return ("sum", g, engine, i) if i >= 0 else ("sum", g - 1, engine, i + PAIRS)
            add("sum", g, "dve", j, 0.7, ("down", "pe", 2 * j + 2), ("spread", "act", j), pair("pool", j - 2), pair("dve", j - 1))
            add("sum", g, "pool", j, 1.2, ("sum", "dve", j), ("down", "act", 0), pair("pool", j - 1))
        add("fold", g, "pe", 0, 0.9, ("sum", "pool", PAIRS - 1))
        add("fold", g, "dve", 0, 0.4, ("fold", "pe", 0))
        if g > 0:
            table["stage", g, "dve", 0][2].append(("conv", g, "pool", 8))
        for (kind, engine, k), (kind_of, engine_of, k_of) in RINGS:
            if g >= 2:
                table[kind, g, engine, k][2].append((kind_of, g - 2, engine_of, k_of))
    table["stage", 0, "pe", 5][2].append(("prep", 0, "dve", 2))
    table["up", 0, "pe", 0][2].append(("prep", 0, "dve", 5))
    return table


def schedule():
    table = tasks()
    fills, frees = {}, {}
    for kind, k, bank, engine, last in BANKS:
        for g in range(GROUPS):
            fills.setdefault((kind, g, "pe", k), []).append(bank)
            frees.setdefault((kind, g, engine, last), []).append(bank)
    end, order = {}, {engine: [] for engine in ("pe", "act", "dve", "pool")}
    busy, bank_free = dict.fromkeys(order, 0.0), dict.fromkeys("STU", 0.0)
    bank_of = dict.fromkeys("STU")
    while len(end) < len(table):
        best = None
        for turn, (length, priority, after) in table.items():
            if turn in end or not all(a in end for a in after):
                continue
            if any(bank_of[b] is not None for b in fills.get(turn, ())):
                continue
            start = max([busy[turn[2]]] + [end[a] + HOP * (a[2] != turn[2]) for a in after] +
                        [bank_free[b] + HOP for b in fills.get(turn, ())])
            if best is None or start - priority < best[0]:
                best = (start - priority, start, turn, start + length)
        _, start, turn, stop = best
        end[turn] = busy[turn[2]] = stop
        order[turn[2]].append(turn[:2] + turn[3:])
        for b in fills.get(turn, ()):
            bank_of[b] = turn
        for b in frees.get(turn, ()):
            bank_of[b], bank_free[b] = None, stop
    return order


ORDER = schedule()


def expert(n):
    return (n - 2) // 4 * 2 + (n - 2) % 2


def part(n):
    return (n - 2) // 2 % 2


def columns(sections):
    at, starts = 0, {}
    for name, width in sections:
        starts[name] = at
        at += width
    return starts, at


STEM, N_STEM = columns([("conv_w", TAPS * C), ("conv_b", C), ("gamma", C), ("beta", C), ("alpha", C), ("fc2_b", C)])
EARLY, N_EARLY = columns([
    ("b1p", 2 * E), ("b1s", 2), ("fc1_b", 2), ("b2p", PAIRS), ("b2s", 1), ("g1", 1), ("b1", 1), ("g2", 1), ("b2", 1),
    ("q", C), ("rot", 16), ("fc1", FF), ("wr", E), ("kv", 2 * C),
    ("ident", P), ("fold", C), ("hmask", HEADS), ("vmask", 2 * C), ("pri", BUCKETS), ("iota", E), ("sel", PAIRS * P),
    ("kcol", 1)])
LATE, N_LATE = columns([("w1s", FF), ("w1p", E * FF), ("fc2", 2 * C), ("w2s", 2 * C), ("w2p", E * 2 * C)])


def constants():
    p = np.arange(P)[:, None]
    hmask = np.zeros((P, HEADS), np.float32)
    hmask[:C] = p[:C] // 8 == np.arange(HEADS)
    hmask[C] = 1.0
    chan = np.arange(C)[None, :]
    kcol = np.zeros((P, 1), np.float32)
    kcol[C], kcol[C + 1] = MASKED, -MASKED
    return {
        "ident": np.eye(P),
        "fold": np.tile(np.eye(C), (2, 1)),
        "hmask": hmask,
        "vmask": np.concatenate([p // M + 4 * h == chan // 8 for h in range(2)], 1),
        "pri": np.tile(8.0 - np.arange(BUCKETS), (P, 1)),
        "iota": np.tile(np.arange(E), (P, 1)),
        "sel": np.concatenate([(p % 8 == 2 * j + np.arange(P)[None, :] // C) & (p < 16) for j in range(PAIRS)], 1),
        "kcol": kcol,
    }


def build(nc, xp, stem_d, early_d, late_d, out):
    (WQ, WROT, WFC1, WR, W1S, W1P), NW = (0, 64, 96, 352, 360, 616), 616 + E * FF
    SEGS = [(WQ, C), (WROT, 32), (WFC1, FF), (WR, E), (W1S, FF), (W1P, E * FF)]
    HEAD = 4

    ctx = ExitStack()
    with ctx:
        def sb(name, shape, dt=F32):
            return ctx.enter_context(nc.sbuf_tensor(name, shape, dt))

        def ring(name, shape, dt=F32):
            pair = [sb(f"{name}{k}", shape, dt) for k in range(2)]
            return lambda g: pair[g % 2]

        stem = sb("stem", [P, N_STEM])
        early = sb("early", [P, N_EARLY])
        late = sb("late", [P, N_LATE])
        ident16 = sb("ident16", [P, P], F16)
        sel16 = sb("sel16", [16, PAIRS, P], F16)
        ones_mean = sb("ones_mean", [P, P])
        ones_row = sb("ones_row", [1, P])
        nhalf = sb("nhalf", [P, 8])
        x_taps = sb("x_taps", [P, GROUPS, GB, TAPS * C])
        prod = sb("prod", [P, GB, TAPS * C])
        y_all = sb("y_all", [P, NB, C])
        wall = sb("wall", [P, WR])
        w_hi = sb("w_hi", [P, NW], F16)
        w_lo = sb("w_lo", [P, NW], F16)
        w_amax = sb("w_amax", [P, 6])
        w_max = sb("w_max", [P, 6])
        w_some = sb("w_some", [P, 6])
        w_pow = sb("w_pow", [P, 6])
        w_scale = sb("w_scale", [P, 6])
        w_inv = sb("w_inv", [P, 6])
        inv_q = sb("inv_q", [P, 1])
        inv_r = sb("inv_r", [P, 1])
        gb1 = sb("gb1", [C, C + 1])
        kaug = sb("kaug", [C + 2, C + 1])
        vaug = sb("vaug", [C + 2, C])
        bq = sb("bq", [C, 1])
        brot = sb("brot", [1, GB, HASHES, 2, 4])
        bfc1 = sb("bfc1", [P, 2])

        ysum = ring("ysum", [P, GB])
        yc = ring("yc", [P, GB, C])
        ysq = ring("ysq", [P, GB, C])
        sqs = ring("sqs", [P, GB])
        gve = ring("gve", [P, GB])
        grstd = ring("grstd", [P, GB])
        h1 = ring("h1", [P, GB, C])
        st = ring("st", [P, 3, GB, 6])
        mv = ring("mv", [P, 3, GB, 2])
        vv1 = ring("vv1", [P, 2, GB])
        rr1 = ring("rr1", [P, 2, GB])
        vv2 = ring("vv2", [P, GB])
        rr2 = ring("rr2", [P, GB])
        vv3 = ring("vv3", [P, GB])
        rr3 = ring("rr3", [P, GB])
        xhat = ring("xhat", [P, GB, C + 1])
        xa = ring("xa", [P, GB, C])
        xs1 = ring("xs1", [P, GB, 2, C], F16)
        xT1 = ring("xT1", [P, TOK], F16)
        qT = ring("qT", [C + 1, TOK])
        rmax = ring("rmax", [P, GB * HASHES])
        req = ring("req", [P, GB * HASHES, BUCKETS])
        rfirst = ring("rfirst", [P, GB * HASHES])
        oh = ring("oh", [P, GB, M])
        cnt = ring("cnt", [P, 1])
        rcnt = ring("rcnt", [P, 1])
        pooled = ring("pooled", [P, C + 2])
        pT = ring("pT", [C + 2, GB, 4, M])
        kbd = ring("kbd", [C + 1, GB, HEADS, M])
        vbd = ring("vbd", [P, GB, 2, P])
        smax = ring("smax", [P, GB * HEADS])
        sexp = ring("sexp", [P, GB * HEADS, M])
        eT = ring("eT", [P, GB * 2, P])
        rden = ring("rden", [P, GB, HEADS])
        r = ring("r", [P, GB, C])
        rb = ring("rb", [P, GB, C])
        yhat = ring("yhat", [P, GB, C])
        xs2 = ring("xs2", [P, GB, 2, C], F16)
        xT2 = ring("xT2", [P, TOK], F16)
        fg = ring("fg", [P, 2, TOK])
        h2 = ring("h2", [P, GB, C])
        xf = ring("xf", [P, GB, C])
        xs3 = ring("xs3", [P, GB, 2, C], F16)
        xT3 = ring("xT3", [P, TOK], F16)

        v8 = sb("v8", [P, GB, 8])
        i8 = sb("i8", [P, GB, 8], U32)
        oh2 = sb("oh2", [P, GB, 2, E])
        dlt = sb("dlt", [P, GB])
        th = sb("th", [P, GB])
        tw = sb("tw", [P, GB, 2])
        mask = sb("mask", [P, GB, E])
        ms = sb("ms", [P, GB, 2, E], F16)
        maskT = sb("maskT", [16, TOK], F16)
        mbc = sb("mbc", [P, PAIRS, TOK])
        g_ring = sb("g_ring", [P, 4, TOK])
        zt = sb("zt", [P, 2, TOK])
        zsum = ring("zsum", [P, TOK])
        ot = ring("ot", [P, GB, C])

        def bank(name, shape):
            return ctx.enter_context(nc.psum_tensor(name, shape, F32))

        H = bank("H", [P, 2, 512])
        Y = bank("Y", [P, 2, 512])
        S = bank("S", [P, 2, 512])
        Tb = bank("Tb", [P, 512])
        Ub = bank("Ub", [P, 512])
        misc, misc_kv = Y[:, 0, :], Y[:, 1, :]
        U16 = Ub[:, :].bitcast(F16)

        names = """
            augmented x_in0 x_in1 x_in2 x_in3 stem_in early_in late_in static pool_step prep_step
            gained gb1 misc_ps misc consts16 amax_head amax_rest wmax_head wmax_rest scale_head scale_rest
            hi_head hi_rest lo_head lo_rest conv0 conv_rest
            stage_step ysum mean yc ysq sqs var gve grstd vv1 rr1 xhat xh1 xl1 xt1_ps xT1 q_ps qT rot_ps
            oh pool_ps pooled pt_ps pT kv_ps kvbd scores ssub sexp et_ps eT pv_ps r rb
            vv2 rr2 yhat yh yl xt2_ps xT2 fc1_ps fg fc2_ps h2 vv3 rr3 xf xh3 xl3 xt3_ps xT3
            moe_step router best th_in th ms maskt_ps maskT mbc_ps mbc
            mm1 gelu mm2 zsum_init z zadd folded ot stored0 stored1 stored2 stored3
        """.split()
        s = {n: ctx.enter_context(nc.semaphore(n)) for n in names}

        class Chain:

            def __init__(self, eng, sem):
                self.eng, self.sem, self.n = eng, sem, 0

            def link(self, ins):
                self.n += 1
                ins.then_inc(self.sem, 1)
                self.eng.wait_ge(self.sem, self.n)

        def bc(ap, axis, shape):
            return ap.unsqueeze(axis).to_broadcast(shape)

        def sec(name, n, rows=P):
            return early[0:rows, EARLY[name]:EARLY[name] + n]

        def stem_row(name):
            return bc(stem[:, STEM[name]:STEM[name] + C], 1, [P, GB, C])

        def seg_src(k):
            at, n = SEGS[k]
            if k < 3:
                return wall[:, at:at + n]
            return sec("wr", n) if k == 3 else late[:, LATE["w1s" if k == 4 else "w1p"]:][:, 0:n]

        def late_w(name, *dims):
            return late[:, LATE[name]:LATE[name] + int(np.prod(dims)) * C]

        fc2w = late_w("fc2", 2).rearrange("p (c d) -> p c d", d=C)
        w2s = late_w("w2s", 2).rearrange("p (c d) -> p c d", d=C)
        w2p = late_w("w2p", E, 2).rearrange("p (e c d) -> p e c d", e=E, d=C)
        CW = stem[:, STEM["conv_w"]:STEM["conv_w"] + TAPS * C]

        stored = [s[f"stored{g}"] for g in range(GROUPS)]
        x_in = [s[f"x_in{g}"] for g in range(GROUPS)]
        XROW = xp.shape[1] * C

        block = ctx.enter_context(nc.Block())

        @block.sync
        def _(sp):
            for g in range(GROUPS):
                src = bass.AP(xp.tensor, g * GB * XROW, [[2 * C, P], [XROW, GB], [1, TAPS * C]])
                sp.dma_start(x_taps[:, g, :, :], src).then_inc(x_in[g], 16)
                if g == 0:
                    sp.dma_start(early[:, :], early_d).then_inc(s["early_in"], 16)
                if g == 1:
                    sp.dma_start(late[:, :], late_d).then_inc(s["late_in"], 16)
            for g in range(GROUPS):
                sp.wait_ge(s["ot"], g + 1)
                sp.dma_start(out[GB * g:GB * g + GB].rearrange("b t c -> t b c"), ot(g)[:, :, :]).then_inc(stored[g], 16)
            for g in range(GROUPS):
                sp.wait_ge(stored[g], 16)

        @block.gpsimd
        def _(pool):
            chain = Chain(pool, s["pool_step"])

            for ap, value in [(ones_mean[:, :], 1.0 / (T * C)), (nhalf[:, :], -0.5), (ones_row[:, :], 1.0),
                              (vaug[:, :], 0.0), (kaug[:, :], 0.0)] + [d for g in range(2) for d in (
                                  (xhat(g)[:, :, C:C + 1], 1.0), (qT(g)[C:C + 1, :], 1.0), (pooled(g)[:, C + 1:C + 2], 1.0))]:
                chain.link(pool.memset(ap, value))
            pool.sem_inc(s["static"], 1)

            def conv_piece(g, k):
                if k == 0:
                    pool.wait_ge(s["stem_in"], 16)
                    pool.wait_ge(x_in[g], 16)
                if k < 5:
                    tap = slice(C * k, C * k + C)
                    chain.link(pool.tensor_tensor(prod[:, :, tap], x_taps[:, g, :, tap], bc(CW[:, tap], 1, [P, GB, C]), ALU.mult))
                elif k < 7:
                    a, b, n = ((0, 128, 128), (0, 64, 64))[k - 5]
                    chain.link(pool.tensor_tensor(prod[:, :, a:a + n], prod[:, :, a:a + n], prod[:, :, b:b + n], ALU.add))
                elif k == 7:
                    chain.link(pool.tensor_tensor(prod[:, :, 0:64], prod[:, :, 0:64], prod[:, :, 256:320], ALU.add))
                else:
                    ins = pool.tensor_tensor(y_all[:, GB * g:GB * g + GB, :], prod[:, :, 0:64], stem_row("conv_b"), ALU.add)
                    ins.then_inc(s["conv_rest"], 1)
                    pool.wait_ge(s["conv_rest"], g)

            def rsqrt(ready, out_ap, in_ap, exponent, done, g):
                pool.wait_ge(s[ready], g + 1)
                pool.tensor_tensor(out_ap, in_ap, exponent, ALU.pow).then_inc(s[done], 1)

            def split_low(xs, full, high, done, g):
                pool.wait_ge(s[high], g + 1)
                pool.tensor_tensor(xs[:, :, 1, :], full, xs[:, :, 0, :], ALU.subtract).then_inc(s[done], 1)

            def sum_pair(g, j):
                if j == 0:
                    pool.wait_ge(s["zsum_init"], g + 1)
                else:
                    pool.wait_ge(s["zadd"], PAIRS * g + j)
                pool.wait_ge(s["z"], PAIRS * g + j + 1)
                pool.tensor_tensor(zsum(g)[:, :], zsum(g)[:, :], zt[:, j % 2, :], ALU.add).then_inc(s["zadd"], 1)

            def stage(g, slot):
                if slot == 3:
                    rsqrt("gve", grstd(g)[:, :], gve(g)[:, :], nhalf[:, 0:GB], "grstd", g)
                elif slot == 4:
                    rsqrt("vv1", rr1(g)[:, :, :], vv1(g)[:, :, :], nhalf[:, :].rearrange("p (k b) -> p k b", k=2), "rr1", g)
                elif slot == 5:
                    split_low(xs1(g), xhat(g)[:, :, 0:C], "xh1", "xl1", g)
                elif slot == 6:
                    if g >= 2:
                        pool.wait_ge(s["h2"], g - 1)
                    chain.link(pool.tensor_tensor(rb(g)[:, :, :], h1(g)[:, :, :], stem_row("fc2_b"), ALU.add))
                elif slot == 12:
                    rsqrt("vv2", rr2(g)[:, :], vv2(g)[:, :], nhalf[:, 0:GB], "rr2", g)
                elif slot == 13:
                    split_low(xs2(g), yhat(g)[:, :, :], "yh", "yl", g)
                elif slot == 14:
                    pool.tensor_tensor(rb(g)[:, :, :], rb(g)[:, :, :], r(g)[:, :, :], ALU.add).then_inc(s["rb"], 1)
                elif slot == 15:
                    rsqrt("vv3", rr3(g)[:, :], vv3(g)[:, :], nhalf[:, 0:GB], "rr3", g)
                elif slot == 16:
                    split_low(xs3(g), xf(g)[:, :, :], "xh3", "xl3", g)

            def maxima(lo, hi, ready, done):
                pool.wait_ge(s[ready], 1)
                pool.partition_all_reduce(w_max[:, lo:hi], w_amax[:, lo:hi], P, bass.bass_isa.ReduceOp.max).then_inc(s[done], 1)

            def prep(_, k):
                if k == 0:
                    maxima(0, HEAD, "amax_head", "wmax_head")
                elif k == 3:
                    maxima(HEAD, 6, "amax_rest", "wmax_rest")

            for kind, g, k in ORDER["pool"]:
                {"prep": prep, "conv": conv_piece, "stage": stage, "sum": sum_pair}[kind](g, k)

        @block.scalar
        def _(act):
            act.dma_start(stem[:, :], stem_d).then_inc(s["stem_in"], 16)

            def high_parts(lo, hi, scaled, done):
                act.wait_ge(s[scaled], 1)
                for k in range(lo, hi):
                    at, n = SEGS[k]
                    ins = act.activation(w_hi[:, at:at + n], seg_src(k), ACT.Copy, scale=w_scale[:, k:k + 1])
                ins.then_inc(s[done], 1)

            def copy(ready, out_ap, in_ap, done, g):
                act.wait_ge(s[ready], g + 1)
                act.activation(out_ap, in_ap, ACT.Copy).then_inc(s[done], 1)

            def up(g, m):
                n = CHUNKS * g + m
                act.wait_ge(s["mm1"], n + 1)
                if n >= 4:
                    act.wait_ge(s["mm2"], (n - 4) // 2 + 1)
                shared = m < 2
                col = EARLY["b1s"] + m if shared else EARLY["b1p"] + 2 * expert(m) + part(m)
                act.activation(g_ring[:, n % 4, :], H[:, n % 2, :], ACT.Gelu, bias=early[:, col:col + 1],
                               scale=w_inv[:, 4:5] if shared else w_inv[:, 5:6]).then_inc(s["gelu"], 1)

            def route(g, k):
                if k == 1:
                    act.wait_ge(s["th_in"], g + 1)
                    act.activation(th[:, :], dlt[:, :], ACT.Tanh, scale=inv_r[:, 0:1]).then_inc(s["th"], 1)
                elif k == 3:
                    copy("maskt_ps", maskT[:, :], U16[0:16, 0:TOK], "maskT", g)

            def spread(g, j):
                if g > 0:
                    act.wait_ge(s["z"], PAIRS * (g - 1) + j + 1)
                act.wait_ge(s["mbc_ps"], PAIRS * g + j + 1)
                act.activation(mbc[:, j, :], S[:, j % 2, :], ACT.Copy).then_inc(s["mbc"], 1)

            def down(g, _):
                if g >= 2:
                    act.wait_ge(s["folded"], g - 1)
                act.wait_ge(s["mm2"], STEPS * g + 1)
                act.activation(zsum(g)[:, :], Y[:, 0, :], ACT.Identity, bias=sec("b2s", 1)).then_inc(s["zsum_init"], 1)

            def stage(g, slot):
                if slot == 1:
                    act.wait_ge(s["yc"], g + 1)
                    act.activation(ysq(g)[:, :, :], yc(g)[:, :, :], ACT.Square).then_inc(s["ysq"], 1)
                elif slot == 5:
                    copy("xhat", xs1(g)[:, :, 0, :], xhat(g)[:, :, 0:C], "xh1", g)
                elif slot == 8:
                    copy("pt_ps", pT(g)[:, :, :, :], Tb[0:C + 2, 0:P].rearrange("c (b m) -> c b m", b=GB).unsqueeze(2)
                         .to_broadcast([C + 2, GB, 4, M]), "pT", g)
                elif slot == 10:
                    act.wait_ge(s["ssub"], g + 1)
                    act.activation(sexp(g)[:, :, :], sexp(g)[:, :, :], ACT.Exp).then_inc(s["sexp"], 1)
                elif slot == 11:
                    copy("et_ps", eT(g)[:, :, :].rearrange("p a b -> p (a b)"), S[:, :, :].rearrange("p a b -> p (a b)"),
                         "eT", g)
                elif slot == 13:
                    copy("yhat", xs2(g)[:, :, 0, :], yhat(g)[:, :, :], "yh", g)
                elif slot == 16:
                    copy("xf", xs3(g)[:, :, 0, :], xf(g)[:, :, :], "xh3", g)
                elif slot == 6:
                    copy("xt1_ps", xT1(g)[:, :], U16[:, 0:TOK], "xT1", g)
                elif slot == 7:
                    act.wait_ge(s["q_ps"], g + 1)
                    act.activation(qT(g)[0:C, :], S[0:C, 0, :], ACT.Identity, bias=bq[:, 0:1],
                                   scale=inv_q[0:C, 0:1]).then_inc(s["qT"], 1)
                elif slot == 14:
                    copy("xt2_ps", xT2(g)[:, :], U16[:, 0:TOK], "xT2", g)
                elif slot == 15:
                    for c in range(2):
                        act.wait_ge(s["fc1_ps"], 2 * g + c + 1)
                        act.activation(fg(g)[:, c, :], S[:, c, :], ACT.Gelu, bias=bfc1[:, c:c + 1],
                                       scale=w_inv[:, 2:3]).then_inc(s["fg"], 1)
                elif slot == 17:
                    if g >= 2:
                        act.wait_ge(s["mm1"], CHUNKS * (g - 1))
                    copy("xt3_ps", xT3(g)[:, :], U16[:, 0:TOK], "xT3", g)

            act.wait_ge(s["early_in"], 16)
            act.activation(ident16[:, :], sec("ident", P), ACT.Copy)
            for k in range(2):
                act.activation(vbd(k)[:, :, :, C:2 * C], sec("vmask", 2 * C).rearrange("p (k c) -> p k c", k=2)
                               .unsqueeze(1).to_broadcast([P, GB, 2, C]), ACT.Copy)
            act.activation(sel16[:, :, :].rearrange("p j k -> p (j k)"), sec("sel", PAIRS * P, 16), ACT.Copy).then_inc(
                s["consts16"], 1)

            def prep(_, k):
                if k == 1:
                    high_parts(0, HEAD, "scale_head", "hi_head")
                    act.wait_ge(s["misc_ps"], 1)
                    act.wait_ge(s["static"], 1)
                    act.activation(kaug[0:C + 1, 0:C], misc_kv[0:C + 1, 0:C], ACT.Copy)
                    act.activation(kaug[C:C + 2, C:C + 1], early[C:C + 2, EARLY["kcol"]:EARLY["kcol"] + 1], ACT.Copy)
                    act.activation(vaug[0:C + 1, :], misc_kv[0:C + 1, C:2 * C], ACT.Copy).then_inc(s["augmented"], 1)
                elif k == 4:
                    high_parts(HEAD, 6, "scale_rest", "hi_rest")

            for kind, g, k in ORDER["act"]:
                {"prep": prep, "stage": stage, "route": route, "spread": spread, "up": up, "down": down}[kind](g, k)

        @block.vector
        def _(dve):
            pchain = Chain(dve, s["prep_step"])
            chain = Chain(dve, s["stage_step"])
            mchain = Chain(dve, s["moe_step"])

            def maxima(lo, hi, done):
                for k in range(lo, hi):
                    ins = dve.tensor_reduce(w_amax[:, k:k + 1], seg_src(k), AX, ALU.max, apply_absolute_value=True)
                ins.then_inc(s[done], 1)

            def scales(lo, hi, ready, done):
                dve.wait_ge(s[ready], 1)
                pchain.link(dve.tensor_scalar(w_some[:, lo:hi], w_max[:, lo:hi], TINY, None, ALU.max))
                pchain.link(dve.tensor_scalar(w_pow[:, lo:hi].bitcast(U32), w_some[:, lo:hi].bitcast(U32), 0x7F800000, None,
                                            ALU.bitwise_and))
                pchain.link(dve.tensor_scalar(w_inv[:, lo:hi], w_pow[:, lo:hi], 1.0 / FULL, None, ALU.mult))
                dve.reciprocal(w_scale[:, lo:hi], w_inv[:, lo:hi]).then_inc(s[done], 1)
                dve.wait_ge(s[done], 1)

            def low_parts(lo, hi, high, done):
                dve.wait_ge(s[high], 1)
                for k in range(lo, hi):
                    at, n = SEGS[k]
                    ins = dve.scalar_tensor_tensor(w_lo[:, at:at + n], seg_src(k), w_scale[:, k:k + 1],
                                                   w_hi[:, at:at + n], ALU.mult, ALU.subtract)
                ins.then_inc(s[done], 1)

            def conv_first():
                q = sexp(0)[:, :, :].rearrange("p a m -> p (a m)")
                q = q[:, 0:GB * TAPS * C - GB * C].rearrange("p (b n) -> p b n", b=GB)
                taps = x_taps[:, 0, :, :]
                y = y_all[:, 0:GB, :]
                dve.wait_ge(s["stem_in"], 16)
                dve.wait_ge(x_in[0], 16)
                dve.tensor_tensor(y, taps[:, :, 256:320], bc(CW[:, 256:320], 1, [P, GB, C]), ALU.mult)
                pchain.link(dve.tensor_tensor(q, taps[:, :, 0:256], bc(CW[:, 0:256], 1, [P, GB, 4 * C]), ALU.mult))
                dve.tensor_tensor(q[:, :, 0:128], q[:, :, 0:128], q[:, :, 128:256], ALU.add)
                pchain.link(dve.tensor_tensor(y, y, stem_row("conv_b"), ALU.add))
                pchain.link(dve.tensor_tensor(q[:, :, 0:64], q[:, :, 0:64], q[:, :, 64:128], ALU.add))
                dve.tensor_tensor(y, y, q[:, :, 0:64], ALU.add).then_inc(s["conv0"], 1)
                dve.wait_ge(s["conv0"], 1)

            def stats(k, src, g):
                for b in range(GB):
                    ins = dve.bn_stats(st(g)[:, k, b, :], src[:, b, :])
                chain.link(ins)
                for b in range(GB):
                    ins = dve.bn_aggr(mv(g)[:, k, b, :], st(g)[:, k, b, :])
                chain.link(ins)

            def normalise(k, dst, src, rstd, g):
                for b in range(GB):
                    ins = dve.tensor_scalar(dst[:, b, 0:C], src[:, b, :], mv(g)[:, k, b, 0:1], rstd[:, b:b + 1],
                                            ALU.subtract, ALU.mult)
                return ins

            def route(g, k):
                if k == 0:
                    dve.wait_ge(s["router"], g + 1)
                    for b in range(GB):
                        ins = dve.max(v8[:, b, :], Tb[:, E * b:E * b + E])
                    mchain.link(ins)
                    dve.tensor_tensor(dlt[:, :], v8[:, :, 1], v8[:, :, 0], ALU.subtract).then_inc(s["th_in"], 1)
                    for b in range(GB):
                        ins = dve.max_index(i8[:, b, :], v8[:, b, :], Tb[:, E * b:E * b + E])
                    ins.then_inc(s["best"], 1)
                    dve.wait_ge(s["best"], g + 1)
                    mchain.link(dve.tensor_tensor(
                        oh2[:, :, :, :], sec("iota", E).unsqueeze(1).unsqueeze(1).to_broadcast([P, GB, 2, E]),
                        i8[:, :, 0:2].unsqueeze(3).to_broadcast([P, GB, 2, E]), ALU.is_equal))
                elif k == 2:
                    if g > 0:
                        dve.wait_ge(s["maskt_ps"], g)
                    dve.wait_ge(s["th"], g + 1)
                    dve.tensor_scalar(tw[:, :, 0], th[:, :], -0.5, 0.5, ALU.mult, ALU.add)
                    mchain.link(dve.tensor_scalar(tw[:, :, 1], th[:, :], 0.5, 0.5, ALU.mult, ALU.add))
                    mchain.link(dve.tensor_tensor(oh2[:, :, :, :], oh2[:, :, :, :],
                                                  tw[:, :, :].unsqueeze(3).to_broadcast([P, GB, 2, E]), ALU.mult))
                    mchain.link(dve.tensor_tensor(mask[:, :, :], oh2[:, :, 0, :], oh2[:, :, 1, :], ALU.add))
                    mchain.link(dve.tensor_copy(ms[:, :, 0, :], mask[:, :, :]))
                    dve.tensor_tensor(ms[:, :, 1, :], mask[:, :, :], ms[:, :, 0, :], ALU.subtract).then_inc(s["ms"], 1)

            def sum_pair(g, j):
                dve.wait_ge(s["mm2"], STEPS * g + 3 + 2 * j)
                dve.wait_ge(s["mbc"], PAIRS * g + j + 1)
                if PAIRS * g + j >= 2:
                    dve.wait_ge(s["zadd"], PAIRS * g + j - 1)
                dve.scalar_tensor_tensor(zt[:, j % 2, :], Y[:, (j + 1) % 2, :],
                                         early[:, EARLY["b2p"] + j:EARLY["b2p"] + j + 1],
                                         mbc[:, j, :], ALU.add, ALU.mult).then_inc(s["z"], 1)

            def fold(g, _):
                dve.wait_ge(s["folded"], g + 1)
                if g >= 2:
                    dve.wait_ge(stored[g - 2], 16)
                dve.tensor_tensor(ot(g)[:, :, :], Y[:, 1, 0:GB * C].rearrange("p (b c) -> p b c", b=GB), h2(g)[:, :, :],
                                  ALU.add).then_inc(s["ot"], 1)

            def stage(g, slot):
                y = y_all[:, GB * g:GB * g + GB, :]
                hashed = [P, GB * HASHES, BUCKETS]
                if slot == 0:
                    if g > 0:
                        dve.wait_ge(s["conv_rest"], g)
                    if g >= 2:
                        dve.wait_ge(s["pv_ps"], g - 1)
                    dve.tensor_reduce(ysum(g)[:, :], y, AX, ALU.add).then_inc(s["ysum"], 1)
                elif slot == 1:
                    dve.wait_ge(s["mean"], g + 1)
                    dve.tensor_tensor(yc(g)[:, :, :], y, bc(Ub[:, 0:GB], 2, [P, GB, C]), ALU.subtract).then_inc(s["yc"], 1)
                elif slot == 2:
                    dve.wait_ge(s["ysq"], g + 1)
                    dve.tensor_reduce(sqs(g)[:, :], ysq(g)[:, :, :], AX, ALU.add).then_inc(s["sqs"], 1)
                elif slot == 3:
                    dve.wait_ge(s["var"], g + 1)
                    dve.tensor_scalar(gve(g)[:, :], Tb[:, 0:GB], GN_EPS, None, ALU.add).then_inc(s["gve"], 1)
                elif slot == 4:
                    dve.wait_ge(s["grstd"], g + 1)
                    for b in range(GB):
                        ins = dve.scalar_tensor_tensor(yc(g)[:, b, :], yc(g)[:, b, :], grstd(g)[:, b:b + 1],
                                                       stem[:, STEM["gamma"]:STEM["gamma"] + C], ALU.mult, ALU.mult)
                    chain.link(ins)
                    chain.link(dve.tensor_tensor(yc(g)[:, :, :], yc(g)[:, :, :], stem_row("beta"), ALU.add))
                    chain.link(dve.scalar_tensor_tensor(ysq(g)[:, :, :], yc(g)[:, :, :], 0.0, stem_row("alpha"),
                                                        ALU.min, ALU.mult))
                    chain.link(dve.scalar_tensor_tensor(h1(g)[:, :, :], yc(g)[:, :, :], 0.0, ysq(g)[:, :, :],
                                                        ALU.max, ALU.add))
                    stats(0, h1(g), g)
                    dve.tensor_scalar(vv1(g)[:, 0, :], mv(g)[:, 0, :, 1], LN_EPS, None, ALU.add)
                    dve.tensor_scalar(vv1(g)[:, 1, :], mv(g)[:, 0, :, 1], 1.0 + LN_EPS, LN_EPS ** 2, ALU.mult,
                                      ALU.add).then_inc(s["vv1"], 1)
                elif slot == 5:
                    dve.wait_ge(s["rr1"], g + 1)
                    normalise(0, xhat(g), h1(g), rr1(g)[:, 1, :], g).then_inc(s["xhat"], 1)
                elif slot == 8:
                    chain.link(normalise(0, xa(g), h1(g), rr1(g)[:, 0, :], g))
                elif slot == 6:
                    dve.wait_ge(s["rot_ps"], g + 1)
                    rot = Tb[:, 0:GB * M].rearrange("p (a i) -> p a i", i=BUCKETS)
                    chain.link(dve.tensor_reduce(rmax(g)[:, :], rot, AX, ALU.max))
                    chain.link(dve.tensor_tensor(req(g)[:, :, :], rot, bc(rmax(g)[:, :], 2, hashed), ALU.is_equal))
                    chain.link(dve.tensor_tensor(req(g)[:, :, :], req(g)[:, :, :], bc(sec("pri", BUCKETS), 1, hashed), ALU.mult))
                    chain.link(dve.tensor_reduce(rfirst(g)[:, :], req(g)[:, :, :], AX, ALU.max))
                    dve.tensor_tensor(oh(g)[:, :, :].rearrange("p b (h i) -> p (b h) i", i=BUCKETS), req(g)[:, :, :],
                                      bc(rfirst(g)[:, :], 2, hashed), ALU.is_equal).then_inc(s["oh"], 1)
                elif slot == 7:
                    dve.wait_ge(s["pool_ps"], g + 1)
                    chain.link(dve.tensor_scalar(cnt(g)[:, :], Ub[:, C:C + 1], 1.0, None, ALU.max))
                    chain.link(dve.reciprocal(rcnt(g)[:, :], cnt(g)[:, :]))
                    dve.tensor_scalar(pooled(g)[:, 0:C + 1], Ub[:, 0:C + 1], rcnt(g)[:, 0:1], None, ALU.mult).then_inc(
                        s["pooled"], 1)
                elif slot == 9:
                    dve.wait_ge(s["kv_ps"], g + 1)
                    dve.tensor_tensor(
                        kbd(g)[:, :, :, :], Ub[0:C + 1, 0:P].rearrange("p (b m) -> p b m", b=GB).unsqueeze(2).to_broadcast(
                            [C + 1, GB, HEADS, M]),
                        sec("hmask", HEADS, C + 1).unsqueeze(1).unsqueeze(3).to_broadcast([C + 1, GB, HEADS, M]), ALU.mult)
                    dve.tensor_tensor(
                        vbd(g)[:, :, :, 0:C], Ub[:, P:P + GB * C].rearrange("p (b c) -> p b c", b=GB).unsqueeze(2).to_broadcast(
                            [P, GB, 2, C]),
                        sec("vmask", 2 * C).rearrange("p (k c) -> p k c", k=2).unsqueeze(1).to_broadcast(
                            [P, GB, 2, C]), ALU.mult).then_inc(s["kvbd"], 1)
                elif slot == 10:
                    dve.wait_ge(s["scores"], g + 1)
                    sc = S[:, :, :].rearrange("p a (b m) -> p (a b) m", m=M)
                    chain.link(dve.tensor_reduce(smax(g)[:, :], sc, AX, ALU.max))
                    dve.tensor_tensor(sexp(g)[:, :, :], sc, bc(smax(g)[:, :], 2, [P, GB * HEADS, M]), ALU.subtract).then_inc(
                        s["ssub"], 1)
                elif slot == 12:
                    dve.wait_ge(s["pv_ps"], g + 1)
                    if g >= 2:
                        dve.wait_ge(s["xT3"], g - 1)
                    pv = Tb[:, :].rearrange("p (b c) -> p b c", b=GB)
                    chain.link(dve.reciprocal(rden(g)[:, :, :], pv[:, :, C:2 * C:8]))
                    chain.link(dve.tensor_tensor(
                        r(g)[:, :, :].rearrange("p b (h d) -> p b h d", h=HEADS),
                        pv[:, :, 0:C].rearrange("p b (h d) -> p b h d", h=HEADS),
                        rden(g)[:, :, :].unsqueeze(3).to_broadcast([P, GB, HEADS, 8]), ALU.mult))
                    dve.tensor_tensor(r(g)[:, :, :], r(g)[:, :, :], xa(g)[:, :, :], ALU.add).then_inc(s["r"], 1)
                    dve.wait_ge(s["r"], g + 1)
                    stats(1, r(g), g)
                    dve.tensor_scalar(vv2(g)[:, :], mv(g)[:, 1, :, 1], LN_EPS, None, ALU.add).then_inc(s["vv2"], 1)
                elif slot == 13:
                    dve.wait_ge(s["rr2"], g + 1)
                    normalise(1, yhat(g), r(g), rr2(g), g).then_inc(s["yhat"], 1)
                elif slot == 15:
                    dve.wait_ge(s["fc2_ps"], g + 1)
                    dve.wait_ge(s["rb"], g + 1)
                    if g >= 2:
                        dve.wait_ge(s["ot"], g - 1)
                    dve.tensor_tensor(h2(g)[:, :, :], Tb[:, 0:GB * C].rearrange("p (b c) -> p b c", b=GB), rb(g)[:, :, :],
                                      ALU.add).then_inc(s["h2"], 1)
                    dve.wait_ge(s["h2"], g + 1)
                    stats(2, h2(g), g)
                    dve.tensor_scalar(vv3(g)[:, :], mv(g)[:, 2, :, 1], LN_EPS, None, ALU.add).then_inc(s["vv3"], 1)
                elif slot == 16:
                    dve.wait_ge(s["rr3"], g + 1)
                    normalise(2, xf(g), h2(g), rr3(g), g).then_inc(s["xf"], 1)


            def prep(_, k):
                if k == 0:
                    dve.wait_ge(s["early_in"], 16)
                    dve.tensor_scalar(gb1[:, 0:C], sec("ident", C, C), sec("g1", 1, C), None, ALU.mult)
                    dve.tensor_copy(gb1[:, C:C + 1], sec("b1", 1, C)).then_inc(s["gb1"], 1)
                    wrot = wall[:, WROT:WROT + 32].rearrange("p (h k i) -> p h k i", h=HASHES, k=2)
                    rot_in = sec("rot", 16).rearrange("p (h i) -> p h i", h=HASHES)
                    dve.tensor_scalar(wall[:, WQ:WQ + C], sec("q", C), sec("g1", 1), None, ALU.mult)
                    dve.tensor_scalar(wrot[:, :, 0, :], rot_in, sec("g1", 1), None, ALU.mult)
                    dve.tensor_scalar(wrot[:, :, 1, :], rot_in, sec("g1", 1), -1.0, ALU.mult, ALU.mult)
                    pchain.link(dve.tensor_scalar(wall[:, WFC1:WFC1 + FF], sec("fc1", FF), sec("g2", 1), None, ALU.mult))
                    maxima(0, HEAD, "amax_head")
                elif k == 1:
                    scales(0, HEAD, "wmax_head", "scale_head")
                    dve.tensor_scalar(inv_q[:, :], w_inv[:, 0:1], 8.0 ** -0.5, None, ALU.mult)
                    dve.tensor_scalar(inv_r[:, :], w_inv[:, 3:4], 0.5, None, ALU.mult)
                    dve.wait_ge(s["misc_ps"], 1)
                    dve.tensor_scalar(bq[:, :], misc[0:C, 128:129], 8.0 ** -0.5, None, ALU.mult)
                    for side, sign in enumerate((1.0, -1.0)):
                        dve.tensor_scalar(brot[:, :, :, side, :], misc[0:1, 130:146].rearrange("p (h i) -> p h i", h=HASHES)
                                          .unsqueeze(1).to_broadcast([1, GB, HASHES, 4]), w_scale[0:1, 1:2], sign,
                                          ALU.mult, ALU.mult)
                    dve.tensor_tensor(bfc1[:, :], misc[:, 146:148], sec("fc1_b", 2), ALU.add).then_inc(s["misc"], 1)
                elif k == 2:
                    low_parts(0, HEAD, "hi_head", "lo_head")
                elif k == 3:
                    dve.wait_ge(s["late_in"], 16)
                    maxima(HEAD, 6, "amax_rest")
                elif k == 4:
                    scales(HEAD, 6, "wmax_rest", "scale_rest")
                elif k == 5:
                    low_parts(HEAD, 6, "hi_rest", "lo_rest")

            conv_first()
            for kind, g, k in ORDER["dve"]:
                {"prep": prep, "stage": stage, "route": route, "sum": sum_pair, "fold": fold}[kind](g, k)

        @block.tensor
        def _(pe):
            ident = sec("ident", P)
            held = {}

            def take(*banks):
                for b in banks:
                    if b in held:
                        pe.wait_ge(*held[b])

            def lend(b, sem, value):
                held[b] = (s[sem], value)

            def split_product(out_ap, at, n, rhs):
                pe.matmul(out_ap, w_hi[:, at:at + n], rhs, start=True, stop=False)
                return pe.matmul(out_ap, w_lo[:, at:at + n], rhs, start=False, stop=True)

            def transposes(xs, low, done, g):
                take("U")
                pe.wait_ge(s[low], g + 1)
                for b in range(GB):
                    ins = pe.transpose(U16[:, P * b:P * b + P], xs[:, b, :, :].rearrange("p k c -> p (k c)"), ident16[:, :])
                ins.then_inc(s[done], 1)

            def route(g, k):
                if k == 0:
                    take("T")
                    pe.wait_ge(s["xT3"], g + 1)
                    for b in range(GB):
                        pe.matmul(Tb[:, E * b:E * b + E], xT3(g)[:, P * b:P * b + P], w_hi[:, WR:WR + E], start=True, stop=False)
                        ins = pe.matmul(Tb[:, E * b:E * b + E], xT3(g)[:, P * b:P * b + P], w_lo[:, WR:WR + E],
                                        start=False, stop=True)
                    ins.then_inc(s["router"], 1)
                    lend("T", "best", g + 1)
                elif k == 3:
                    take("U")
                    pe.wait_ge(s["ms"], g + 1)
                    for b in range(GB):
                        ins = pe.transpose(U16[0:16, P * b:P * b + P], ms[:, b, :, :].rearrange("p k e -> p (k e)"), ident16[:, :])
                    ins.then_inc(s["maskt_ps"], 1)
                    lend("U", "maskT", g + 1)

            def spread(g, j):
                take(f"S{j % 2}")
                pe.wait_ge(s["maskT"], g + 1)
                pe.matmul(S[:, j % 2, :], sel16[:, j, :], maskT[:, :], start=True, stop=True).then_inc(s["mbc_ps"], 1)
                lend(f"S{j % 2}", "mbc", PAIRS * g + j + 1)

            def up(g, m):
                n = CHUNKS * g + m
                pe.wait_ge(s["xT3"], g + 1)
                if n >= 2:
                    pe.wait_ge(s["gelu"], n - 1)
                if n == 0:
                    pe.wait_ge(s["lo_rest"], 1)
                at = W1S + P * m if m < 2 else W1P + FF * expert(m) + P * part(m)
                split_product(H[:, n % 2, :], at, P, xT3(g)[:, :]).then_inc(s["mm1"], 1)

            def down(g, k):
                j = (k - 1) // 2
                bank_ = 0 if k == 0 else (j + 1) % 2
                opens = k == 0 or k % 2 == 1
                if g == 0 and k == 0:
                    pe.wait_ge(s["augmented"], 1)
                    pe.wait_ge(s["misc"], 1)
                    pe.wait_ge(s["late_in"], 16)
                if k == 0 and g > 0:
                    pe.wait_ge(s["z"], PAIRS * g)
                elif k == 1 and g > 0:
                    pe.wait_ge(s["ot"], g)
                elif k == 3:
                    pe.wait_ge(s["zsum_init"], g + 1)
                elif k > 3 and opens:
                    pe.wait_ge(s["z"], PAIRS * g + j - 1)
                pe.wait_ge(s["gelu"], CHUNKS * g + 2 * k + 2)
                for half in range(2):
                    n = 2 * k + half
                    w = w2s[:, half, :] if k == 0 else w2p[:, expert(n), part(n), :]
                    ins = pe.matmul(Y[C * half:C * half + C, bank_, :], w, g_ring[:, (CHUNKS * g + n) % 4, :],
                                    start=opens, stop=(k == 0 or not opens), skip_group_check=True)
                ins.then_inc(s["mm2"], 1)

            def fold(g, _):
                pe.wait_ge(s["zadd"], PAIRS * (g + 1))
                for b in range(GB):
                    ins = pe.matmul(Y[:, 1, C * b:C * b + C], zsum(g)[:, P * b:P * b + P], sec("fold", C),
                                    start=True, stop=True)
                ins.then_inc(s["folded"], 1)

            def stage(g, slot):
                if slot == 0:
                    take("U")
                    pe.wait_ge(s["ysum"], g + 1)
                    pe.matmul(Ub[:, 0:GB], ones_mean[:, :], ysum(g)[:, :], start=True, stop=True).then_inc(s["mean"], 1)
                    lend("U", "yc", g + 1)
                elif slot == 2:
                    take("T")
                    pe.wait_ge(s["sqs"], g + 1)
                    pe.matmul(Tb[:, 0:GB], ones_mean[:, :], sqs(g)[:, :], start=True, stop=True).then_inc(s["var"], 1)
                    lend("T", "gve", g + 1)
                elif slot == 5:
                    if g == 0:
                        pe.wait_ge(s["consts16"], 1)
                        pe.wait_ge(s["misc"], 1)
                        pe.wait_ge(s["lo_head"], 1)
                        pe.wait_ge(s["augmented"], 1)
                    transposes(xs1(g), "xl1", "xt1_ps", g)
                    lend("U", "xT1", g + 1)
                elif slot == 6:
                    take("S0", "T")
                    pe.wait_ge(s["xT1"], g + 1)
                    pe.matmul(Tb[:, 0:GB * M], ones_row[:, :], brot[:, :, :, :, :].rearrange("p b h k i -> p (b h k i)"),
                              start=True, stop=False, skip_group_check=True)
                    for b in range(GB):
                        for w in (w_hi, w_lo):
                            ins = pe.matmul(Tb[:, M * b:M * b + M], xT1(g)[:, P * b:P * b + P], w[:, WROT:WROT + M],
                                            start=False, stop=(w is w_lo), skip_group_check=True)
                    ins.then_inc(s["rot_ps"], 1)
                    lend("T", "oh", g + 1)
                    split_product(S[0:C, 0, :], WQ, C, xT1(g)[:, :]).then_inc(s["q_ps"], 1)
                    lend("S0", "qT", g + 1)
                elif slot == 7:
                    take("U")
                    pe.wait_ge(s["oh"], g + 1)
                    for b in range(GB):
                        ins = pe.matmul(Ub[M * b:M * b + M, 0:C + 1], oh(g)[:, b, :], xhat(g)[:, b, :], start=True, stop=True,
                                        tile_position=(0, M * b))
                    ins.then_inc(s["pool_ps"], 1)
                    lend("U", "pooled", g + 1)
                elif slot == 8:
                    take("T")
                    pe.wait_ge(s["pooled"], g + 1)
                    pe.transpose(Tb[0:C + 2, 0:P], pooled(g)[:, :], ident).then_inc(s["pt_ps"], 1)
                    lend("T", "pT", g + 1)
                elif slot == 9:
                    take("U")
                    pe.wait_ge(s["pT"], g + 1)
                    pe.matmul(Ub[0:C + 1, 0:P], kaug[:, :], pT(g)[:, :, 0, :], start=True, stop=True)
                    for b in range(GB):
                        ins = pe.matmul(Ub[:, P + C * b:P + C * b + C], pT(g)[:, b, :, :].rearrange("c h m -> c (h m)"),
                                        vaug[:, :], start=True, stop=True)
                    ins.then_inc(s["kv_ps"], 1)
                    lend("U", "kvbd", g + 1)
                elif slot == 10:
                    take("S0", "S1")
                    pe.wait_ge(s["kvbd"], g + 1)
                    pe.wait_ge(s["qT"], g + 1)
                    for b in range(GB):
                        ins = pe.matmul(S[:, b // 2, 256 * (b % 2):256 * (b % 2) + 256], qT(g)[:, P * b:P * b + P],
                                        kbd(g)[:, b, :, :].rearrange("p h m -> p (h m)"), start=True, stop=True)
                    ins.then_inc(s["scores"], 1)
                    lend("S0", "ssub", g + 1)
                    lend("S1", "ssub", g + 1)
                elif slot == 11:
                    take("S0", "S1")
                    pe.wait_ge(s["sexp"], g + 1)
                    for k in range(2 * GB):
                        ins = pe.transpose(S[:, k // 4, P * (k % 4):P * (k % 4) + P],
                                           sexp(g)[:, 4 * k:4 * k + 4, :].rearrange("p h m -> p (h m)"), ident)
                    ins.then_inc(s["et_ps"], 1)
                    lend("S0", "eT", g + 1)
                    lend("S1", "eT", g + 1)
                elif slot == 12:
                    take("T")
                    pe.wait_ge(s["eT"], g + 1)
                    for b in range(GB):
                        for half in range(2):
                            ins = pe.matmul(Tb[:, P * b:P * b + P], eT(g)[:, 2 * b + half, :], vbd(g)[:, b, half, :],
                                            start=(half == 0), stop=(half == 1))
                    ins.then_inc(s["pv_ps"], 1)
                    lend("T", "r", g + 1)
                elif slot == 13:
                    transposes(xs2(g), "yl", "xt2_ps", g)
                    lend("U", "xT2", g + 1)
                elif slot == 14:
                    pe.wait_ge(s["xT2"], g + 1)
                    for c in range(2):
                        take(f"S{c}")
                        split_product(S[:, c, :], WFC1 + P * c, P, xT2(g)[:, :]).then_inc(s["fc1_ps"], 1)
                        lend(f"S{c}", "fg", 2 * g + c + 1)
                elif slot == 15:
                    take("T")
                    if g == 0:
                        pe.wait_ge(s["late_in"], 16)
                    pe.wait_ge(s["fg"], 2 * (g + 1))
                    for b in range(GB):
                        for c in range(2):
                            ins = pe.matmul(Tb[:, C * b:C * b + C], fg(g)[:, c, P * b:P * b + P], fc2w[:, c, :],
                                            start=(c == 0), stop=(c == 1))
                    ins.then_inc(s["fc2_ps"], 1)
                    lend("T", "h2", g + 1)
                elif slot == 16:
                    transposes(xs3(g), "xl3", "xt3_ps", g)
                    lend("U", "xT3", g + 1)

            def prep(_, k):
                pe.wait_ge(s["early_in"], 16)
                pe.wait_ge(s["gb1"], 1)
                pe.matmul(misc_kv[0:C + 1, 0:2 * C], gb1[:, :], sec("kv", 2 * C, C), start=True, stop=True)
                pe.matmul(misc[0:C, 128:129], sec("q", C, C), sec("b1", 1, C), start=True, stop=True)
                pe.matmul(misc[0:1, 130:146], sec("b1", 1, C), sec("rot", 16, C), start=True, stop=True)
                for c in range(2):
                    ins = pe.matmul(misc[:, 146 + c:147 + c], early[0:C, EARLY["fc1"] + P * c:EARLY["fc1"] + P * c + P],
                                    sec("b2", 1, C), start=True, stop=True)
                ins.then_inc(s["misc_ps"], 1)

            pe.wait_ge(s["static"], 1)
            for kind, g, k in ORDER["pe"]:
                {"prep": prep, "stage": stage, "route": route, "spread": spread, "up": up, "down": down, "fold": fold}[kind](
                    g, k)


def lay_out(a):
    def both(w):
        return np.tile(w.reshape(C, -1), (2, 1))

    def everywhere(v):
        return np.tile(v.reshape(1, -1), (P, 1))

    def by_feature(w):
        return w.reshape(-1, P, C).transpose(1, 0, 2).reshape(P, -1)

    parts = {
        "conv_w": everywhere(a["L0_tok_w"]), "conv_b": everywhere(a["L0_tok_b"]), "gamma": everywhere(a["L0_tok_gamma"]),
        "beta": everywhere(a["L0_tok_beta"]), "alpha": everywhere(a["L0_tok_alpha"]), "fc2_b": everywhere(a["L0_attn_fc2_b"]),
        "b1p": a["L0_ffn_b1p"].reshape(-1, P).T, "b1s": a["L0_ffn_b1s"].reshape(-1, P).T,
        "fc1_b": a["L0_attn_fc1_b"].reshape(-1, P).T, "b2p": a["L0_ffn_b2p"].reshape(-1, P).T,
        "b2s": np.pad(a["L0_ffn_b2s"], (0, C))[:, None],
        "g1": both(a["L0_attn_norm1_g"]), "b1": both(a["L0_attn_norm1_b"]),
        "g2": both(a["L0_attn_norm2_g"]), "b2": both(a["L0_attn_norm2_b"]),
        "q": both(a["L0_attn_q_w"]), "rot": both(a["L0_attn_rotations"]), "fc1": both(a["L0_attn_fc1_w"]),
        "wr": both(a["L0_ffn_Wr"]), "kv": both(a["L0_attn_kv_w"]),
        "w1s": both(a["L0_ffn_W1s"]), "w1p": both(a["L0_ffn_W1p"].transpose(1, 0, 2)),
        "fc2": by_feature(a["L0_attn_fc2_w"]), "w2s": by_feature(a["L0_ffn_W2s"]), "w2p": by_feature(a["L0_ffn_W2p"]),
        **constants(),
    }
    packed = {name: np.ascontiguousarray(np.concatenate([np.asarray(parts[k], np.float32) for k in starts], 1))
              for name, starts in (("stem", STEM), ("early", EARLY), ("late", LATE))}
    return {"xp": np.pad(a["x"], ((0, 0), (1, 2), (0, 0))), **packed}


def kernel(**inputs):
    import concourse.bacc as bacc
    from concourse.bass_utils import run_bass_kernel_spmd

    nc = bacc.Bacc("TRN2", target_bir_lowering=False, num_devices=1)
    arrays, aps = {}, []
    laid = lay_out({k: np.asarray(v) for k, v in inputs.items()})
    for name in ("xp", "stem", "early", "late"):
        arrays[f"in_{name}_dram"] = laid[name]
        aps.append(nc.dram_tensor(f"in_{name}_dram", laid[name].shape, F32, kind="ExternalInput").ap())
    out = nc.dram_tensor("out_0_dram", (NB, T, C), F32, kind="ExternalOutput").ap()
    build(nc, *aps, out)
    r = run_bass_kernel_spmd(nc, [arrays], core_ids=[0])
    return r.results[0]["out_0_dram"]
```

```python
from contextlib import ExitStack

import numpy as np

import concourse.bass as bass
from concourse import mybir

F32 = mybir.dt.float32
F16 = mybir.dt.float16
U32 = mybir.dt.uint32
ALU = mybir.AluOpType
ACT = mybir.ActivationFunctionType
AX = mybir.AxisListType.X

P = 128
C = 64
E = 8
FF = 256
NB, T2 = 16, 256
T = T2 // 2
GN_EPS = 1e-3
LN_EPS = 1e-5
TAPS = 5
HASHES, BUCKETS, HEADS = 4, 8, 8
M = HASHES * BUCKETS
GB = 4
GROUPS = NB // GB
TOK = GB * T
PAIRS = E // 2
CHUNKS = 2 + 2 * E
STEPS = CHUNKS // 2
HB = GB * 8 // 2
MASKED = float(2.0 ** 100)
TINY = 1e-30
FULL = 8192.0

STAGE = [
    ("dve", 0, 0.4, []), ("pe", 0, 0.2, ["dve0"]), ("dve", 1, 0.4, ["pe0"]), ("act", 1, 0.35, ["dve1"]),
    ("dve", 2, 0.4, ["act1"]), ("pe", 2, 0.2, ["dve2"]), ("dve", 3, 0.1, ["pe2"]), ("pool", 3, 1.0, ["dve3"]),
    ("dve", 4, 3.45, ["pool3"]), ("pool", 4, 1.0, ["dve4"]), ("pool", 8, 1.5, ["pool4"]), ("dve", 5, 1.2, ["pool4"]),
    ("act", 9, 1.3, ["pool8"]),
    ("pool", 5, 0.65, ["dve5"]), ("pe", 5, 0.25, ["pool5"]), ("act", 6, 0.5, ["pe5"]),
    ("pe", 6, 1, ["act6"]), ("dve", 6, 1.5, ["pe6"]), ("act", 7, 0.7, ["pe6"]), ("pool", 6, 0.7, ["dve4"]),
    ("pe", 7, 0.25, ["dve6"]), ("dve", 7, 0.6, ["pe7"]), ("pe", 8, 0.2, ["dve7"]), ("act", 8, 0.55, ["pe8"]),
    ("pe", 9, 1.05, ["act8"]), ("dve", 9, 1.2, ["pe9"]), ("dve", 19, 0.6, ["pe9"]),
    ("pe", 10, 1.0, ["dve9", "act7"]), ("dve", 10, 1.3, ["pe10"]), ("act", 10, 0.5, ["dve10"]),
    ("pe", 11, 0.5, ["act10"]), ("act", 11, 0.5, ["pe11"]), ("pe", 12, 0.9, ["act11", "dve19"]),
    ("pe", 20, 0.9, ["pe10"]), ("dve", 20, 1.3, ["pe20", "dve10"]), ("act", 20, 0.5, ["dve20", "act10"]),
    ("pe", 21, 0.5, ["act20", "pe11"]), ("act", 21, 0.5, ["pe21", "act11"]), ("pe", 22, 0.9, ["act21", "pe12"]),
    ("dve", 12, 2.5, ["pe22", "act9"]), ("pool", 12, 1.0, ["dve12"]), ("dve", 13, 1.2, ["pool12"]),
    ("pool", 13, 0.65, ["dve13"]), ("pool", 14, 0.7, ["dve12", "pool6"]),
    ("pe", 13, 0.25, ["pool13"]), ("act", 14, 0.5, ["pe13"]), ("pe", 14, 0.9, ["act14"]), ("act", 15, 1.35, ["pe14"]),
    ("pe", 15, 1.7, ["act15"]), ("dve", 15, 1.65, ["pe15", "pool14"]), ("pool", 15, 1.0, ["dve15"]),
    ("dve", 16, 1.2, ["pool15"]), ("pool", 16, 0.65, ["dve16"]), ("pe", 16, 0.25, ["pool16"]),
    ("act", 17, 0.5, ["pe16"]),
]
RINGS = [(("stage", "act", 7), ("stage", "pe", 22)), (("stage", "dve", 9), ("stage", "pe", 22)), (("stage", "pool", 6), ("stage", "dve", 15)),
         (("stage", "pe", 12), ("stage", "act", 17)), (("stage", "pe", 15), ("fold", "dve", 0)),
         (("stage", "pe", 16), ("up", "pe", CHUNKS - 1)), (("down", "act", 0), ("fold", "pe", 0))]
BANKS = [("stage", 0, "U", "dve", 1), ("stage", 2, "T", "dve", 3), ("stage", 5, "U", "act", 6),
         ("stage", 6, "T", "dve", 6), ("stage", 6, "S0", "act", 7), ("stage", 7, "U", "dve", 7),
         ("stage", 8, "T", "act", 8), ("stage", 9, "U", "dve", 19), ("stage", 10, "S0", "dve", 10),
         ("stage", 20, "S1", "dve", 20), ("stage", 11, "S0", "act", 11), ("stage", 21, "S1", "act", 21),
         ("stage", 12, "T", "dve", 12), ("stage", 13, "U", "act", 14), ("stage", 14, "S0", "act", 15),
         ("stage", 14, "S1", "act", 15), ("stage", 15, "T", "dve", 15), ("stage", 16, "U", "act", 17),
         ("route", 0, "T", "dve", 0), ("route", 3, "U", "dve", 3)] + [("spread", j, f"S{j % 2}", "dve", j) for j in range(PAIRS)]
PREP = [("act", 0, 2.1, [("stage", "act", 1)]), ("dve", 0, 0.7, ["act0"]), ("pool", 0, 0.5, ["dve0"]),
        ("pe", 0, 0.8, ["act0"]),
        ("dve", 1, 0.6, ["pool0"]), ("act", 1, 2.0, ["dve1", "pe0"]), ("dve", 2, 0.7, ["act1"]),
        ("dve", 3, 1.4, ["dve2"]), ("pool", 3, 0.5, ["dve3"]), ("dve", 4, 0.6, ["pool3"]), ("act", 4, 2.4, ["dve4"]),
        ("act", 5, 2.4, ["act4"])] + [("pool", 5 + k, 1.25, ["act5"] if k == 0 else [f"pool{4 + k}"]) for k in range(4)]
URGENT = {("conv", "pool", 0): 28, ("fold", "dve", 0): -6, ("fold", "pe", 0): -5, ("prep", "dve", 0): 15,
          ("prep", "pe", 0): 1, ("prep", "pool", 5): -1, ("prep", "pool", 6): 2, ("prep", "pool", 7): 6,
          ("route", "act", 1): -4.2, ("route", "dve", 0): -3, ("route", "dve", 3): -8, ("route", "pe", 0): 0.2,
          ("route", "pe", 3): -2.5, ("spread", "dve", 0): -8, ("spread", "pe", 0): 2, ("stage", "act", 1): 1.5,
          ("stage", "act", 6): 2, ("stage", "act", 8): -13, ("stage", "act", 10): -2.5, ("stage", "act", 11): -3.5,
          ("stage", "act", 14): -9, ("stage", "act", 15): -5, ("stage", "act", 17): -3, ("stage", "act", 21): -0.5,
          ("stage", "dve", 0): 12, ("stage", "dve", 1): 2, ("stage", "dve", 3): -2.2, ("stage", "dve", 4): 7.1,
          ("stage", "dve", 5): 1.2, ("stage", "dve", 6): -7, ("stage", "dve", 7): -11.5, ("stage", "dve", 12): -7.6,
          ("stage", "dve", 13): -9, ("stage", "dve", 16): -2, ("stage", "dve", 19): 13, ("stage", "dve", 20): 4.7,
          ("stage", "pe", 0): 27, ("stage", "pe", 2): 3, ("stage", "pe", 5): 4, ("stage", "pe", 11): -2,
          ("stage", "pe", 12): 0.2, ("stage", "pe", 15): 1.4, ("stage", "pe", 16): 1.5, ("stage", "pe", 20): 0.5,
          ("stage", "pe", 22): 1, ("stage", "pool", 3): 4, ("stage", "pool", 4): 0.8, ("stage", "pool", 6): -1,
          ("stage", "pool", 8): 1, ("stage", "pool", 12): -7.5, ("stage", "pool", 14): -3, ("sum", "dve", 0): -9,
          ("sum", "pool", 0): -4, ("up", "act", 0): -5.3, ("up", "pe", 0): 10}
RANKED = 3.381
HOP = 0.15
BEGIN = {"pe": 5.0, "act": 0.0, "dve": 8.0, "pool": 7.0}
FILLER = 0.22
FILL = 0.6
SWITCH = 1.3
TABLES = {("stage", 10): "exp", ("stage", 20): "exp", ("stage", 15): "gelu", ("route", 1): "gelu"}


def tasks():
    table = {}

    def add(kind, g, engine, k, length, *after):
        after = [a if len(a) == 4 else (a[0], g, a[1], a[2]) for a in after]
        which = (kind, engine, k if kind in ("stage", "prep", "route") else 0)
        table[kind, g, engine, k] = (length, URGENT.get(which, 0.0), [a for a in after if a[1] >= 0])

    def names(kind, after):
        return [(kind, a.rstrip("0123456789"), int(a.lstrip("abcdefghijklmnopqrstuvwxyz"))) if isinstance(a, str) else a
                for a in after]

    for engine, k, length, after in PREP:
        add("prep", 0, engine, k, length, *names("prep", after))
    for g in range(GROUPS):
        if g > 0:
            for k in range(9):
                before = [("conv", "pool", k - 1)] if k > 0 else [("conv", g - 1, "pool", 8)] if g > 1 else []
                add("conv", g, "pool", k, 1.2 if k == 5 else 0.75, *before)
        for engine, k, length, after in STAGE:
            add("stage", g, engine, k, length, ("stage", g - 1, engine, k), *names("stage", after))
        add("route", g, "pe", 0, 0.2, ("stage", "act", 17))
        add("route", g, "dve", 0, 0.85, ("route", "pe", 0), ("route", g - 1, "dve", 2))
        add("route", g, "act", 1, 0.1, ("route", "dve", 0))
        add("route", g, "dve", 2, 1.25, ("route", "act", 1), ("route", g - 1, "pe", 3))
        add("route", g, "pe", 3, 0.25, ("route", "dve", 2))
        add("route", g, "dve", 3, 0.4, ("route", "pe", 3), ("spread", g - 1, "pe", PAIRS - 1))
        for j in range(PAIRS):
            add("spread", g, "pe", j, 0.25, ("route", "dve", 3), ("sum", g - 1, "dve", j),
                *([("spread", "pe", j - 1)] if j else []))
            add("spread", g, "dve", j, 0.6, ("spread", "pe", j))
        for n in range(CHUNKS):
            def chunk(kind, engine, m):
                return (kind, g, engine, m) if m >= 0 else (kind, g - 1, engine, m + CHUNKS)
            add("up", g, "pe", n, 0.45, ("stage", "act", 17), chunk("up", "pe", n - 1), chunk("up", "act", n - 2))
            used = CHUNKS * g + n - 4
            add("up", g, "act", n, 0.7, ("up", "pe", n), chunk("up", "act", n - 1),
                ("down", used // CHUNKS, "pe", used % CHUNKS // 2))
        for k in range(STEPS):
            waits = {0: ("sum", g - 1, "dve", PAIRS - 1), 1: ("fold", g - 1, "dve", 0), 3: ("down", "act", 0),
                     5: ("sum", "dve", 0), 7: ("sum", "dve", 1)}.get(k, ("up", "act", 2 * k + 1))
            add("down", g, "pe", k, 0.9, ("up", "act", 2 * k + 1), waits,
                ("down", "pe", k - 1) if k > 0 else ("down", g - 1, "pe", STEPS - 1))
        add("down", g, "act", 0, 0.5, ("down", "pe", 0))
        for j in range(PAIRS):
            def pair(engine, i):
                return ("sum", g, engine, i) if i >= 0 else ("sum", g - 1, engine, i + PAIRS)
            add("sum", g, "dve", j, 0.8, ("down", "pe", 2 * j + 2), ("spread", "dve", j), pair("pool", j - 2), pair("dve", j - 1))
            add("sum", g, "pool", j, 1.2, ("sum", "dve", j), ("down", "act", 0), pair("pool", j - 1))
        add("fold", g, "pe", 0, 0.45, ("sum", "pool", PAIRS - 1))
        add("fold", g, "dve", 0, 0.8, ("fold", "pe", 0))
        if g > 0:
            table["stage", g, "dve", 0][2].append(("conv", g, "pool", 8))
        for (kind, engine, k), (kind_of, engine_of, k_of) in RINGS:
            if g >= 2:
                table[kind, g, engine, k][2].append((kind_of, g - 2, engine_of, k_of))
    table["stage", 0, "pe", 5][2].append(("prep", 0, "dve", 2))
    table["up", 0, "pe", 0][2].append(("prep", 0, "pool", 8))
    return table


def schedule():
    table = tasks()
    fills, frees = {}, {}
    for kind, k, bank, engine, last in BANKS:
        for g in range(GROUPS):
            fills.setdefault((kind, g, "pe", k), []).append(bank)
            frees.setdefault((kind, g, engine, last), []).append(bank)
    rank = dict.fromkeys(table, 0.0)
    changed = True
    while changed:
        changed = False
        for turn, (length, _, after) in table.items():
            for a in after:
                if rank[a] < rank[turn] + length:
                    rank[a], changed = rank[turn] + length, True
    loaded, warm = None, False
    end, order = {}, {engine: [] for engine in ("pe", "act", "dve", "pool")}
    busy, bank_free = dict(BEGIN), dict.fromkeys(("S0", "S1", "T", "U"), 0.0)
    bank_of = dict.fromkeys(bank_free)
    followers = {turn: [] for turn in table}
    for turn, (_, _, after) in table.items():
        for a in set(after):
            followers[a].append(turn)
    missing = {turn: len(set(after)) for turn, (_, _, after) in table.items()}
    ready = [turn for turn in table if missing[turn] == 0]
    while ready:
        best = None
        for turn in ready:
            length, priority, after = table[turn]
            if any(bank_of[b] is not None for b in fills.get(turn, ())):
                continue
            start = max([busy[turn[2]]] + [end[a] + HOP * (a[2] != turn[2]) for a in after] +
                        [bank_free[b] + HOP for b in fills.get(turn, ())])
            if turn[2] == "act":
                functions = "gelu" if turn[0] == "up" else TABLES.get((turn[0], turn[3]))
                if functions not in (None, loaded):
                    start = max(start, busy["act"] + SWITCH)
            score = start - priority - RANKED * rank[turn]
            if best is None or score < best[0]:
                best = (score, start, turn, start + length)
        _, start, turn, stop = best
        idle_from = busy[turn[2]]
        end[turn] = busy[turn[2]] = stop
        ready.remove(turn)
        for other in followers[turn]:
            missing[other] -= 1
            if missing[other] == 0:
                ready.append(other)
        if turn[2] == "act":
            loaded = "gelu" if turn[0] == "up" else TABLES.get((turn[0], turn[3]), loaded)
        if turn[2] == "pe" and not warm:
            order["pe"].append(("filler", 0, int(FILL * (start - idle_from) / FILLER)))
        warm = warm or turn[0] == "up"
        order[turn[2]].append(turn[:2] + turn[3:])
        for b in fills.get(turn, ()):
            bank_of[b] = turn
        for b in frees.get(turn, ()):
            bank_of[b], bank_free[b] = None, stop
    return order


ORDER = schedule()


def expert(n):
    return (n - 2) // 4 * 2 + (n - 2) % 2


def part(n):
    return (n - 2) // 2 % 2


def columns(sections):
    at, starts = 0, {}
    for name, width in sections:
        starts[name] = at
        at += width
    return starts, at


STEM, N_STEM = columns([("conv_w", TAPS * C), ("conv_b", C), ("gamma", C), ("beta", C), ("alpha", C), ("fc2_b", C)])
EARLY, N_EARLY = columns([
    ("b1p", 2 * E), ("b1s", 2), ("fc1_b", 2), ("b2p", PAIRS), ("b2s", 1), ("g1", 1), ("b1", 1), ("g2", 1), ("b2", 1),
    ("q", C), ("rot", 16), ("fc1", FF), ("wr", E), ("kv", 2 * C),
    ("ident", P), ("hmask", HEADS), ("vmask", 2 * C), ("pri", BUCKETS), ("iota", E), ("sel", PAIRS * P),
    ("kcol", 1)])
SCAN, N_SCAN = columns([("w1s", FF // 2), ("w1p", E * FF // 2)])
LATE, N_LATE = columns([("w1s", FF), ("w1p", E * FF), ("fc2", 2 * C), ("w2s", 2 * C), ("w2p", E * 2 * C)])


def constants():
    p = np.arange(P)[:, None]
    hmask = np.zeros((P, HEADS), np.float32)
    hmask[:C] = p[:C] // 8 == np.arange(HEADS)
    hmask[C] = 1.0
    chan = np.arange(C)[None, :]
    kcol = np.zeros((P, 1), np.float32)
    kcol[C], kcol[C + 1] = MASKED, -MASKED
    return {
        "ident": np.eye(P),
        "hmask": hmask,
        "vmask": np.concatenate([p // M + 4 * h == chan // 8 for h in range(2)], 1),
        "pri": np.tile(8.0 - np.arange(BUCKETS), (P, 1)),
        "iota": np.tile(np.arange(E), (P, 1)),
        "sel": np.concatenate([(p % 8 == 2 * j + np.arange(P)[None, :] // C) & (p < 16) for j in range(PAIRS)], 1),
        "kcol": kcol,
    }


def build(nc, xp, stem_d, early_d, scan_d, late_d, out):
    (WQ, WROT, WFC1, WR, W1S, W1P), NW = (0, 64, 96, 352, 360, 616), 616 + E * FF
    SEGS = [(WQ, C), (WROT, 32), (WFC1, FF), (WR, E), (W1S, FF), (W1P, E * FF)]
    HEAD = 4

    ctx = ExitStack()
    with ctx:
        def sb(name, shape, dt=F32):
            return ctx.enter_context(nc.sbuf_tensor(name, shape, dt))

        def own(name, shape, dt=F32):
            every = [sb(f"{name}_{g}", shape, dt) for g in range(GROUPS)]
            return lambda g: every[g]

        def ring(name, shape, dt=F32):
            pair = [sb(f"{name}{k}", shape, dt) for k in range(2)]
            return lambda g: pair[g % 2]

        stem = sb("stem", [P, N_STEM])
        early = sb("early", [P, N_EARLY])
        late = sb("late", [P, N_LATE])
        scan = sb("scan", [P, N_SCAN])
        ident16 = sb("ident16", [P, P], F16)
        sel16 = sb("sel16", [16, PAIRS, P], F16)
        ones_mean = sb("ones_mean", [P, P])
        ones_row = sb("ones_row", [1, P])
        nhalf = sb("nhalf", [P, 8])
        x_taps = sb("x_taps", [P, GROUPS, GB, TAPS * C])
        prod = sb("prod", [P, GB, TAPS * C])
        y_all = sb("y_all", [P, NB, C])
        wall = sb("wall", [P, WR])
        w_hi = sb("w_hi", [P, NW], F16)
        w_lo = sb("w_lo", [P, NW], F16)
        w_amax = sb("w_amax", [P, 6])
        w_max = sb("w_max", [P, 6])
        w_some = sb("w_some", [P, 6])
        w_pow = sb("w_pow", [P, 6])
        w_scale = sb("w_scale", [P, 6])
        w_inv = sb("w_inv", [P, 6])
        inv_q = sb("inv_q", [P, 1])
        inv_r = sb("inv_r", [P, 1])
        gb1 = sb("gb1", [C, C + 1])
        kaug = sb("kaug", [C + 2, C + 1])
        vaug = sb("vaug", [C + 2, C])
        bq = sb("bq", [C, 1])
        brot = sb("brot", [1, GB, HASHES, 2, 4])
        bfc1 = sb("bfc1", [P, 2])

        ysum = own("ysum", [P, GB])
        yc = own("yc", [P, GB, C])
        ysq = own("ysq", [P, GB, C])
        sqs = own("sqs", [P, GB])
        gve = own("gve", [P, GB])
        grstd = own("grstd", [P, GB])
        h1 = own("h1", [P, GB, C])
        st = own("st", [P, 3, GB, 6])
        mv = own("mv", [P, 3, GB, 2])
        vv1 = own("vv1", [P, 2, GB])
        rr1 = own("rr1", [P, 2, GB])
        nr0 = own("nr0", [P, GB])
        nb0 = own("nb0", [P, GB])
        vv2 = ring("vv2", [P, GB])
        rr2 = ring("rr2", [P, GB])
        vv3 = ring("vv3", [P, GB])
        rr3 = ring("rr3", [P, GB])
        xhat = own("xhat", [P, GB, C + 1])
        xa = own("xa", [P, GB, C])
        xs1 = own("xs1", [P, GB, 2, C], F16)
        xT1 = own("xT1", [P, TOK], F16)
        qT = ring("qT", [C + 1, TOK])
        rmax = own("rmax", [P, GB * HASHES])
        req = own("req", [P, GB * HASHES, BUCKETS])
        rfirst = own("rfirst", [P, GB * HASHES])
        oh = own("oh", [P, GB, M])
        cnt = own("cnt", [P, 1])
        rcnt = own("rcnt", [P, 1])
        pooled = own("pooled", [P, C + 2])
        pT = own("pT", [C + 2, GB, 4, M])
        kbd = ring("kbd", [C + 1, GB, HEADS, M])
        vbd = ring("vbd", [P, GB, 2, C + HEADS])
        smax = own("smax", [P, GB * HEADS])
        sexp = ring("sexp", [P, GB * HEADS, M])
        eT = ring("eT", [P, GB * 2, P])
        rden = ring("rden", [P, GB, HEADS])
        r = ring("r", [P, GB, C])
        rb = ring("rb", [P, GB, C])
        yhat = ring("yhat", [P, GB, C])
        xs2 = ring("xs2", [P, GB, 2, C], F16)
        xT2 = ring("xT2", [P, TOK], F16)
        fg = ring("fg", [P, 2, TOK])
        h2 = ring("h2", [P, GB, C])
        xf = ring("xf", [P, GB, C])
        xs3 = ring("xs3", [P, GB, 2, C], F16)
        xT3 = ring("xT3", [P, TOK], F16)

        v8 = sb("v8", [P, GB, 8])
        i8 = sb("i8", [P, GB, 8], U32)
        oh2 = sb("oh2", [P, GB, 2, E])
        dlt = sb("dlt", [P, GB])
        th = sb("th", [P, GB])
        tw = sb("tw", [P, GB, 2])
        mask = sb("mask", [P, GB, E])
        ms = sb("ms", [P, GB, 2, E], F16)
        maskT = sb("maskT", [16, TOK], F16)
        mbc = sb("mbc", [P, PAIRS, TOK])
        g_ring = sb("g_ring", [P, 4, TOK])
        zt = sb("zt", [P, 2, TOK])
        zsum = ring("zsum", [P, TOK])
        ot = ring("ot", [P, GB, C])

        def bank(name, shape):
            return ctx.enter_context(nc.psum_tensor(name, shape, F32))

        H = bank("H", [P, 2, 512])
        Y = bank("Y", [P, 2, 512])
        S = bank("S", [P, 2, 512])
        Tb = bank("Tb", [P, 512])
        Ub = bank("Ub", [P, 512])
        misc, misc_kv = Y[:, 0, :], Y[:, 1, :]
        U16 = Ub[:, :].bitcast(F16)

        names = """
            augmented x_in0 x_in1 x_in2 x_in3 stem_in early_in scan_in late_in static pool_step prep_step
            gb1 misc_ps rot_wall wall brot_half consts16 amax_head amax_rest wmax_head wmax_rest scale_head scale_rest
            hi_head hi_rest scaled_rest lo_head lo_rest last_tap conv0 conv_rest
            stage_step ysum mean yc ysq sqs var gve grstd vv1 rr1 rr0 nr0 nb0 xa xh1 xl1 xt1_ps xT1 q_ps qT rot_ps
            oh pool_ps pooled pt_ps pT kv_ps kbd vbd scores ssub sexp et_ps eT pv_ps r rb
            vv2 rr2 yh yl xt2_ps xT2 fc1_ps fg fc2_ps h2 vv3 rr3 xh3 xl3 xt3_ps xT3
            moe_step router best th_in th ms maskt_ps maskT mbc_ps mbc
            mm1 gelu mm2 zsum_init z zadd folded ot stored0 stored1 stored2 stored3
        """.split()
        s = {n: ctx.enter_context(nc.semaphore(n)) for n in names}

        class Chain:

            def __init__(self, eng, sem):
                self.eng, self.sem, self.n = eng, sem, 0

            def link(self, ins):
                self.n += 1
                ins.then_inc(self.sem, 1)
                self.eng.wait_ge(self.sem, self.n)

        def bc(ap, axis, shape):
            return ap.unsqueeze(axis).to_broadcast(shape)

        def sec(name, n, rows=P):
            return early[0:rows, EARLY[name]:EARLY[name] + n]

        def stem_row(name):
            return bc(stem[:, STEM[name]:STEM[name] + C], 1, [P, GB, C])

        def seg_src(k):
            at, n = SEGS[k]
            if k < 3:
                return wall[:, at:at + n]
            return sec("wr", n) if k == 3 else late[:, LATE["w1s" if k == 4 else "w1p"]:][:, 0:n]

        def late_w(name, *dims):
            return late[:, LATE[name]:LATE[name] + int(np.prod(dims)) * C]

        fc2w = late_w("fc2", 2).rearrange("p (c d) -> p c d", d=C)
        w2s = late_w("w2s", 2).rearrange("p (c d) -> p c d", d=C)
        w2p = late_w("w2p", E, 2).rearrange("p (e c d) -> p e c d", e=E, d=C)
        CW = stem[:, STEM["conv_w"]:STEM["conv_w"] + TAPS * C]

        stored = [s[f"stored{g}"] for g in range(GROUPS)]
        x_in = [s[f"x_in{g}"] for g in range(GROUPS)]
        XROW = xp.shape[1] * C

        block = ctx.enter_context(nc.Block())

        @block.sync
        def _(sp):
            for g in range(GROUPS):
                src = bass.AP(xp.tensor, g * GB * XROW, [[2 * C, P], [XROW, GB], [1, TAPS * C]])
                sp.dma_start(x_taps[:, g, :, :], src).then_inc(x_in[g], 16)
                if g == 1:
                    sp.dma_start(early[:, :], early_d).then_inc(s["early_in"], 16)
                    sp.dma_start(scan[:, :], scan_d).then_inc(s["scan_in"], 16)
                    sp.dma_start(late[:, :], late_d).then_inc(s["late_in"], 16)
            for g in range(GROUPS):
                sp.wait_ge(s["ot"], g + 1)
                sp.dma_start(out[GB * g:GB * g + GB].rearrange("b t c -> t b c"), ot(g)[:, :, :]).then_inc(stored[g], 16)
            for g in range(GROUPS):
                sp.wait_ge(stored[g], 16)

        @block.gpsimd
        def _(pool):
            chain = Chain(pool, s["pool_step"])

            for ap, value in [(ones_mean[:, :], 1.0 / (T * C)), (nhalf[:, :], -0.5), (ones_row[:, :], 1.0),
                              (vaug[:, :], 0.0), (kaug[:, :], 0.0)] + [(qT(k)[C:C + 1, :], 1.0) for k in range(2)] + [
                                  d for g in range(GROUPS) for d in ((xhat(g)[:, :, C:C + 1], 1.0), (pooled(g)[:, C + 1:C + 2], 1.0))]:
                chain.link(pool.memset(ap, value))
            pool.sem_inc(s["static"], 1)

            def conv_piece(g, k):
                if k == 0:
                    pool.wait_ge(s["stem_in"], 16)
                    pool.wait_ge(x_in[g], 16)
                if k < 5:
                    tap = slice(C * k, C * k + C)
                    chain.link(pool.tensor_tensor(prod[:, :, tap], x_taps[:, g, :, tap], bc(CW[:, tap], 1, [P, GB, C]), ALU.mult))
                elif k < 7:
                    a, b, n = ((0, 128, 128), (0, 64, 64))[k - 5]
                    chain.link(pool.tensor_tensor(prod[:, :, a:a + n], prod[:, :, a:a + n], prod[:, :, b:b + n], ALU.add))
                elif k == 7:
                    chain.link(pool.tensor_tensor(prod[:, :, 0:64], prod[:, :, 0:64], prod[:, :, 256:320], ALU.add))
                else:
                    ins = pool.tensor_tensor(y_all[:, GB * g:GB * g + GB, :], prod[:, :, 0:64], stem_row("conv_b"), ALU.add)
                    ins.then_inc(s["conv_rest"], 1)
                    pool.wait_ge(s["conv_rest"], g)

            def rsqrt(ready, out_ap, in_ap, exponent, done, g):
                pool.wait_ge(s[ready], g + 1)
                pool.tensor_tensor(out_ap, in_ap, exponent, ALU.pow).then_inc(s[done], 1)

            def split_low(xs, full, high, done, g):
                pool.wait_ge(s[high], g + 1)
                pool.tensor_tensor(xs[:, :, 1, :], full, xs[:, :, 0, :], ALU.subtract).then_inc(s[done], 1)

            def sum_pair(g, j):
                if j == 0:
                    pool.wait_ge(s["zsum_init"], g + 1)
                else:
                    pool.wait_ge(s["zadd"], PAIRS * g + j)
                pool.wait_ge(s["z"], PAIRS * g + j + 1)
                pool.tensor_tensor(zsum(g)[:, :], zsum(g)[:, :], zt[:, j % 2, :], ALU.add).then_inc(s["zadd"], 1)

            def stage(g, slot):
                if slot == 3:
                    rsqrt("gve", grstd(g)[:, :], gve(g)[:, :], nhalf[:, 0:GB], "grstd", g)
                elif slot == 4:
                    rsqrt("vv1", rr1(g)[:, 1, :], vv1(g)[:, 1, :], nhalf[:, 0:GB], "rr1", g)
                elif slot == 8:
                    rsqrt("vv1", rr1(g)[:, 0, :], vv1(g)[:, 0, :], nhalf[:, 0:GB], "rr0", g)
                    pool.wait_ge(s["rr0"], g + 1)
                    pool.tensor_scalar(nr0(g)[:, :], rr1(g)[:, 0, :], -1.0, None, ALU.mult).then_inc(s["nr0"], 1)
                    pool.wait_ge(s["nr0"], g + 1)
                    pool.tensor_tensor(nb0(g)[:, :], nr0(g)[:, :], mv(g)[:, 0, :, 0], ALU.mult).then_inc(s["nb0"], 1)
                elif slot == 5:
                    split_low(xs1(g), xhat(g)[:, :, 0:C], "xh1", "xl1", g)
                elif slot == 6:
                    if g >= 2:
                        pool.wait_ge(s["h2"], g - 1)
                    chain.link(pool.tensor_tensor(rb(g)[:, :, :], h1(g)[:, :, :], stem_row("fc2_b"), ALU.add))
                elif slot == 12:
                    rsqrt("vv2", rr2(g)[:, :], vv2(g)[:, :], nhalf[:, 0:GB], "rr2", g)
                elif slot == 13:
                    split_low(xs2(g), yhat(g)[:, :, :], "yh", "yl", g)
                elif slot == 14:
                    pool.tensor_tensor(rb(g)[:, :, :], rb(g)[:, :, :], r(g)[:, :, :], ALU.add).then_inc(s["rb"], 1)
                elif slot == 15:
                    rsqrt("vv3", rr3(g)[:, :], vv3(g)[:, :], nhalf[:, 0:GB], "rr3", g)
                elif slot == 16:
                    split_low(xs3(g), xf(g)[:, :, :], "xh3", "xl3", g)

            def maxima(lo, hi, ready, done):
                pool.wait_ge(s[ready], 1)
                pool.partition_all_reduce(w_max[:, lo:hi], w_amax[:, lo:hi], P, bass.bass_isa.ReduceOp.max).then_inc(s[done], 1)

            def prep(_, k):
                if k == 0:
                    maxima(0, HEAD, "amax_head", "wmax_head")
                elif k == 3:
                    maxima(HEAD, 6, "amax_rest", "wmax_rest")
                elif k >= 5:
                    n = (1 + E) * FF // 4
                    at = (k - 5) * n
                    pool.wait_ge(s["scaled_rest"], 1)
                    pool.tensor_tensor(w_lo[:, W1S + at:W1S + at + n], late[:, LATE["w1s"] + at:LATE["w1s"] + at + n],
                                       w_hi[:, W1S + at:W1S + at + n], ALU.subtract).then_inc(s["lo_rest"], 1)

            first = y_all[:, 0:GB, :]
            pool.wait_ge(s["stem_in"], 16)
            pool.wait_ge(x_in[0], 16)
            chain.link(pool.tensor_tensor(first, x_taps[:, 0, :, 256:320], bc(CW[:, 256:320], 1, [P, GB, C]), ALU.mult))
            pool.tensor_tensor(first, first, stem_row("conv_b"), ALU.add).then_inc(s["last_tap"], 1)
            for kind, g, k in ORDER["pool"]:
                {"prep": prep, "conv": conv_piece, "stage": stage, "sum": sum_pair}[kind](g, k)

        @block.scalar
        def _(act):
            act.dma_start(stem[:, :], stem_d).then_inc(s["stem_in"], 16)

            def high_parts(lo, hi, scaled, done):
                act.wait_ge(s[scaled], 1)
                for k in range(lo, hi):
                    at, n = SEGS[k]
                    ins = act.activation(w_hi[:, at:at + n], seg_src(k), ACT.Copy, scale=w_scale[:, k:k + 1])
                ins.then_inc(s[done], 1)

            def copy(ready, out_ap, in_ap, done, g):
                act.wait_ge(s[ready], g + 1)
                act.activation(out_ap, in_ap, ACT.Copy).then_inc(s[done], 1)

            def up(g, m):
                n = CHUNKS * g + m
                act.wait_ge(s["mm1"], n + 1)
                if n >= 4:
                    act.wait_ge(s["mm2"], (n - 4) // 2 + 1)
                shared = m < 2
                col = EARLY["b1s"] + m if shared else EARLY["b1p"] + 2 * expert(m) + part(m)
                act.activation(g_ring[:, n % 4, :], H[:, n % 2, :], ACT.Gelu, bias=early[:, col:col + 1],
                               scale=w_inv[:, 4:5] if shared else w_inv[:, 5:6]).then_inc(s["gelu"], 1)

            def route(g, k):
                if k == 1:
                    act.wait_ge(s["th_in"], g + 1)
                    act.activation(th[:, :], dlt[:, :], ACT.Tanh, scale=inv_r[:, 0:1]).then_inc(s["th"], 1)

            def down(g, _):
                if g >= 2:
                    act.wait_ge(s["folded"], g - 1)
                act.wait_ge(s["mm2"], STEPS * g + 1)
                act.activation(zsum(g)[:, :], Y[:, 0, :], ACT.Identity, bias=sec("b2s", 1)).then_inc(s["zsum_init"], 1)

            def stage(g, slot):
                if slot == 1:
                    act.wait_ge(s["yc"], g + 1)
                    act.activation(ysq(g)[:, :, :], yc(g)[:, :, :], ACT.Square).then_inc(s["ysq"], 1)
                elif slot == 8:
                    copy("pt_ps", pT(g)[:, :, :, :], Tb[0:C + 2, 0:P].rearrange("c (b m) -> c b m", b=GB).unsqueeze(2)
                         .to_broadcast([C + 2, GB, 4, M]), "pT", g)
                elif slot == 9:
                    act.wait_ge(s["nb0"], g + 1)
                    for b in range(GB):
                        ins = act.activation(xa(g)[:, b, :], h1(g)[:, b, :], ACT.Identity, bias=nb0(g)[:, b:b + 1],
                                             scale=rr1(g)[:, 0, b:b + 1])
                    ins.then_inc(s["xa"], 1)
                elif slot in (10, 20):
                    half = sexp(g)[:, HB * (slot == 20):HB * (slot == 20) + HB, :]
                    act.wait_ge(s["ssub"], 2 * g + slot // 10)
                    act.activation(half, half, ACT.Exp).then_inc(s["sexp"], 1)
                elif slot in (11, 21):
                    h = slot // 20
                    act.wait_ge(s["et_ps"], 2 * g + h + 1)
                    act.activation(eT(g)[:, GB * h:GB * h + GB, :].rearrange("p a b -> p (a b)"), S[:, h, :],
                                   ACT.Copy).then_inc(s["eT"], 1)
                elif slot == 6:
                    copy("xt1_ps", xT1(g)[:, :], U16[:, 0:TOK], "xT1", g)
                elif slot == 7:
                    act.wait_ge(s["q_ps"], g + 1)
                    if g >= 2:
                        act.wait_ge(s["pv_ps"], 2 * (g - 1))
                    act.activation(qT(g)[0:C, :], S[0:C, 0, :], ACT.Identity, bias=bq[:, 0:1],
                                   scale=inv_q[0:C, 0:1]).then_inc(s["qT"], 1)
                elif slot == 14:
                    copy("xt2_ps", xT2(g)[:, :], U16[:, 0:TOK], "xT2", g)
                elif slot == 15:
                    for c in range(2):
                        act.wait_ge(s["fc1_ps"], 2 * g + c + 1)
                        act.activation(fg(g)[:, c, :], S[:, c, :], ACT.Gelu, bias=bfc1[:, c:c + 1],
                                       scale=w_inv[:, 2:3]).then_inc(s["fg"], 1)
                elif slot == 17:
                    if g >= 2:
                        act.wait_ge(s["mm1"], CHUNKS * (g - 1))
                    copy("xt3_ps", xT3(g)[:, :], U16[:, 0:TOK], "xT3", g)


            def prep(_, k):
                if k == 0:
                    act.wait_ge(s["early_in"], 16)
                    wrot = wall[:, WROT:WROT + 32].rearrange("p (h k i) -> p h k i", h=HASHES, k=2)
                    act.activation(gb1[:, 0:C], sec("ident", C, C), ACT.Copy, scale=sec("g1", 1, C))
                    act.activation(gb1[:, C:C + 1], sec("b1", 1, C), ACT.Copy).then_inc(s["gb1"], 1)
                    act.activation(wrot[:, :, 0, :], sec("rot", 16).rearrange("p (h i) -> p h i", h=HASHES), ACT.Copy,
                                   scale=sec("g1", 1)).then_inc(s["rot_wall"], 1)
                    act.activation(wall[:, WQ:WQ + C], sec("q", C), ACT.Copy, scale=sec("g1", 1))
                    act.activation(wall[:, WFC1:WFC1 + FF], sec("fc1", FF), ACT.Copy, scale=sec("g2", 1))
                    act.wait_ge(s["rot_wall"], 1)
                    act.activation(wrot[:, :, 1, :], wrot[:, :, 0, :], ACT.Copy, scale=-1.0).then_inc(s["wall"], 1)
                    act.activation(ident16[:, :], sec("ident", P), ACT.Copy)
                    for k in range(2):
                        act.activation(vbd(k)[:, :, :, C:C + HEADS], sec("vmask", 2 * C).rearrange("p (k c) -> p k c", k=2)[:, :, ::8]
                                       .unsqueeze(1).to_broadcast([P, GB, 2, HEADS]), ACT.Copy)
                    act.activation(sel16[:, :, :].rearrange("p j k -> p (j k)"), sec("sel", PAIRS * P, 16), ACT.Copy).then_inc(
                        s["consts16"], 1)
                elif k == 1:
                    high_parts(0, HEAD, "scale_head", "hi_head")
                    act.wait_ge(s["misc_ps"], 1)
                    act.wait_ge(s["static"], 1)
                    act.activation(kaug[0:C + 1, 0:C], misc_kv[0:C + 1, 0:C], ACT.Copy)
                    act.activation(kaug[C:C + 2, C:C + 1], early[C:C + 2, EARLY["kcol"]:EARLY["kcol"] + 1], ACT.Copy)
                    act.activation(vaug[0:C + 1, :], misc_kv[0:C + 1, C:2 * C], ACT.Copy)
                    act.activation(bq[:, :], misc[0:C, 128:129], ACT.Copy, scale=8.0 ** -0.5)
                    act.activation(brot[:, :, :, 0, :], misc[0:1, 130:146].rearrange("p (h i) -> p h i", h=HASHES)
                                   .unsqueeze(1).to_broadcast([1, GB, HASHES, 4]), ACT.Copy,
                                   scale=w_scale[0:1, 1:2]).then_inc(s["brot_half"], 1)
                    for c in range(2):
                        act.activation(bfc1[:, c:c + 1], misc[:, 146 + c:147 + c], ACT.Identity,
                                       bias=early[:, EARLY["fc1_b"] + c:EARLY["fc1_b"] + c + 1])
                    act.wait_ge(s["brot_half"], 1)
                    act.activation(brot[:, :, :, 1, :], brot[:, :, :, 0, :], ACT.Copy, scale=-1.0).then_inc(s["augmented"], 1)
                    act.wait_ge(s["augmented"], 1)
                elif k == 4:
                    act.wait_ge(s["late_in"], 16)
                    high_parts(HEAD, 6, "scale_rest", "hi_rest")
                elif k == 5:
                    act.wait_ge(s["hi_rest"], 1)
                    for seg in range(HEAD, 6):
                        ins = act.activation(seg_src(seg), seg_src(seg), ACT.Copy, scale=w_scale[:, seg:seg + 1])
                    ins.then_inc(s["scaled_rest"], 1)

            for kind, g, k in ORDER["act"]:
                {"prep": prep, "stage": stage, "route": route, "up": up, "down": down}[kind](g, k)

        @block.vector
        def _(dve):
            pchain = Chain(dve, s["prep_step"])
            chain = Chain(dve, s["stage_step"])
            mchain = Chain(dve, s["moe_step"])

            def maxima(lo, hi, done):
                for k in range(lo, hi):
                    src = seg_src(k) if k < HEAD else scan[:, SCAN["w1s"]:SCAN["w1p"]] if k == 4 else scan[:, SCAN["w1p"]:]
                    ins = dve.tensor_reduce(w_amax[:, k:k + 1], src, AX, ALU.max, apply_absolute_value=True)
                ins.then_inc(s[done], 1)

            def scales(lo, hi, ready, done):
                dve.wait_ge(s[ready], 1)
                pchain.link(dve.tensor_scalar(w_some[:, lo:hi], w_max[:, lo:hi], TINY, None, ALU.max))
                pchain.link(dve.tensor_scalar(w_pow[:, lo:hi].bitcast(U32), w_some[:, lo:hi].bitcast(U32), 0x7F800000, None,
                                            ALU.bitwise_and))
                pchain.link(dve.tensor_scalar(w_inv[:, lo:hi], w_pow[:, lo:hi], 1.0 / FULL, None, ALU.mult))
                dve.reciprocal(w_scale[:, lo:hi], w_inv[:, lo:hi]).then_inc(s[done], 1)
                dve.wait_ge(s[done], 1)

            def low_parts(lo, hi, high, done):
                dve.wait_ge(s[high], 1)
                for k in range(lo, hi):
                    at, n = SEGS[k]
                    ins = dve.scalar_tensor_tensor(w_lo[:, at:at + n], seg_src(k), w_scale[:, k:k + 1],
                                                   w_hi[:, at:at + n], ALU.mult, ALU.subtract)
                ins.then_inc(s[done], 1)

            def conv_first():
                q = sexp(0)[:, :, :].rearrange("p a m -> p (a m)")
                q = q[:, 0:GB * TAPS * C - GB * C].rearrange("p (b n) -> p b n", b=GB)
                taps = x_taps[:, 0, :, :]
                y = y_all[:, 0:GB, :]
                dve.wait_ge(s["stem_in"], 16)
                dve.wait_ge(x_in[0], 16)
                pchain.link(dve.tensor_tensor(q, taps[:, :, 0:256], bc(CW[:, 0:256], 1, [P, GB, 4 * C]), ALU.mult))
                pchain.link(dve.tensor_tensor(q[:, :, 0:128], q[:, :, 0:128], q[:, :, 128:256], ALU.add))
                pchain.link(dve.tensor_tensor(q[:, :, 0:64], q[:, :, 0:64], q[:, :, 64:128], ALU.add))
                dve.wait_ge(s["last_tap"], 1)
                dve.tensor_tensor(y, y, q[:, :, 0:64], ALU.add).then_inc(s["conv0"], 1)
                dve.wait_ge(s["conv0"], 1)

            def stats(k, src, g):
                for b in range(GB):
                    ins = dve.bn_stats(st(g)[:, k, b, :], src[:, b, :])
                chain.link(ins)
                for b in range(GB):
                    ins = dve.bn_aggr(mv(g)[:, k, b, :], st(g)[:, k, b, :])
                chain.link(ins)

            def normalise(k, dst, src, rstd, g):
                for b in range(GB):
                    ins = dve.tensor_scalar(dst[:, b, 0:C], src[:, b, :], mv(g)[:, k, b, 0:1], rstd[:, b:b + 1],
                                            ALU.subtract, ALU.mult)
                return ins

            def route(g, k):
                if k == 0:
                    dve.wait_ge(s["router"], g + 1)
                    for b in range(GB):
                        ins = dve.max(v8[:, b, :], Tb[:, E * b:E * b + E])
                    mchain.link(ins)
                    dve.tensor_tensor(dlt[:, :], v8[:, :, 1], v8[:, :, 0], ALU.subtract).then_inc(s["th_in"], 1)
                    for b in range(GB):
                        ins = dve.max_index(i8[:, b, :], v8[:, b, :], Tb[:, E * b:E * b + E])
                    ins.then_inc(s["best"], 1)
                    dve.wait_ge(s["best"], g + 1)
                    mchain.link(dve.tensor_tensor(
                        oh2[:, :, :, :], sec("iota", E).unsqueeze(1).unsqueeze(1).to_broadcast([P, GB, 2, E]),
                        i8[:, :, 0:2].unsqueeze(3).to_broadcast([P, GB, 2, E]), ALU.is_equal))
                elif k == 2:
                    if g > 0:
                        dve.wait_ge(s["maskt_ps"], g)
                    dve.wait_ge(s["th"], g + 1)
                    dve.tensor_scalar(tw[:, :, 0], th[:, :], -0.5, 0.5, ALU.mult, ALU.add)
                    mchain.link(dve.tensor_scalar(tw[:, :, 1], th[:, :], 0.5, 0.5, ALU.mult, ALU.add))
                    mchain.link(dve.tensor_tensor(oh2[:, :, :, :], oh2[:, :, :, :],
                                                  tw[:, :, :].unsqueeze(3).to_broadcast([P, GB, 2, E]), ALU.mult))
                    mchain.link(dve.tensor_tensor(mask[:, :, :], oh2[:, :, 0, :], oh2[:, :, 1, :], ALU.add))
                    mchain.link(dve.tensor_copy(ms[:, :, 0, :], mask[:, :, :]))
                    dve.tensor_tensor(ms[:, :, 1, :], mask[:, :, :], ms[:, :, 0, :], ALU.subtract).then_inc(s["ms"], 1)

                elif k == 3:
                    dve.wait_ge(s["maskt_ps"], g + 1)
                    if g > 0:
                        dve.wait_ge(s["mbc_ps"], PAIRS * g)
                    dve.tensor_copy(maskT[:, :], U16[0:16, 0:TOK]).then_inc(s["maskT"], 1)

            def spread(g, j):
                if g > 0:
                    dve.wait_ge(s["z"], PAIRS * (g - 1) + j + 1)
                dve.wait_ge(s["mbc_ps"], PAIRS * g + j + 1)
                dve.tensor_copy(mbc[:, j, :], S[:, j % 2, :]).then_inc(s["mbc"], 1)

            def sum_pair(g, j):
                dve.wait_ge(s["mm2"], STEPS * g + 3 + 2 * j)
                dve.wait_ge(s["mbc"], PAIRS * g + j + 1)
                if PAIRS * g + j >= 2:
                    dve.wait_ge(s["zadd"], PAIRS * g + j - 1)
                dve.scalar_tensor_tensor(zt[:, j % 2, :], Y[:, (j + 1) % 2, :],
                                         early[:, EARLY["b2p"] + j:EARLY["b2p"] + j + 1],
                                         mbc[:, j, :], ALU.add, ALU.mult).then_inc(s["z"], 1)

            def fold(g, _):
                dve.wait_ge(s["folded"], g + 1)
                if g >= 2:
                    dve.wait_ge(stored[g - 2], 16)
                halves = Y[:, 1, :].rearrange("p (b k c) -> p b k c", b=GB, k=2)
                mchain.link(dve.tensor_tensor(ot(g)[:, :, :], halves[:, :, 0, :], h2(g)[:, :, :], ALU.add))
                dve.tensor_tensor(ot(g)[:, :, :], halves[:, :, 1, :], ot(g)[:, :, :], ALU.add).then_inc(s["ot"], 1)

            def stage(g, slot):
                y = y_all[:, GB * g:GB * g + GB, :]
                hashed = [P, GB * HASHES, BUCKETS]
                if slot == 0:
                    if g > 0:
                        dve.wait_ge(s["conv_rest"], g)
                    dve.tensor_reduce(ysum(g)[:, :], y, AX, ALU.add).then_inc(s["ysum"], 1)
                elif slot == 1:
                    dve.wait_ge(s["mean"], g + 1)
                    dve.tensor_tensor(yc(g)[:, :, :], y, bc(Ub[:, 0:GB], 2, [P, GB, C]), ALU.subtract).then_inc(s["yc"], 1)
                elif slot == 2:
                    dve.wait_ge(s["ysq"], g + 1)
                    dve.tensor_reduce(sqs(g)[:, :], ysq(g)[:, :, :], AX, ALU.add).then_inc(s["sqs"], 1)
                elif slot == 3:
                    dve.wait_ge(s["var"], g + 1)
                    dve.tensor_scalar(gve(g)[:, :], Tb[:, 0:GB], GN_EPS, None, ALU.add).then_inc(s["gve"], 1)
                elif slot == 4:
                    dve.wait_ge(s["grstd"], g + 1)
                    for b in range(GB):
                        ins = dve.scalar_tensor_tensor(yc(g)[:, b, :], yc(g)[:, b, :], grstd(g)[:, b:b + 1],
                                                       stem[:, STEM["gamma"]:STEM["gamma"] + C], ALU.mult, ALU.mult)
                    chain.link(ins)
                    chain.link(dve.tensor_tensor(yc(g)[:, :, :], yc(g)[:, :, :], stem_row("beta"), ALU.add))
                    chain.link(dve.scalar_tensor_tensor(ysq(g)[:, :, :], yc(g)[:, :, :], 0.0, stem_row("alpha"),
                                                        ALU.min, ALU.mult))
                    chain.link(dve.scalar_tensor_tensor(h1(g)[:, :, :], yc(g)[:, :, :], 0.0, ysq(g)[:, :, :],
                                                        ALU.max, ALU.add))
                    stats(0, h1(g), g)
                    dve.tensor_scalar(vv1(g)[:, 0, :], mv(g)[:, 0, :, 1], LN_EPS, None, ALU.add)
                    dve.tensor_scalar(vv1(g)[:, 1, :], mv(g)[:, 0, :, 1], 1.0 + LN_EPS, LN_EPS ** 2, ALU.mult,
                                      ALU.add).then_inc(s["vv1"], 1)
                elif slot == 5:
                    dve.wait_ge(s["rr1"], g + 1)
                    chain.link(normalise(0, xhat(g), h1(g), rr1(g)[:, 1, :], g))
                    dve.tensor_copy(xs1(g)[:, :, 0, :], xhat(g)[:, :, 0:C]).then_inc(s["xh1"], 1)
                elif slot == 6:
                    dve.wait_ge(s["rot_ps"], g + 1)
                    rot = Tb[:, 0:GB * M].rearrange("p (a i) -> p a i", i=BUCKETS)
                    chain.link(dve.tensor_reduce(rmax(g)[:, :], rot, AX, ALU.max))
                    chain.link(dve.tensor_tensor(req(g)[:, :, :], rot, bc(rmax(g)[:, :], 2, hashed), ALU.is_equal))
                    chain.link(dve.tensor_tensor(req(g)[:, :, :], req(g)[:, :, :], bc(sec("pri", BUCKETS), 1, hashed), ALU.mult))
                    chain.link(dve.tensor_reduce(rfirst(g)[:, :], req(g)[:, :, :], AX, ALU.max))
                    dve.tensor_tensor(oh(g)[:, :, :].rearrange("p b (h i) -> p (b h) i", i=BUCKETS), req(g)[:, :, :],
                                      bc(rfirst(g)[:, :], 2, hashed), ALU.is_equal).then_inc(s["oh"], 1)
                elif slot == 7:
                    dve.wait_ge(s["pool_ps"], g + 1)
                    chain.link(dve.tensor_scalar(cnt(g)[:, :], Ub[:, C:C + 1], 1.0, None, ALU.max))
                    chain.link(dve.reciprocal(rcnt(g)[:, :], cnt(g)[:, :]))
                    dve.tensor_scalar(pooled(g)[:, 0:C + 1], Ub[:, 0:C + 1], rcnt(g)[:, 0:1], None, ALU.mult).then_inc(
                        s["pooled"], 1)
                elif slot == 9:
                    if g >= 2:
                        dve.wait_ge(s["pv_ps"], 2 * (g - 1))
                    dve.wait_ge(s["kv_ps"], g + 1)
                    dve.tensor_tensor(
                        kbd(g)[:, :, :, :], Ub[0:C + 1, 0:P].rearrange("p (b m) -> p b m", b=GB).unsqueeze(2).to_broadcast(
                            [C + 1, GB, HEADS, M]),
                        sec("hmask", HEADS, C + 1).unsqueeze(1).unsqueeze(3).to_broadcast([C + 1, GB, HEADS, M]),
                        ALU.mult).then_inc(s["kbd"], 1)
                elif slot == 19:
                    dve.wait_ge(s["kv_ps"], g + 1)
                    dve.tensor_tensor(
                        vbd(g)[:, :, :, 0:C], Ub[:, P:P + GB * C].rearrange("p (b c) -> p b c", b=GB).unsqueeze(2).to_broadcast(
                            [P, GB, 2, C]),
                        sec("vmask", 2 * C).rearrange("p (k c) -> p k c", k=2).unsqueeze(1).to_broadcast(
                            [P, GB, 2, C]), ALU.mult).then_inc(s["vbd"], 1)
                elif slot in (10, 20):
                    h = slot // 20
                    rows = slice(HB * h, HB * h + HB)
                    dve.wait_ge(s["scores"], 2 * g + h + 1)
                    sc = S[:, h, :].rearrange("p (a m) -> p a m", m=M)
                    chain.link(dve.tensor_reduce(smax(g)[:, rows], sc, AX, ALU.max))
                    dve.tensor_tensor(sexp(g)[:, rows, :], sc, bc(smax(g)[:, rows], 2, [P, HB, M]), ALU.subtract).then_inc(
                        s["ssub"], 1)
                elif slot == 12:
                    dve.wait_ge(s["pv_ps"], 2 * (g + 1))
                    if g >= 2:
                        dve.wait_ge(s["xT3"], g - 1)
                    pv = Tb[:, :].rearrange("p (b c) -> p b c", b=GB)
                    chain.link(dve.reciprocal(rden(g)[:, :, :], pv[:, :, C:C + HEADS]))
                    chain.link(dve.tensor_tensor(
                        r(g)[:, :, :].rearrange("p b (h d) -> p b h d", h=HEADS),
                        pv[:, :, 0:C].rearrange("p b (h d) -> p b h d", h=HEADS),
                        rden(g)[:, :, :].unsqueeze(3).to_broadcast([P, GB, HEADS, 8]), ALU.mult))
                    dve.wait_ge(s["xa"], g + 1)
                    dve.tensor_tensor(r(g)[:, :, :], r(g)[:, :, :], xa(g)[:, :, :], ALU.add).then_inc(s["r"], 1)
                    dve.wait_ge(s["r"], g + 1)
                    stats(1, r(g), g)
                    dve.tensor_scalar(vv2(g)[:, :], mv(g)[:, 1, :, 1], LN_EPS, None, ALU.add).then_inc(s["vv2"], 1)
                elif slot == 13:
                    dve.wait_ge(s["rr2"], g + 1)
                    chain.link(normalise(1, yhat(g), r(g), rr2(g), g))
                    dve.tensor_copy(xs2(g)[:, :, 0, :], yhat(g)[:, :, :]).then_inc(s["yh"], 1)
                elif slot == 15:
                    dve.wait_ge(s["fc2_ps"], g + 1)
                    dve.wait_ge(s["rb"], g + 1)
                    if g >= 2:
                        dve.wait_ge(s["ot"], g - 1)
                    dve.tensor_tensor(h2(g)[:, :, :], Tb[:, 0:GB * C].rearrange("p (b c) -> p b c", b=GB), rb(g)[:, :, :],
                                      ALU.add).then_inc(s["h2"], 1)
                    dve.wait_ge(s["h2"], g + 1)
                    stats(2, h2(g), g)
                    dve.tensor_scalar(vv3(g)[:, :], mv(g)[:, 2, :, 1], LN_EPS, None, ALU.add).then_inc(s["vv3"], 1)
                elif slot == 16:
                    dve.wait_ge(s["rr3"], g + 1)
                    chain.link(normalise(2, xf(g), h2(g), rr3(g), g))
                    dve.tensor_copy(xs3(g)[:, :, 0, :], xf(g)[:, :, :]).then_inc(s["xh3"], 1)


            def prep(_, k):
                if k == 0:
                    dve.wait_ge(s["wall"], 1)
                    maxima(0, HEAD, "amax_head")
                elif k == 1:
                    scales(0, HEAD, "wmax_head", "scale_head")
                    dve.tensor_scalar(inv_q[:, :], w_inv[:, 0:1], 8.0 ** -0.5, None, ALU.mult)
                    dve.tensor_scalar(inv_r[:, :], w_inv[:, 3:4], 0.5, None, ALU.mult)
                elif k == 2:
                    low_parts(0, HEAD, "hi_head", "lo_head")
                elif k == 3:
                    dve.wait_ge(s["scan_in"], 16)
                    maxima(HEAD, 6, "amax_rest")
                elif k == 4:
                    scales(HEAD, 6, "wmax_rest", "scale_rest")

            conv_first()
            for kind, g, k in ORDER["dve"]:
                {"prep": prep, "stage": stage, "route": route, "spread": spread, "sum": sum_pair, "fold": fold}[kind](
                    g, k)

        @block.tensor
        def _(pe):
            ident = sec("ident", P)
            held = {}

            def take(*banks):
                for b in banks:
                    if b in held:
                        pe.wait_ge(*held[b])

            def lend(b, sem, value):
                held[b] = (s[sem], value)

            def split_product(out_ap, at, n, rhs):
                pe.matmul(out_ap, w_hi[:, at:at + n], rhs, start=True, stop=False)
                return pe.matmul(out_ap, w_lo[:, at:at + n], rhs, start=False, stop=True)

            def transposes(xs, low, done, g):
                take("U")
                pe.wait_ge(s[low], g + 1)
                for b in range(GB):
                    ins = pe.transpose(U16[:, P * b:P * b + P], xs[:, b, :, :].rearrange("p k c -> p (k c)"), ident16[:, :])
                ins.then_inc(s[done], 1)

            def route(g, k):
                if k == 0:
                    take("T")
                    pe.wait_ge(s["xT3"], g + 1)
                    for b in range(GB):
                        pe.matmul(Tb[:, E * b:E * b + E], xT3(g)[:, P * b:P * b + P], w_hi[:, WR:WR + E], start=True, stop=False)
                        ins = pe.matmul(Tb[:, E * b:E * b + E], xT3(g)[:, P * b:P * b + P], w_lo[:, WR:WR + E],
                                        start=False, stop=True)
                    ins.then_inc(s["router"], 1)
                    lend("T", "best", g + 1)
                elif k == 3:
                    take("U")
                    pe.wait_ge(s["ms"], g + 1)
                    for b in range(GB):
                        ins = pe.transpose(U16[0:16, P * b:P * b + P], ms[:, b, :, :].rearrange("p k e -> p (k e)"), ident16[:, :])
                    ins.then_inc(s["maskt_ps"], 1)
                    lend("U", "maskT", g + 1)

            def spread(g, j):
                take(f"S{j % 2}")
                pe.wait_ge(s["maskT"], g + 1)
                pe.matmul(S[:, j % 2, :], sel16[:, j, :], maskT[:, :], start=True, stop=True).then_inc(s["mbc_ps"], 1)
                lend(f"S{j % 2}", "mbc", PAIRS * g + j + 1)

            def up(g, m):
                n = CHUNKS * g + m
                pe.wait_ge(s["xT3"], g + 1)
                if n >= 2:
                    pe.wait_ge(s["gelu"], n - 1)
                if n == 0:
                    pe.wait_ge(s["lo_rest"], 4)
                at = W1S + P * m if m < 2 else W1P + FF * expert(m) + P * part(m)
                split_product(H[:, n % 2, :], at, P, xT3(g)[:, :]).then_inc(s["mm1"], 1)

            def down(g, k):
                j = (k - 1) // 2
                bank_ = 0 if k == 0 else (j + 1) % 2
                opens = k == 0 or k % 2 == 1
                if g == 0 and k == 0:
                    pe.wait_ge(s["augmented"], 1)
                    pe.wait_ge(s["late_in"], 16)
                if k == 0 and g > 0:
                    pe.wait_ge(s["z"], PAIRS * g)
                elif k == 1 and g > 0:
                    pe.wait_ge(s["ot"], g)
                elif k == 3:
                    pe.wait_ge(s["zsum_init"], g + 1)
                elif k > 3 and opens:
                    pe.wait_ge(s["z"], PAIRS * g + j - 1)
                pe.wait_ge(s["gelu"], CHUNKS * g + 2 * k + 2)
                for half in range(2):
                    n = 2 * k + half
                    w = w2s[:, half, :] if k == 0 else w2p[:, expert(n), part(n), :]
                    ins = pe.matmul(Y[C * half:C * half + C, bank_, :], w, g_ring[:, (CHUNKS * g + n) % 4, :],
                                    start=opens, stop=(k == 0 or not opens), skip_group_check=True)
                ins.then_inc(s["mm2"], 1)

            def fold(g, _):
                pe.wait_ge(s["zadd"], PAIRS * (g + 1))
                for b in range(GB):
                    ins = pe.transpose(Y[:, 1, P * b:P * b + P], zsum(g)[:, P * b:P * b + P], ident)
                ins.then_inc(s["folded"], 1)

            def stage(g, slot):
                if slot == 0:
                    take("U")
                    pe.wait_ge(s["ysum"], g + 1)
                    pe.matmul(Ub[:, 0:GB], ones_mean[:, :], ysum(g)[:, :], start=True, stop=True).then_inc(s["mean"], 1)
                    lend("U", "yc", g + 1)
                elif slot == 2:
                    take("T")
                    pe.wait_ge(s["sqs"], g + 1)
                    pe.matmul(Tb[:, 0:GB], ones_mean[:, :], sqs(g)[:, :], start=True, stop=True).then_inc(s["var"], 1)
                    lend("T", "gve", g + 1)
                elif slot == 5:
                    if g == 0:
                        pe.wait_ge(s["consts16"], 1)
                        pe.wait_ge(s["lo_head"], 1)
                        pe.wait_ge(s["augmented"], 1)
                    transposes(xs1(g), "xl1", "xt1_ps", g)
                    lend("U", "xT1", g + 1)
                elif slot == 6:
                    take("S0", "T")
                    pe.wait_ge(s["xT1"], g + 1)
                    pe.matmul(Tb[:, 0:GB * M], ones_row[:, :], brot[:, :, :, :, :].rearrange("p b h k i -> p (b h k i)"),
                              start=True, stop=False, skip_group_check=True)
                    for b in range(GB):
                        for w in (w_hi, w_lo):
                            ins = pe.matmul(Tb[:, M * b:M * b + M], xT1(g)[:, P * b:P * b + P], w[:, WROT:WROT + M],
                                            start=False, stop=(w is w_lo), skip_group_check=True)
                    ins.then_inc(s["rot_ps"], 1)
                    lend("T", "oh", g + 1)
                    split_product(S[0:C, 0, :], WQ, C, xT1(g)[:, :]).then_inc(s["q_ps"], 1)
                    lend("S0", "qT", g + 1)
                elif slot == 7:
                    take("U")
                    pe.wait_ge(s["oh"], g + 1)
                    for b in range(GB):
                        ins = pe.matmul(Ub[M * b:M * b + M, 0:C + 1], oh(g)[:, b, :], xhat(g)[:, b, :], start=True, stop=True,
                                        tile_position=(0, M * b))
                    ins.then_inc(s["pool_ps"], 1)
                    lend("U", "pooled", g + 1)
                elif slot == 8:
                    take("T")
                    pe.wait_ge(s["pooled"], g + 1)
                    pe.transpose(Tb[0:C + 2, 0:P], pooled(g)[:, :], ident).then_inc(s["pt_ps"], 1)
                    lend("T", "pT", g + 1)
                elif slot == 9:
                    take("U")
                    pe.wait_ge(s["pT"], g + 1)
                    pe.matmul(Ub[0:C + 1, 0:P], kaug[:, :], pT(g)[:, :, 0, :], start=True, stop=True)
                    for b in range(GB):
                        ins = pe.matmul(Ub[:, P + C * b:P + C * b + C], pT(g)[:, b, :, :].rearrange("c h m -> c (h m)"),
                                        vaug[:, :], start=True, stop=True)
                    ins.then_inc(s["kv_ps"], 1)
                    lend("U", "vbd", g + 1)
                elif slot in (10, 20):
                    h = slot // 20
                    take(f"S{h}")
                    pe.wait_ge(s["kbd"], g + 1)
                    pe.wait_ge(s["qT"], g + 1)
                    for b in (2 * h, 2 * h + 1):
                        ins = pe.matmul(S[:, b // 2, 256 * (b % 2):256 * (b % 2) + 256], qT(g)[:, P * b:P * b + P],
                                        kbd(g)[:, b, :, :].rearrange("p h m -> p (h m)"), start=True, stop=True)
                    ins.then_inc(s["scores"], 1)
                    lend(f"S{h}", "ssub", 2 * g + h + 1)
                elif slot in (11, 21):
                    h = slot // 20
                    take(f"S{h}")
                    pe.wait_ge(s["sexp"], 2 * g + h + 1)
                    for k in range(GB * h, GB * h + GB):
                        ins = pe.transpose(S[:, k // 4, P * (k % 4):P * (k % 4) + P],
                                           sexp(g)[:, 4 * k:4 * k + 4, :].rearrange("p h m -> p (h m)"), ident)
                    ins.then_inc(s["et_ps"], 1)
                    lend(f"S{h}", "eT", 2 * g + h + 1)
                elif slot in (12, 22):
                    h = slot // 20
                    if h == 0:
                        take("T")
                        pe.wait_ge(s["vbd"], g + 1)
                    pe.wait_ge(s["eT"], 2 * g + h + 1)
                    for b in (2 * h, 2 * h + 1):
                        for half in range(2):
                            ins = pe.matmul(Tb[:, P * b:P * b + C + HEADS], eT(g)[:, 2 * b + half, :], vbd(g)[:, b, half, :],
                                            start=(half == 0), stop=(half == 1))
                    ins.then_inc(s["pv_ps"], 1)
                    lend("T", "r", g + 1)
                elif slot == 13:
                    transposes(xs2(g), "yl", "xt2_ps", g)
                    lend("U", "xT2", g + 1)
                elif slot == 14:
                    pe.wait_ge(s["xT2"], g + 1)
                    for c in range(2):
                        take(f"S{c}")
                        split_product(S[:, c, :], WFC1 + P * c, P, xT2(g)[:, :]).then_inc(s["fc1_ps"], 1)
                        lend(f"S{c}", "fg", 2 * g + c + 1)
                elif slot == 15:
                    take("T")
                    if g == 0:
                        pe.wait_ge(s["late_in"], 16)
                    pe.wait_ge(s["fg"], 2 * (g + 1))
                    for b in range(GB):
                        for c in range(2):
                            ins = pe.matmul(Tb[:, C * b:C * b + C], fg(g)[:, c, P * b:P * b + P], fc2w[:, c, :],
                                            start=(c == 0), stop=(c == 1))
                    ins.then_inc(s["fc2_ps"], 1)
                    lend("T", "h2", g + 1)
                elif slot == 16:
                    transposes(xs3(g), "xl3", "xt3_ps", g)
                    lend("U", "xT3", g + 1)

            def prep(_, k):
                pe.wait_ge(s["early_in"], 16)
                pe.wait_ge(s["gb1"], 1)
                pe.matmul(misc_kv[0:C + 1, 0:2 * C], gb1[:, :], sec("kv", 2 * C, C), start=True, stop=True)
                pe.matmul(misc[0:C, 128:129], sec("q", C, C), sec("b1", 1, C), start=True, stop=True)
                pe.matmul(misc[0:1, 130:146], sec("b1", 1, C), sec("rot", 16, C), start=True, stop=True)
                for c in range(2):
                    ins = pe.matmul(misc[:, 146 + c:147 + c], early[0:C, EARLY["fc1"] + P * c:EARLY["fc1"] + P * c + P],
                                    sec("b2", 1, C), start=True, stop=True)
                ins.then_inc(s["misc_ps"], 1)

            pe.wait_ge(s["static"], 1)
            def filler(_, n):
                for _ in range(n):
                    pe.matmul(H[:, 0, 0:P], ones_mean[:, :], ones_mean[:, :], start=True, stop=True)

            for kind, g, k in ORDER["pe"]:
                {"prep": prep, "filler": filler, "stage": stage, "route": route, "spread": spread, "up": up, "down": down, "fold": fold}[kind](
                    g, k)


def lay_out(a):
    def both(w):
        return np.tile(w.reshape(C, -1), (2, 1))

    def everywhere(v):
        return np.tile(v.reshape(1, -1), (P, 1))

    def by_feature(w):
        return w.reshape(-1, P, C).transpose(1, 0, 2).reshape(P, -1)

    parts = {
        "conv_w": everywhere(a["L0_tok_w"]), "conv_b": everywhere(a["L0_tok_b"]), "gamma": everywhere(a["L0_tok_gamma"]),
        "beta": everywhere(a["L0_tok_beta"]), "alpha": everywhere(a["L0_tok_alpha"]), "fc2_b": everywhere(a["L0_attn_fc2_b"]),
        "b1p": a["L0_ffn_b1p"].reshape(-1, P).T, "b1s": a["L0_ffn_b1s"].reshape(-1, P).T,
        "fc1_b": a["L0_attn_fc1_b"].reshape(-1, P).T, "b2p": a["L0_ffn_b2p"].reshape(-1, P).T,
        "b2s": np.pad(a["L0_ffn_b2s"], (0, C))[:, None],
        "g1": both(a["L0_attn_norm1_g"]), "b1": both(a["L0_attn_norm1_b"]),
        "g2": both(a["L0_attn_norm2_g"]), "b2": both(a["L0_attn_norm2_b"]),
        "q": both(a["L0_attn_q_w"]), "rot": both(a["L0_attn_rotations"]), "fc1": both(a["L0_attn_fc1_w"]),
        "wr": both(a["L0_ffn_Wr"]), "kv": both(a["L0_attn_kv_w"]),
        "w1s": both(a["L0_ffn_W1s"]), "w1p": both(a["L0_ffn_W1p"].transpose(1, 0, 2)),
        "fc2": by_feature(a["L0_attn_fc2_w"]), "w2s": by_feature(a["L0_ffn_W2s"]), "w2p": by_feature(a["L0_ffn_W2p"]),
        **constants(),
    }
    w1s, w1p = a["L0_ffn_W1s"], a["L0_ffn_W1p"].transpose(1, 0, 2).reshape(C, -1)
    scan = np.concatenate([np.concatenate(np.split(w, 2, 1), 0) for w in (w1s, w1p)], 1)
    packed = {name: np.ascontiguousarray(np.concatenate([np.asarray(parts[k], np.float32) for k in starts], 1))
              for name, starts in (("stem", STEM), ("early", EARLY), ("late", LATE))}
    return {"xp": np.pad(a["x"], ((0, 0), (1, 2), (0, 0))), "scan": np.ascontiguousarray(scan), **packed}


def kernel(**inputs):
    import concourse.bacc as bacc
    from concourse.bass_utils import run_bass_kernel_spmd

    nc = bacc.Bacc("TRN2", target_bir_lowering=False, num_devices=1)
    arrays, aps = {}, []
    laid = lay_out({k: np.asarray(v) for k, v in inputs.items()})
    for name in ("xp", "stem", "early", "scan", "late"):
        arrays[f"in_{name}_dram"] = laid[name]
        aps.append(nc.dram_tensor(f"in_{name}_dram", laid[name].shape, F32, kind="ExternalInput").ap())
    out = nc.dram_tensor("out_0_dram", (NB, T, C), F32, kind="ExternalOutput").ap()
    build(nc, *aps, out)
    r = run_bass_kernel_spmd(nc, [arrays], core_ids=[0])
    return r.results[0]["out_0_dram"]
```
